# Optimizing a Trainium2 kernel written in Bass

```python
import numpy as np
import jax
import jax.numpy as jnp

def _softmax(x, axis=-1):
    return jax.nn.softmax(x, axis=axis)

def _gelu(x):
    return jax.nn.gelu(x, approximate=True)

def _silu(x):
    return jax.nn.silu(x)

def _sigmoid(x):
    return jax.nn.sigmoid(x)

def _layernorm(x, axis=-1, eps=1e-05):
    m = jnp.mean(x, axis=axis, keepdims=True)
    v = jnp.var(x, axis=axis, keepdims=True)
    return (x - m) / jnp.sqrt(v + eps)

def _scatter_add(tgt, idx, src, axis=0):
    return tgt.at[idx].add(src)

def _segment_sum(src, seg, n):
    return jax.ops.segment_sum(src, seg, n)
kernel_name = 'mk_gnn_ffn_d1_gnn_r8_eb9bb8'

def setup_inputs(seed: int=0):
    np.random.seed(seed)
    _w = jnp.asarray

    def _rec_inputs():
        import jax
        import jax.numpy as jnp
        _gk = jax.random.key(seed)
        x = -0.0006008 + 1.001 * jax.random.normal(jax.random.fold_in(_gk, 1), (6250, 256), jnp.float32)
        src = jax.random.randint(jax.random.fold_in(_gk, 2), (100000,), 0, 6250, jnp.int32)
        dst = jax.random.randint(jax.random.fold_in(_gk, 3), (100000,), 0, 6250, jnp.int32)
        _o = jnp.argsort(dst, stable=True)
        src = src[_o]
        dst = dst[_o]
        edge_weight = jax.random.uniform(jax.random.fold_in(_gk, 12), (100000,), jnp.float32, 0.0, 0.999998)
        return (x, src, dst, edge_weight)
    x, src, dst, edge_weight = _rec_inputs()

    def _L0_gnn_setup():
        import jax, jax.numpy as jnp
        import numpy as np
        N, E = (1250, 40000)
        IN_DIM, OUT_DIM, HEADS = (256, 32, 8)
        HD = OUT_DIM * HEADS
        EPS = 1e-16

        def _make_conv_params(key, in_dim, heads, d):
            hd = heads * d
            ks = jax.random.split(key, 8)
            s = 0.02
            return {'Wq': jax.random.normal(ks[0], (in_dim, hd)) * s, 'bq': jnp.zeros((hd,)), 'Wk': jax.random.normal(ks[1], (in_dim, hd)) * s, 'bk': jnp.zeros((hd,)), 'Wv': jax.random.normal(ks[2], (in_dim, hd)) * s, 'bv': jnp.zeros((hd,)), 'We': jax.random.normal(ks[3], (1, hd)) * s, 'Wskip': jax.random.normal(ks[4], (in_dim, hd)) * s, 'bskip': jnp.zeros((hd,)), 'Wbeta': jax.random.normal(ks[5], (3 * hd, 1)) * s}

        def transformer_conv(x, src, dst, edge_attr, p, heads, d):
            n = x.shape[0]
            q = (x @ p['Wq'] + p['bq']).reshape(n, heads, d)
            k = (x @ p['Wk'] + p['bk']).reshape(n, heads, d)
            v = (x @ p['Wv'] + p['bv']).reshape(n, heads, d)
            e = (edge_attr @ p['We']).reshape(-1, heads, d)
            kj = k[src] + e
            vj = v[src] + e
            alpha = jnp.einsum('ehd,ehd->eh', q[dst], kj) / jnp.sqrt(jnp.asarray(d, x.dtype))
            m = jax.ops.segment_max(alpha, dst, num_segments=n)
            m = jnp.where(jnp.isfinite(m), m, 0.0)
            ex = jnp.exp(alpha - m[dst])
            denom = jax.ops.segment_sum(ex, dst, num_segments=n)
            w = ex / (denom[dst] + EPS)
            out = jax.ops.segment_sum(w[:, :, None] * vj, dst, num_segments=n)
            out = out.reshape(n, heads * d)
            xr = x @ p['Wskip'] + p['bskip']
            beta = jax.nn.sigmoid(jnp.concatenate([out, xr, out - xr], axis=-1) @ p['Wbeta'])
            return beta * xr + (1.0 - beta) * out
        key = jax.random.key(seed)
        kx, ke, kw, k1, k2 = jax.random.split(key, 5)
        inp = {'x': jax.random.normal(kx, (N, IN_DIM), dtype=jnp.float32), 'edge_index': jax.random.randint(ke, (2, E), 0, N, dtype=jnp.int64), 'edge_weight': jax.random.uniform(kw, (E,), dtype=jnp.float32)}
        p1 = _make_conv_params(k1, IN_DIM, HEADS, OUT_DIM)
        p2 = _make_conv_params(k2, HD, HEADS, OUT_DIM)
        for name, v in p1.items():
            inp[name + '1'] = v
        for name, v in p2.items():
            inp[name + '2'] = v
        return inp
    _L0_gnn_all = _L0_gnn_setup()
    _L0_gnn_in = {k: v for k, v in _L0_gnn_all.items() if k in ('Wq1', 'bq1', 'Wk1', 'bk1', 'Wv1', 'bv1', 'We1', 'Wskip1', 'bskip1', 'Wbeta1', 'Wq2', 'bq2', 'Wk2', 'bk2', 'Wv2', 'bv2', 'We2', 'Wskip2', 'bskip2', 'Wbeta2')}
    del _L0_gnn_all

    def _L0_ffn_setup():
        import math
        import jax, jax.numpy as jnp
        import numpy as np
        CAPACITY_FACTOR = 1.25
        key = jax.random.key(seed)
        ks = jax.random.split(key, 5)
        B, L, D, F, E = (8, 1024, 256, 1024, 8)
        h = jax.random.normal(ks[0], (B, L, D), dtype=jnp.float32)
        gate_w = jax.random.normal(ks[1], (D, E), dtype=jnp.float32) * 0.02
        gate_b = jnp.zeros((E,), dtype=jnp.float32)
        w1 = jax.random.normal(ks[2], (E, D, F), dtype=jnp.float32) * (1.0 / math.sqrt(D))
        b1 = jnp.zeros((E, F), dtype=jnp.float32)
        w2 = jax.random.normal(ks[3], (E, F, D), dtype=jnp.float32) * (1.0 / math.sqrt(F))
        b2 = jnp.zeros((E, D), dtype=jnp.float32)
        return {'h': h, 'gate_w': gate_w, 'gate_b': gate_b, 'w1': w1, 'b1': b1, 'w2': w2, 'b2': b2}
    _L0_ffn_all = _L0_ffn_setup()
    _L0_ffn_in = {k: v for k, v in _L0_ffn_all.items() if k in ('gate_w', 'gate_b', 'w1', 'b1', 'w2', 'b2')}
    del _L0_ffn_all
    return {'x': x, 'src': src, 'dst': dst, 'edge_weight': edge_weight, 'L0_gnn_Wq1': _L0_gnn_in['Wq1'], 'L0_gnn_bq1': _L0_gnn_in['bq1'], 'L0_gnn_Wk1': _L0_gnn_in['Wk1'], 'L0_gnn_bk1': _L0_gnn_in['bk1'], 'L0_gnn_Wv1': _L0_gnn_in['Wv1'], 'L0_gnn_bv1': _L0_gnn_in['bv1'], 'L0_gnn_We1': _L0_gnn_in['We1'], 'L0_gnn_Wskip1': _L0_gnn_in['Wskip1'], 'L0_gnn_bskip1': _L0_gnn_in['bskip1'], 'L0_gnn_Wbeta1': _L0_gnn_in['Wbeta1'], 'L0_gnn_Wq2': _L0_gnn_in['Wq2'], 'L0_gnn_bq2': _L0_gnn_in['bq2'], 'L0_gnn_Wk2': _L0_gnn_in['Wk2'], 'L0_gnn_bk2': _L0_gnn_in['bk2'], 'L0_gnn_Wv2': _L0_gnn_in['Wv2'], 'L0_gnn_bv2': _L0_gnn_in['bv2'], 'L0_gnn_We2': _L0_gnn_in['We2'], 'L0_gnn_Wskip2': _L0_gnn_in['Wskip2'], 'L0_gnn_bskip2': _L0_gnn_in['bskip2'], 'L0_gnn_Wbeta2': _L0_gnn_in['Wbeta2'], 'L0_ffn_gate_w': _L0_ffn_in['gate_w'], 'L0_ffn_gate_b': _L0_ffn_in['gate_b'], 'L0_ffn_w1': _L0_ffn_in['w1'], 'L0_ffn_b1': _L0_ffn_in['b1'], 'L0_ffn_w2': _L0_ffn_in['w2'], 'L0_ffn_b2': _L0_ffn_in['b2']}

def reference(x, src, dst, edge_weight, L0_gnn_Wq1, L0_gnn_bq1, L0_gnn_Wk1, L0_gnn_bk1, L0_gnn_Wv1, L0_gnn_bv1, L0_gnn_We1, L0_gnn_Wskip1, L0_gnn_bskip1, L0_gnn_Wbeta1, L0_gnn_Wq2, L0_gnn_bq2, L0_gnn_Wk2, L0_gnn_bk2, L0_gnn_Wv2, L0_gnn_bv2, L0_gnn_We2, L0_gnn_Wskip2, L0_gnn_bskip2, L0_gnn_Wbeta2, L0_ffn_gate_w, L0_ffn_gate_b, L0_ffn_w1, L0_ffn_b1, L0_ffn_w2, L0_ffn_b2):
    import jax
    import jax.numpy as jnp

    def _L0_gnn_ref(x, edge_index, edge_weight, Wq1, bq1, Wk1, bk1, Wv1, bv1, We1, Wskip1, bskip1, Wbeta1, Wq2, bq2, Wk2, bk2, Wv2, bv2, We2, Wskip2, bskip2, Wbeta2):
        import jax, jax.numpy as jnp
        import numpy as np
        N, E = (1250, 40000)
        IN_DIM, OUT_DIM, HEADS = (256, 32, 8)
        HD = OUT_DIM * HEADS
        EPS = 1e-16

        def _make_conv_params(key, in_dim, heads, d):
            hd = heads * d
            ks = jax.random.split(key, 8)
            s = 0.02
            return {'Wq': jax.random.normal(ks[0], (in_dim, hd)) * s, 'bq': jnp.zeros((hd,)), 'Wk': jax.random.normal(ks[1], (in_dim, hd)) * s, 'bk': jnp.zeros((hd,)), 'Wv': jax.random.normal(ks[2], (in_dim, hd)) * s, 'bv': jnp.zeros((hd,)), 'We': jax.random.normal(ks[3], (1, hd)) * s, 'Wskip': jax.random.normal(ks[4], (in_dim, hd)) * s, 'bskip': jnp.zeros((hd,)), 'Wbeta': jax.random.normal(ks[5], (3 * hd, 1)) * s}

        def transformer_conv(x, src, dst, edge_attr, p, heads, d):
            n = x.shape[0]
            q = (x @ p['Wq'] + p['bq']).reshape(n, heads, d)
            k = (x @ p['Wk'] + p['bk']).reshape(n, heads, d)
            v = (x @ p['Wv'] + p['bv']).reshape(n, heads, d)
            e = (edge_attr @ p['We']).reshape(-1, heads, d)
            kj = k[src] + e
            vj = v[src] + e
            alpha = jnp.einsum('ehd,ehd->eh', q[dst], kj) / jnp.sqrt(jnp.asarray(d, x.dtype))
            m = jax.ops.segment_max(alpha, dst, num_segments=n)
            m = jnp.where(jnp.isfinite(m), m, 0.0)
            ex = jnp.exp(alpha - m[dst])
            denom = jax.ops.segment_sum(ex, dst, num_segments=n)
            w = ex / (denom[dst] + EPS)
            out = jax.ops.segment_sum(w[:, :, None] * vj, dst, num_segments=n)
            out = out.reshape(n, heads * d)
            xr = x @ p['Wskip'] + p['bskip']
            beta = jax.nn.sigmoid(jnp.concatenate([out, xr, out - xr], axis=-1) @ p['Wbeta'])
            return beta * xr + (1.0 - beta) * out
        src, dst = (edge_index[0], edge_index[1])
        ea = edge_weight[:, None]
        p1 = dict(Wq=Wq1, bq=bq1, Wk=Wk1, bk=bk1, Wv=Wv1, bv=bv1, We=We1, Wskip=Wskip1, bskip=bskip1, Wbeta=Wbeta1)
        p2 = dict(Wq=Wq2, bq=bq2, Wk=Wk2, bk=bk2, Wv=Wv2, bv=bv2, We=We2, Wskip=Wskip2, bskip=bskip2, Wbeta=Wbeta2)
        h = transformer_conv(x, src, dst, ea, p1, HEADS, OUT_DIM)
        h = transformer_conv(h, src, dst, ea, p2, HEADS, OUT_DIM)
        h = transformer_conv(h, src, dst, ea, p2, HEADS, OUT_DIM)
        return h

    def _L0_ffn_ref(h, gate_w, gate_b, w1, b1, w2, b2):
        import math
        import jax, jax.numpy as jnp
        import numpy as np
        CAPACITY_FACTOR = 1.25
        B, L, D = h.shape
        E = gate_w.shape[1]
        T = B * L
        C = max(1, math.ceil(CAPACITY_FACTOR * T / E))
        x = h.reshape(T, D)
        logits = x @ gate_w + gate_b
        probs = jax.nn.softmax(logits, axis=-1)
        idx = jnp.argmax(probs, axis=-1)
        prb = jnp.take_along_axis(probs, idx[:, None], axis=1)[:, 0]
        one_hot = jax.nn.one_hot(idx, E, dtype=jnp.float32)
        pos = (jnp.cumsum(one_hot, axis=0) * one_hot).sum(-1).astype(jnp.int32) - 1
        kept = pos < C
        pos_safe = jnp.where(kept, pos, C)
        buf = jnp.zeros((E, C, D), dtype=h.dtype).at[idx, pos_safe].set(x, mode='drop')
        hmid = jax.nn.relu(jnp.einsum('ecd,edf->ecf', buf, w1) + b1[:, None, :])
        ybuf = jnp.einsum('ecf,efd->ecd', hmid, w2) + b2[:, None, :]
        pos_g = jnp.minimum(pos, C - 1)
        y_tok = ybuf[idx, pos_g] * (prb * kept)[:, None]
        y = y_tok.reshape(B, L, D)
        y = jnp.nan_to_num(y, nan=0.0, posinf=10000.0, neginf=-10000.0)
        return y
    edge_index = jnp.stack([src, dst])
    x = x + _L0_gnn_ref(_layernorm(x, axis=-1), edge_index, edge_weight, L0_gnn_Wq1, L0_gnn_bq1, L0_gnn_Wk1, L0_gnn_bk1, L0_gnn_Wv1, L0_gnn_bv1, L0_gnn_We1, L0_gnn_Wskip1, L0_gnn_bskip1, L0_gnn_Wbeta1, L0_gnn_Wq2, L0_gnn_bq2, L0_gnn_Wk2, L0_gnn_bk2, L0_gnn_Wv2, L0_gnn_bv2, L0_gnn_We2, L0_gnn_Wskip2, L0_gnn_bskip2, L0_gnn_Wbeta2)
    x = x + _L0_ffn_ref(_layernorm(x, axis=-1)[None], L0_ffn_gate_w, L0_ffn_gate_b, L0_ffn_w1, L0_ffn_b1, L0_ffn_w2, L0_ffn_b2)[0]
    return x

_drawn_inputs = setup_inputs


def setup_inputs(seed=0):
    import zlib

    import numpy as np

    out = dict(_drawn_inputs(seed))
    spreads = {'L0_gnn_bq1': (0.0, 0.8),
     'L0_gnn_bk1': (0.0, 0.8),
     'L0_gnn_bv1': (0.0, 0.8),
     'L0_gnn_bskip1': (0.0, 0.8),
     'L0_gnn_bq2': (0.0, 0.8),
     'L0_gnn_bk2': (0.0, 0.8),
     'L0_gnn_bv2': (0.0, 0.1),
     'L0_gnn_bskip2': (0.0, 0.1),
     'L0_ffn_gate_b': (0.0, 0.1),
     'L0_ffn_b1': (0.0, 0.61),
     'L0_ffn_b2': (0.0, 0.431)}
    factors = {'edge_weight': 8.0,
     'L0_gnn_Wq1': 8.0,
     'L0_gnn_Wk1': 8.0,
     'L0_gnn_Wv1': 8.0,
     'L0_gnn_We1': 8.0,
     'L0_gnn_Wskip1': 5.209,
     'L0_gnn_Wbeta1': 8.0,
     'L0_gnn_Wq2': 8.0,
     'L0_gnn_Wk2': 8.0,
     'L0_gnn_Wv2': 3.03,
     'L0_gnn_We2': 4.748,
     'L0_gnn_Wbeta2': 6.974}
    for name, (base, spread) in spreads.items():
        noise = np.random.default_rng([zlib.crc32(name.encode()), seed]).standard_normal(out[name].shape)
        drawn = base * np.exp(spread * noise) if base else spread * noise
        out[name] = jnp.asarray(drawn.astype(out[name].dtype))
    for name, factor in factors.items():
        out[name] = (out[name] * factor).astype(out[name].dtype)
    return out
```

```python
from contextlib import ExitStack

import numpy as np

import concourse.bass as bass
from concourse import mybir

F32 = mybir.dt.float32
I32 = mybir.dt.int32
ALU = mybir.AluOpType
ACT = mybir.ActivationFunctionType
AX = mybir.AxisListType.X
ds = bass.ds

P = 128
NODES, EDGES, D, HEADS = 6250, 100000, 256, 8
HD = D // HEADS
LAYERS = 3
J = 4
SE = P * J
SUPER = -(-EDGES // SE)
NBLK = 50
REAL_BLK = -(-NODES // P)
NPAD = NBLK * P
U = 4
STEPS = -(-(SUPER + REAL_BLK - 1) // U) * U
NB = STEPS // U
KH = STEPS // 2
PB = U * HEADS
AW = HD + 2
QW = D + HEADS
QX = 2 * D + HEADS
BIG = 1e30
HUGE = 1e38
SCALE = float(HD) ** -0.5
FAR = 1 << 20

START = 1
EXPERTS, FF = 8, 1024
CAP = max(1, -(-5 * NODES // (4 * EXPERTS)))
CAPP = 1024
CT = CAPP // P
HALF = 489
assert NB % 2 == 1 and NBLK % 10 == 0 and 2 * HALF >= CAP and STEPS % 2 == 0


class Chain:

    def __init__(self, eng, sem, per=None, start=0):
        self.eng, self.sem, self.per, self.start, self.base, self.n = eng, sem, per, start, start, 0

    def at(self, iteration):
        assert self.n in (0, self.per), (self.n, self.per)
        self.base, self.n = iteration * self.per + self.start, 0

    def inc(self, ins):
        self.n += 1
        ins.then_inc(self.sem, 1)

    def wait(self):
        self.eng.wait_ge(self.sem, self.base + self.n)

    def link(self, ins):
        self.inc(ins)
        self.wait()


KB = 13
KACT = 4
SEMAPHORES = ""


def build(nc, a, out):
    dram = lambda name, shape, dt=F32: nc.dram_tensor(name, shape, dt, kind="Internal").ap()
    h_dram = dram("h_dram", (NPAD, D))
    kv_dram = dram("kv_dram", (NPAD, 2 * D))
    qx_dram = dram("qx_dram", (NPAD, QX))
    res_dram = dram("res_dram", (STEPS * HEADS, SE + 1))
    meta_dram = dram("meta_dram", (4, STEPS))
    x2_dram = dram("x2_dram", (NPAD, D))
    xn_dram = dram("xn_dram", (NPAD, D))
    slots_dram = dram("slots_dram", (EXPERTS * CAPP, D))
    y_dram = dram("y_dram", (EXPERTS * 2 * HALF, D))

    with ExitStack() as ctx:
        def sb(name, shape, dt=F32):
            return ctx.enter_context(nc.sbuf_tensor("s_" + name, shape, dt))

        def pb(name, shape):
            return ctx.enter_context(nc.psum_tensor(name, shape, F32))

        def sem(name):
            return ctx.enter_context(nc.semaphore(name))

        psQ = pb("psQ", [P, 4, 512])
        psG = pb("psG", [P, 512])
        psA = pb("psA", [P, 512])
        psT = pb("psT", [P, 512])
        psB = pb("psB", [P, 512])

        iota_i = sb("iota_i", [P, SUPER], I32)
        part_i = sb("part_i", [P, 4], I32)
        sel_i = sb("sel_i", [P, HEADS + U + U * HEADS], I32)
        iota_r = sb("iota_r", [P, P])
        iota_c = sb("iota_c", [P, 1])
        ident = sb("ident", [P, P])
        tri = sb("tri", [P, P])
        ones = sb("ones", [P, P])
        selA = sb("selA", [PB, HEADS])
        selB = sb("selB", [PB, U])
        selD = sb("selD", [HEADS, U, HEADS])
        e8 = sb("e8", [P, EXPERTS])
        srcI = sb("srcI", [P, STEPS, J], I32)
        ndl = sb("ndl", [P, STEPS, J])
        ewT = sb("ewT", [P, STEPS, J])
        dn8 = sb("dn8", [HEADS, STEPS])
        dd8 = sb("dd8", [HEADS, STEPS])
        blkI = sb("blkI", [1, STEPS], I32)
        crossc = sb("crossc", [PB, NB])
        accT = sb("acc", [P, NBLK * HEADS * AW])
        acc = accT[:, :].rearrange("p (b h w) -> p b h w", b=NBLK, h=HEADS)
        RING = 2 * U * J * 2 * D
        ringT = sb("ring", [P, RING])
        kv = ringT[:, :].rearrange("p (r s j w) -> p r s j w", r=2, s=U, j=J)
        G = sb("G", [P, 2, U, J, P])
        OH = sb("OH", [P, 2, J, P])
        qring = sb("qring", [P, U, QW])
        prod = sb("prod", [P, 2, J, D])
        al1 = sb("al1", [P, 2, J, HEADS])
        al2 = sb("al2", [P, 2, J, HEADS])
        alpha = sb("alpha", [P, 2, J, U, HEADS])
        res = sb("res", [PB, SE + 1])
        F1 = sb("F1", [PB, SE])
        F2 = sb("F2", [PB, SE])
        M = sb("M", [PB, SE])
        Dm = sb("Dm", [PB, SE])
        pT = sb("pT", [PB, SE])
        LB = sb("LB", [PB, U])
        Us = sb("Us", [HEADS, U + 1])
        cc = sb("cc", [HEADS, U])
        lhs2 = sb("lhs2", [HEADS, U, HEADS])
        ccol = sb("ccol", [PB, 1])
        gd = sb("gd", [PB, 1])
        gx = sb("gx", [PB, 1])
        gm = sb("gm", [PB, PB])
        crossOH = sb("crossOH", [PB, P])
        pB = sb("pB", [P, J, U, HEADS])
        fB = sb("fB", [P, U, HEADS])
        W = sb("W", [P, 2, J, HEADS, AW])
        idxb = sb("idxb", [P, 2, U, J], I32)
        we_bc = sb("we_bc", [P, D])
        wb_bc = sb("wb_bc", [P, 3, D])
        wA = sb("wA", [P, D])
        wB = sb("wB", [P, D])
        den = sb("den", [P, 2, HEADS])
        rden = sb("rden", [P, 2, HEADS])
        tew = sb("tew", [P, 2, HEADS])
        zc = sb("zc", [P, 2])
        ez = sb("ez", [P, 2])
        beta = sb("beta", [P, 2])
        stats = sb("stats", [P, 2, 6])
        mv = sb("mv", [P, 2, 2])
        ve = sb("ve", [P, 2])
        sd = sb("sd", [P, 2])
        rstd = sb("rstd", [P, 2])
        lastI = sb("lastI", [P, SUPER - 1], I32)
        tI = sb("tI", [P, 2], I32)
        small3 = sb("small3", [P, 2, 3])

        def view(at, *shape, of=ringT, room=RING, dt=None):
            n = int(np.prod(shape))
            assert at + n <= room, (at, n)
            names = " ".join(f"d{i}" for i in range(len(shape)))
            flat = of[:, at:at + n]
            if dt is not None:
                flat = flat.bitcast(dt)
            if len(shape) == 1:
                return flat, at + n
            return flat.rearrange(f"p ({names}) -> p {names}",
                                  **{f"d{i}": x for i, x in enumerate(shape)}), at + n

        o = 0
        rawI, o = view(o, 2, SE, dt=I32)
        srcR, o = view(o, 2, SE, dt=I32)
        dstF, o = view(o, 2, SE)
        srcF, o = view(o, 2, SE)
        ewF, o = view(o, 2, SE)
        dloc, o = view(o, 2, SE)
        res2, o = view(o, 2, SE + 1)
        posA, o = view(o, SUPER - 1)
        cmpT, o = view(o, SUPER - 1)
        kcol, o = view(o, 2)
        tcol, o = view(o, 2)
        nbc, o = view(o, 2)
        o += o % 2
        row = [None] * 10
        for i in range(10):
            row[i], _ = view(i * STEPS, STEPS, of=accT, room=NBLK * HEADS * AW)
        EU = 5
        ACCN = NBLK * HEADS * AW
        o = 10 * STEPS
        lx, o = view(o, EU, 2, D, of=accT, room=ACCN)
        ly, o = view(o, EU, 2, D, of=accT, room=ACCN)
        lh, o = view(o, EU, 2, D, of=accT, room=ACCN)
        o = 0
        wcat, o = view(o, 2, 4 * D)
        bias_bc, o = view(o, 4 * D)
        hb, o = view(o, 2, D)
        hT, o = view(o, 2, 2, P)
        kvb, o = view(o, 2, 2 * D)
        qxb, o = view(o, 2, QX)
        qprod, o = view(o, D)
        o = 0
        xr, o = view(o, EU, 2, D)
        hout, o = view(o, EU, 2, D)
        ov, o = view(o, 2, D)
        tw, o = view(o, 2, D)
        q1, o = view(o, 2, D)

        class Sems(dict):
            def __missing__(self, name):
                self[name] = sem(name)
                return self[name]

        s = Sems()
        for name in SEMAPHORES.split():
            s[name]
        kv_in = [[sem(f"kv_in_{r}_{i}") for i in range(U)] for r in range(2)]
        q_in = [sem(f"q_in_{i}") for i in range(U)]
        x_in = [sem(f"x_in_{i}") for i in range(EU)]
        xr_in = [sem(f"xr_in_{i}") for i in range(EU)]
        h_st = [sem(f"h_stored_{i}") for i in range(EU)]
        hb_in = [sem(f"hb_in_{i}") for i in range(2)]
        pst = [sem(f"proj_stored_{i}") for i in range(2)]
        PAIRS = NBLK // 2
        LOOPS = PAIRS // EU

        class Batch:

            def __init__(self, l, B, par, half):
                self.B, self.par = B, par
                self.g = l * NB + B
                self.use = l * ((NB + 1) // 2 if par == 0 else NB // 2) + half

            def k(self, i):
                return self.B * U + i

            def n(self, i):
                return self.g * U + i

        def edge_loop(eng, l, body):
            body(Batch(l, 0, 0, 0), None)
            with eng.Fori(0, NB // 2) as m:
                body(Batch(l, m * 2 + 1, 1, m), Batch(l, m * 2, 0, m))
                body(Batch(l, m * 2 + 2, 0, m + 1), Batch(l, m * 2 + 1, 1, m))
            body(None, Batch(l, NB - 1, 0, NB // 2))

        def rounds(eng, n, body):
            body(0, True)
            with eng.Fori(1, n) as m:
                body(m, False)

        ZERO_DMAS = EXPERTS * CAPP * D // (P * 2 * U * J * P)
        flat3 = lambda x: x.rearrange("p b e -> p (b e)")

        def held(eng):
            eng.sem_inc(s["held"], 1)

        NGATE = NBLK * EXPERTS
        o = 0
        hm, o = view(o, FF // P, 2 * HALF, of=accT, room=ACCN)
        lg, o = view(o, NBLK, EXPERTS, of=accT, room=ACCN)
        ex, o = view(o, NBLK, EXPERTS, of=accT, room=ACCN)
        eq, o = view(o, NBLK, EXPERTS, of=accT, room=ACCN)
        oh, o = view(o, NBLK, EXPERTS, of=accT, room=ACCN)
        cum, o = view(o, NBLK, EXPERTS, of=accT, room=ACCN)
        tot, o = view(o, NBLK, EXPERTS, of=accT, room=ACCN)
        run, o = view(o, NBLK, EXPERTS, of=accT, room=ACCN)
        mx, o = view(o, NBLK, of=accT, room=ACCN)
        se, o = view(o, NBLK, of=accT, room=ACCN)
        ms, o = view(o, NBLK, of=accT, room=ACCN)
        pos, o = view(o, NBLK, of=accT, room=ACCN)
        base, o = view(o, NBLK, of=accT, room=ACCN)
        kept, o = view(o, NBLK, of=accT, room=ACCN)
        wgt, o = view(o, NBLK, of=accT, room=ACCN)
        slf, o = view(o, NBLK, of=accT, room=ACCN)
        slotw, o = view(o, NBLK, of=accT, room=ACCN, dt=I32)
        slotr, o = view(o, NBLK, of=accT, room=ACCN, dt=I32)
        gb_bc, o = view(o, EXPERTS, of=accT, room=ACCN)
        gw, o = view(o, 2, EXPERTS, of=accT, room=ACCN)
        b1c, o = view(o, 2, FF // P, of=accT, room=ACCN)
        b2b, o = view(o, 2, D, of=accT, room=ACCN)
        o = 0
        w1, o = view(o, 2, 2, FF)
        w2, o = view(o, 2, FF // P, D)
        xs, o = view(o, 2, CT, D)
        xsT, o1 = view(o, 2, CAPP)
        xsc, _ = view(o, EU, D)
        yb, _ = view(o1, CT, D)
        hbg, o = view(o1, 2, D)
        hTg, o = view(o, 2, 2, P)
        o = 0
        yg, o = view(o, EU, D)
        x2b, o = view(o, EU, D)
        fo, o = view(o, EU, D)
        fin, o = view(o, D)
        nn, o = view(o, D)
        ty, o = view(o, D)
        cl, o = view(o, D)
        idx5 = sb("idx5", [P, 2 * EU], I32)
        w_ex = [sem(f"w_ex_{i}") for i in range(2)]
        xs_in = [sem(f"xs_in_{i}") for i in range(2)]
        sc_in = [sem(f"sc_in_{i}") for i in range(EU)]
        sc_done = [sem(f"sc_done_{i}") for i in range(EU)]
        yg_in = [sem(f"yg_in_{i}") for i in range(EU)]
        x2_in = [sem(f"x2_in_{i}") for i in range(EU)]
        o_st = [sem(f"o_stored_{i}") for i in range(EU)]
        H_ALL = (LAYERS + 1) * LOOPS * 16
        G_ALL = LAYERS * NBLK
        SROUNDS = NBLK // EU

        def moe_sync(sp):
            for i in range(EU):
                sp.wait_ge(h_st[i], H_ALL)
            with sp.Fori(0, LOOPS) as m:
                for r in range(EU):
                    sp.wait_ge(h_st[r], m * 32 + H_ALL)
                    for src, dst in ((a["x"], lx), (h_dram, lh)):
                        sp.dma_start(dst[:, r, :, :], src[ds((m * EU + r) * 2 * P, 2 * P), :]
                                     .rearrange("(n p) d -> p n d", n=2)).then_inc(x_in[r], 16)
            for i in range(EU):
                sp.wait_ge(h_st[i], H_ALL + 32 * LOOPS)
            for c in range(2):
                sp.dma_start(gw[:, c, :], a["gate_w"][c * P:(c + 1) * P, :]).then_inc(s["gate_in"], 16)
            sp.dma_start(gb_bc, a["gate_b"].to_broadcast([P, EXPERTS])).then_inc(s["gate_in"], 16)
            with sp.Fori(0, PAIRS) as m:
                for r in range(2):
                    sp.wait_ge(s["tr_done"], m * 2 + (G_ALL + r + 1))
                    sp.dma_start(hbg[:, r, :], xn_dram[ds((m * 2 + r) * P, P), :]).then_inc(hb_in[r], 16)
            def load_rows(m, first):
                for r in range(EU):
                    if not first:
                        sp.wait_ge(sc_done[r], m * 16)
                    sp.dma_start(xsc[:, r, :], xn_dram[ds((m * EU + r) * P, P), :]).then_inc(sc_in[r], 16)

            rounds(sp, SROUNDS, load_rows)
            for r in range(EU):
                sp.wait_ge(sc_done[r], SROUNDS * 16)
            with sp.Fori(0, EXPERTS // 2) as m:
                for r in range(2):
                    sp.wait_ge(s["y_mm"], m * (2 * CT) + (r * CT + CT))
                    for c in range(2):
                        sp.dma_start(w1[:, r, c, :], a["w1"][ds(m * (2 * D) + (r * D + c * P), P), :]
                                     ).then_inc(w_ex[r], 16)
                    sp.dma_start(w2[:, r, :, :], a["w2"][ds(m * (2 * FF) + r * FF, FF), :]
                                 .rearrange("(f p) d -> p f d", p=P)).then_inc(w_ex[r], 16)
                    sp.dma_start(b1c[:, r, :], a["b1"][ds(m * (2 * P) + r * P, P), :]).then_inc(w_ex[r], 16)
                    sp.wait_ge(s["y_ev"], m * (2 * CT) + (r * CT - CT + 2 + CT))
                    sp.dma_start(b2b[:, r, :], a["b2"][ds(m * 2 + r, 1), :].to_broadcast([P, D])
                                 ).then_inc(w_ex[r], 16)
                    sp.dma_start(xs[:, r, :, :], slots_dram[ds(m * (2 * CAPP) + r * CAPP, CAPP), :]
                                 .rearrange("(t p) d -> p t d", p=P)).then_inc(xs_in[r], 16)
            sp.wait_ge(s["y_st"], EXPERTS * 32)
            with sp.Fori(0, SROUNDS) as m:
                for r in range(EU):
                    sp.wait_ge(s["fo_done"], m * EU + r + 1)
                    sp.dma_start(x2b[:, r, :], x2_dram[ds((m * EU + r) * P, P), :]).then_inc(x2_in[r], 16)

        def moe_pool(pool):
            with pool.Fori(0, LOOPS) as m:
                for r in range(EU):
                    pool.wait_ge(s["ln_done"], m * EU + (PAIRS + r + 1 + EU))
                    for dst, src in ((xn_dram, ly), (x2_dram, lh)):
                        pool.dma_start(dst[ds((m * EU + r) * 2 * P, 2 * P), :].rearrange("(n p) d -> p n d", n=2),
                                       src[:, r, :, :]).then_inc(h_st[r], 16)
            pool.wait_ge(s["slots_ready"], 1)
            def scatter(m, first):
                for r in range(EU):
                    if not first:
                        pool.wait_ge(sc_done[r], m * 16)
                        held(pool)
                    pool.tensor_copy(idx5[:, r:r + 1], slotw[:, ds(m * EU + r, 1)]).then_inc(s["sidx"], 1)
                    pool.wait_ge(s["sidx"], m * EU + r + 1)
                    pool.wait_ge(sc_in[r], m * 16 + 16)
                    held(pool)
                    pool.indirect_dma_start(slots_dram, bass.IndirectOffsetOnAxis(ap=idx5[:, r:r + 1], axis=0),
                                            xsc[:, r, :], None, bounds_check=EXPERTS * CAPP - 1,
                                            oob_is_err=False).then_inc(sc_done[r], 16)

            rounds(pool, SROUNDS, scatter)
            with pool.Fori(0, EXPERTS // 2) as m:
                for r in range(2):
                    pool.wait_ge(s["y_ev"], m * (2 * CT) + (r * CT + CT + 2))
                    full = 2 * HALF // P
                    rest = 2 * HALF - full * P
                    pool.dma_start(y_dram[ds(m * (4 * HALF) + r * 2 * HALF, full * P), :]
                                   .rearrange("(t p) d -> p t d", p=P), yb[:, 0:full, :]).then_inc(s["y_st"], 16)
                    pool.dma_start(y_dram[ds(m * (4 * HALF) + (r * 2 * HALF + full * P), rest), :],
                                   yb[0:rest, full, :]).then_inc(s["y_st"], 16)
            pool.wait_ge(s["y_st"], EXPERTS * 32)
            with pool.Fori(0, SROUNDS) as m:
                for r in range(EU):
                    pool.wait_ge(s["fo_done"], m * EU + r + 1)
                    held(pool)
                    pool.tensor_copy(idx5[:, EU + r:EU + r + 1], slotr[:, ds(m * EU + r, 1)]).then_inc(s["gidx"], 1)
                    pool.wait_ge(s["gidx"], m * EU + r + 1)
                    held(pool)
                    pool.indirect_dma_start(yg[:, r, :], None, y_dram,
                                            bass.IndirectOffsetOnAxis(ap=idx5[:, EU + r:EU + r + 1], axis=0)
                                            ).then_inc(yg_in[r], 16)

        def moe_act(act):
            with act.Fori(0, LOOPS) as m:
                for r in range(EU):
                    act.wait_ge(s["ln_var"], m * EU + (PAIRS + r + 1))
                    act.activation(sd[:, :], ve[:, :], ACT.Sqrt).then_inc(s["ln_sd"], 1)
            with act.Fori(0, PAIRS) as m:
                for r in range(2):
                    act.wait_ge(s["tr_done"], m * 2 + (G_ALL + r + 1 + 2))
                    act.wait_ge(s["mm_done"], m * 2 + (G_ALL + r + 1))
                    act.activation(hTg[:, r, :, :].rearrange("p c t -> p (c t)"), psG[:, 0:D], ACT.Copy
                                   ).then_inc(s["hT_done"], 1)
            act.wait_ge(s["lm_ready"], 1)
            act.activation(flat3(ex), flat3(eq), ACT.Exp).then_inc(s["ex_ready"], 1)
            with act.Fori(0, EXPERTS // 2) as m:
                for r in range(2):
                    e16 = m * 32 + r * 16
                    for b in range(4):
                        act.wait_ge(s["xt_ps"], m * 8 + (r * 4 + b + 1))
                        act.activation(xsT[:, :, b * 2 * P:(b + 1) * 2 * P].rearrange("p c (t e) -> p t c e", t=2),
                                       psQ[:, b, :].rearrange("p (t c e) -> p t c e", t=2, c=2), ACT.Copy
                                       ).then_inc(s["xt_cp"], 1)
                    act.wait_ge(w_ex[r], m * (5 * 16) + 5 * 16)
                    act.wait_ge(s["y_mm"], m * (2 * CT) + (r * CT + 2 * CT))
                    for q in range(2 * (FF // P)):
                        f, half = q // 2, q % 2
                        act.wait_ge(s["h_mm"], e16 + (q + 1))
                        act.activation(hm[:, f, half * HALF:(half + 1) * HALF], psQ[:, q % 4, 0:HALF], ACT.Relu,
                                       bias=b1c[:, r, f:f + 1]).then_inc(s["h_cp"], 1)
            with act.Fori(0, SROUNDS) as m:
                for r in range(EU):
                    act.wait_ge(s["fo_done"], m * EU + (r + 1 + EU))
                    act.dma_start(out[ds((m * EU + r) * P, P), :], fo[:, r, :]).then_inc(o_st[r], 16)
            for r in range(EU):
                act.wait_ge(o_st[r], SROUNDS * 16)

        def moe_pe(pe):
            pe.wait_ge(s["gate_in"], 3 * 16)
            with pe.Fori(0, PAIRS) as m:
                for r in range(2):
                    pe.wait_ge(hb_in[r], m * 16 + (LAYERS * PAIRS + 1) * 16)
                    pe.wait_ge(s["hT_done"], m * 2 + (G_ALL + r) + START)
                    for c in range(2):
                        last = pe.transpose(psG[:, c * P:(c + 1) * P], hbg[:, r, c * P:(c + 1) * P], ident[:, :])
                    last.then_inc(s["tr_done"], 1)
                    pe.wait_ge(s["hT_done"], m * 2 + (G_ALL + r + 1) + START)
                    pe.wait_ge(s["ev_done"], m * 2 + (G_ALL + r + 1))
                    for c in range(2):
                        last = pe.matmul(psQ[:, r, 0:EXPERTS], hTg[:, r, c, :], gw[:, c, :],
                                         start=(c == 0), stop=(c == 1))
                    last.then_inc(s["mm_done"], 1)
            pe.wait_ge(s["oh_ready"], 1)
            pe.matmul(psT[:, 0:NGATE], tri[:, :], flat3(oh), start=True, stop=True)
            pe.matmul(psB[:, 0:NGATE], ones[:, :], flat3(oh), start=True, stop=True).then_inc(s["cnt_mm"], 1)
            with pe.Fori(0, EXPERTS // 2) as m:
                for r in range(2):
                    e16 = m * 32 + r * 16
                    pe.wait_ge(xs_in[r], m * 16 + 16)
                    pe.wait_ge(s["h_cp"], e16 + START)
                    for b in range(4):
                        for t in range(2):
                            for c in range(2):
                                last = pe.transpose(psQ[:, b, (2 * t + c) * P:(2 * t + c + 1) * P],
                                                    xs[:, r, 2 * b + t, c * P:(c + 1) * P], ident[:, :])
                        last.then_inc(s["xt_ps"], 1)
                    pe.wait_ge(s["xt_cp"], m * 8 + (r * 4 + 4))
                    pe.wait_ge(w_ex[r], m * (5 * 16) + 5 * 16)
                    for q in range(2 * (FF // P)):
                        f, half = q // 2, q % 2
                        if q >= 4:
                            pe.wait_ge(s["h_cp"], e16 + (q - 3) + START)
                        for c in range(2):
                            last = pe.matmul(psQ[:, q % 4, 0:HALF], w1[:, r, c, f * P:(f + 1) * P],
                                             xsT[:, c, half * HALF:(half + 1) * HALF],
                                             start=(c == 0), stop=(c == 1))
                        last.then_inc(s["h_mm"], 1)
                    pe.wait_ge(s["h_cp"], e16 + 16 + START)
                    for t in range(CT):
                        n = min(P, 2 * HALF - t * P)
                        bank = (psA, psT)[t % 2]
                        pe.wait_ge(s["y_ev"], m * (2 * CT) + (r * CT + t + 1))
                        for f in range(FF // P):
                            last = pe.matmul(bank[0:n, 0:D], hm[:, f, t * P:t * P + n], w2[:, r, f, :],
                                             start=(f == 0), stop=(f == FF // P - 1))
                        last.then_inc(s["y_mm"], 1)

        def moe_dve(dve, layer_norm):
            mc = Chain(dve, s["moe_add"], 1)
            with dve.Fori(0, LOOPS) as m:
                for r in range(EU):
                    mc.at(m * EU + r)
                    dve.wait_ge(x_in[r], m * 32 + (LOOPS + 2) * 16)
                    mc.link(dve.tensor_tensor(lh[:, r, :, :], lh[:, r, :, :], lx[:, r, :, :], ALU.add))
                    layer_norm(lh[:, r, :, :], ly[:, r, :, :], m * EU + r + PAIRS, h_st[r], m * 32 + (H_ALL))
            dve.wait_ge(s["gate_in"], 3 * 16)
            with dve.Fori(0, PAIRS) as m:
                for r in range(2):
                    dve.wait_ge(s["mm_done"], m * 2 + (G_ALL + r + 1 + 2))
                    dve.tensor_tensor(lg[:, ds(m * 2 + r, 1), :].rearrange("p b e -> p (b e)"),
                                      psQ[:, r, 0:EXPERTS], gb_bc, ALU.add).then_inc(s["ev_done"], 1)
            dve.wait_ge(s["ev_done"], G_ALL + NBLK + 2)
            c = Chain(dve, s["route"])
            per_token = lambda v: v.unsqueeze(2).to_broadcast([P, NBLK, EXPERTS])
            e8_bc = e8[:, :].unsqueeze(1).to_broadcast([P, NBLK, EXPERTS])
            c.link(dve.tensor_reduce(mx, lg, AX, ALU.max))
            c.link(dve.tensor_tensor(eq, lg, per_token(mx), ALU.subtract))
            dve.sem_inc(s["lm_ready"], 1)
            c.link(dve.tensor_scalar(oh, eq, 0.0, None, ALU.is_equal))
            c.link(dve.tensor_tensor(oh, oh, e8_bc, ALU.mult))
            c.link(dve.tensor_reduce(ms, oh, AX, ALU.max))
            c.link(dve.tensor_tensor(oh, e8_bc, per_token(ms), ALU.is_equal))
            dve.sem_inc(s["oh_ready"], 1)
            dve.wait_ge(s["ex_ready"], 1)
            c.link(dve.tensor_reduce(se, ex, AX, ALU.add))
            c.link(dve.reciprocal(wgt, se))
            dve.wait_ge(s["cnt_mm"], 1)
            for e in range(EXPERTS):
                last = dve.tensor_tensor_scan(run[:, :, e], ones[:, 0:NBLK], psB[:, e:NGATE:EXPERTS], 0.0,
                                              ALU.mult, ALU.add)
            c.link(last)
            c.link(dve.tensor_tensor(flat3(run), flat3(run), psB[:, 0:NGATE], ALU.subtract))
            c.link(dve.tensor_tensor(flat3(run), flat3(run), psT[:, 0:NGATE], ALU.add))
            c.link(dve.tensor_tensor(run, run, oh, ALU.mult))
            c.link(dve.tensor_reduce(pos, run, AX, ALU.add))
            c.link(dve.tensor_scalar(kept, pos, float(CAP), None, ALU.is_le))
            c.link(dve.tensor_tensor(wgt, wgt, kept, ALU.mult))
            c.link(dve.tensor_scalar(base, ms, -float(CAPP), float(EXPERTS * CAPP - 1), ALU.mult, ALU.add))
            c.link(dve.tensor_scalar(kept, kept, -float(1 << 20), float(1 << 20), ALU.mult, ALU.add))
            c.link(dve.tensor_tensor(slf, base, pos, ALU.add))
            c.link(dve.tensor_tensor(slf, slf, kept, ALU.add))
            c.link(dve.tensor_copy(slotw, slf))
            c.link(dve.tensor_scalar(pos, pos, float(CAP), None, ALU.min))
            c.link(dve.tensor_scalar(base, ms, -float(2 * HALF), float(EXPERTS * 2 * HALF - 1), ALU.mult, ALU.add))
            c.link(dve.tensor_tensor(slf, base, pos, ALU.add))
            c.link(dve.tensor_copy(slotr, slf))
            dve.sem_inc(s["slots_ready"], 1)
            def add_bias(m, first):
                for r in range(2):
                    dve.wait_ge(w_ex[r], m * (5 * 16) + 5 * 16)
                    if r or not first:
                        dve.wait_ge(s["y_st"], m * 64 + r * 32)
                    for t in range(CT):
                        n = min(P, 2 * HALF - t * P)
                        bank = (psA, psT)[t % 2]
                        dve.wait_ge(s["y_mm"], m * (2 * CT) + (r * CT + t + 1 + 2 * CT))
                        dve.tensor_tensor(yb[0:n, t, :], bank[0:n, 0:D], b2b[0:n, r, :], ALU.add
                                          ).then_inc(s["y_ev"], 1)

            rounds(dve, EXPERTS // 2, add_bias)
            fc = Chain(dve, s["final"], 6)
            def combine(m, first):
                for r in range(EU):
                    fc.at(m * EU + r)
                    dve.wait_ge(yg_in[r], m * 16 + 16)
                    fc.link(dve.tensor_scalar(ty, yg[:, r, :], wgt[:, ds(m * EU + r, 1)], None, ALU.mult))
                    fc.inc(dve.tensor_scalar(fin, ty, 0.0, 0.0, ALU.mult, ALU.is_equal))
                    fc.inc(dve.tensor_scalar(cl, ty, HUGE, 10000.0, ALU.is_ge, ALU.mult))
                    fc.link(dve.tensor_scalar(nn, ty, -HUGE, -10000.0, ALU.is_le, ALU.mult))
                    fc.link(dve.tensor_tensor(cl, cl, nn, ALU.add))
                    held(dve)
                    fc.link(dve.copy_predicated(cl, fin.bitcast(I32), ty))
                    dve.wait_ge(x2_in[r], m * 16 + 16)
                    if not first:
                        dve.wait_ge(o_st[r], m * 16)
                    dve.tensor_tensor(fo[:, r, :], cl, x2b[:, r, :], ALU.add).then_inc(s["fo_done"], 1)
                    dve.wait_ge(s["fo_done"], m * EU + (r + 1 + EU))

            rounds(dve, SROUNDS, combine)

        block = ctx.enter_context(nc.Block())

        @block.sync
        def _(sp):
            sp.dma_start(lastI[0:KH, :], a["last"].to_broadcast([KH, SUPER - 1])).then_inc(s["last_in"], 16)
            sp.wait_ge(s["steps_ready"], 1)
            for g in range(2):
                for h in range(HEADS):
                    sp.dma_start(res_dram[g * KH * HEADS + h:(g + 1) * KH * HEADS:HEADS, :],
                                 res2[0:KH, g, :]).then_inc(s["setup_st"], 16)
                for i in range(3):
                    sp.dma_start(meta_dram[i:i + 1, g * KH:(g + 1) * KH].rearrange("a k -> k a"),
                                 small3[0:KH, g, i:i + 1], allow_slow_non_contiguous=True).then_inc(s["setup_st"], 16)
            sp.wait_ge(s["setup_st"], 2 * (HEADS + 3) * 16)
            for i in range(3):
                sp.dma_start(row[i][0:HEADS, :], meta_dram[i:i + 1, :].to_broadcast([HEADS, STEPS])
                             ).then_inc(s["rows_in"], 16)
            sp.wait_ge(s["rows_ready"], 1)
            sp.dma_start(meta_dram[3:4, :], row[9][0:1, :]).then_inc(s["setup_st"], 16)
            sp.wait_ge(s["setup_st"], 2 * (HEADS + 3) * 16 + 16)
            for i in range(U):
                sp.dma_start(crossc[i * HEADS:(i + 1) * HEADS, :],
                             meta_dram[3:4, i:STEPS:U].to_broadcast([HEADS, NB]),
                             allow_slow_non_contiguous=True).then_inc(s["cross_in"], 16)
            with sp.Fori(0, LOOPS) as m:
                for r in range(EU):
                    sp.wait_ge(s["ln_done"], m * EU + r + 1)
                    sp.dma_start(lx[:, r, :, :], a["x"][ds((m * EU + r) * 2 * P, 2 * P), :]
                                 .rearrange("(n p) d -> p n d", n=2)).then_inc(x_in[r], 16)
            with sp.Fori(0, LAYERS) as l:
                for i in range(EU):
                    sp.wait_ge(h_st[i], (l + 1) * (16 * LOOPS))
                for c in range(2):
                    sp.dma_start(wcat[:, c, :], a["wcat"][ds(l * D + c * P, P), :]).then_inc(s["w_in"], 16)
                sp.dma_start(bias_bc[:, :], a["bcat"][ds(l, 1), :].to_broadcast([P, 4 * D])).then_inc(s["w_in"], 16)
                sp.dma_start(we_bc[:, :], a["we"][ds(l, 1), :].to_broadcast([P, D])).then_inc(s["w_in"], 16)
                for i in range(3):
                    sp.dma_start(wb_bc[:, i, :], a["wbeta"][ds(l * 3 + i, 1), :].to_broadcast([P, D])
                                 ).then_inc(s["w_in"], 16)
                with sp.Fori(0, PAIRS) as m:
                    for r in range(2):
                        sp.wait_ge(s["tr_done"], l * NBLK + m * 2 + r + 1)
                        sp.dma_start(hb[:, r, :], h_dram[ds((m * 2 + r) * P, P), :]).then_inc(hb_in[r], 16)
                for r in range(2):
                    sp.wait_ge(pst[r], (l + 1) * (PAIRS * 32))
                held(sp)

                def body(an, bn):
                    if an is None:
                        return
                    blocks = []
                    for i in range(U):
                        blocks.append(sp.value_load(blkI[0:1, ds(an.k(i), 1)], min_val=0,
                                                    max_val=NBLK - 1))
                    for i, b in enumerate(blocks):
                        sp.wait_ge(s["q_ready"], (an.n(i) + 1) * 2)
                        sp.dma_start(qring[:, i, :], qx_dram[ds(b * P, P), 2 * D - D:QX]).then_inc(q_in[i], 16)
                    sp.wait_ge(s["scanned"], an.g + START)
                    sp.dma_start(res[:, :], res_dram[ds(an.k(0) * HEADS, PB), :]).then_inc(s["res_in"], 16)

                edge_loop(sp, l, body)
                sp.wait_ge(s["acc_done"], (l + 1) * STEPS + START)
                held(sp)
                with sp.Fori(0, LOOPS) as m:
                    for r in range(EU):
                        sp.wait_ge(s["hout_ready"], l * PAIRS + m * EU + r + 1)
                        sp.dma_start(xr[:, r, :, :], qx_dram[ds((m * EU + r) * 2 * P, 2 * P), 0:D]
                                     .rearrange("(n p) d -> p n d", n=2)).then_inc(xr_in[r], 16)
            moe_sync(sp)

        @block.gpsimd
        def _(pool):
            for name, n in (("q_ready", 2 * U), ("agg_done", 2 * U), ("v_used", 2 * U), ("qb_free", 2), ("tr_done", 2),
                            ("mm_done", 2), ("ev_done", 2), ("hout_ready", EU), ("ln_done", EU), ("y_mm", 2 * CT),
                            ("y_ev", 2), ("fo_done", EU)):
                pool.sem_inc(s[name], n)
            for name in ("scanned", "hT_done", "pb_done", "w_dve", "acc_done", "oh_done", "chain_B", "act_B", "h_cp"):
                pool.sem_inc(s[name], START)
            pool.iota(iota_i[:, :], [[1, SUPER]], base=0, channel_multiplier=0).then_inc(s["iotas"], 1)
            pool.iota(part_i[:, 0:1], [[1, 1]], base=0, channel_multiplier=1).then_inc(s["iotas"], 1)
            pool.iota(part_i[:, 1:3], [[KH, 2]], base=0, channel_multiplier=1).then_inc(s["iotas"], 1)
            pool.iota(sel_i[0:PB, 0:HEADS], [[-1, HEADS]], base=0, channel_multiplier=1).then_inc(s["iotas"], 1)
            pool.iota(sel_i[0:PB, HEADS:HEADS + U], [[-HEADS, U]], base=0, channel_multiplier=1
                      ).then_inc(s["iotas"], 1)
            pool.iota(sel_i[0:HEADS, HEADS + U:], [[0, U], [1, HEADS]], base=0, channel_multiplier=-1
                      ).then_inc(s["iotas"], 1)
            pool.memset(ones[:, :], 1.0).then_inc(s["iotas"], 1)
            pool.memset(Us[:, :], 0.0).then_inc(s["iotas"], 1)
            pool.memset(G[:, :, :, :, :].rearrange("p r i j n -> p (r i j n)"), 0.0).then_inc(s["zeros"], 1)
            pool.wait_ge(s["zeros"], 1)
            ZW = 2 * U * J * P
            flat_slots = slots_dram.rearrange("(p r) d -> p (r d)", p=P)
            for i in range(ZERO_DMAS):
                pool.dma_start(flat_slots[:, i * ZW:(i + 1) * ZW], G[:, :, :, :, :].rearrange(
                    "p r i j n -> p (r i j n)")).then_inc(s["zero_st"], 16)
            pool.wait_ge(s["t_ready"], 1)
            for g in range(2):
                for name, dst in (("dst", rawI), ("src", srcR), ("ew", ewF)):
                    pool.indirect_dma_start(dst[0:KH, g, :], None, a[name],
                                            bass.IndirectOffsetOnAxis(ap=tI[0:KH, g:g + 1], axis=0)
                                            ).then_inc(s["steps_in"], 16)
            with pool.Fori(0, LOOPS) as m:
                for r in range(EU):
                    pool.wait_ge(s["ln_done"], m * EU + r + 1 + EU)
                    pool.dma_start(h_dram[ds((m * EU + r) * 2 * P, 2 * P), :].rearrange("(n p) d -> p n d", n=2),
                                   ly[:, r, :, :]).then_inc(h_st[r], 16)
            with pool.Fori(0, LAYERS) as l:
                pool.wait_ge(s["hout_ready"], l * PAIRS + EU)
                for i in range(EU):
                    pool.wait_ge(h_st[i], (l + 1) * (16 * LOOPS))
                pool.wait_ge(s["rows_used"], 1)
                held(pool)
                pool.memset(accT[:, :], 0.0).then_inc(s["acc_zero"], 1)
                with pool.Fori(0, PAIRS) as m:
                    for r in range(2):
                        pool.wait_ge(s["pout"], l * NBLK + m * 2 + r + 1)
                        pool.dma_start(kv_dram[ds((m * 2 + r) * P, P), :], kvb[:, r, :]).then_inc(pst[r], 16)
                        pool.dma_start(qx_dram[ds((m * 2 + r) * P, P), :], qxb[:, r, :]).then_inc(pst[r], 16)
                for r in range(2):
                    pool.wait_ge(pst[r], (l + 1) * (PAIRS * 32))
                held(pool)

                def body(an, bn):
                    if an is None:
                        return
                    for i in range(U):
                        pool.wait_ge(s["v_used"], an.n(i) + 1)
                        held(pool)
                        pool.tensor_copy(idxb[:, an.par, i, :], srcI[:, ds(an.k(i), 1), :].rearrange(
                            "p k j -> p (k j)")).then_inc(s["idx_done"], 1)
                        pool.wait_ge(s["idx_done"], an.n(i) + 1)
                        held(pool)
                        for j in range(J):
                            pool.indirect_dma_start(
                                kv[:, an.par, i, j, :], None, kv_dram,
                                bass.IndirectOffsetOnAxis(ap=idxb[:, an.par, i, j:j + 1], axis=0)
                            ).then_inc(kv_in[an.par][i], 16)

                edge_loop(pool, l, body)
                with pool.Fori(0, LOOPS) as m:
                    for r in range(EU):
                        pool.wait_ge(s["hout_ready"], l * PAIRS + m * EU + r + 1 + EU)
                        pool.dma_start(h_dram[ds((m * EU + r) * 2 * P, 2 * P), :]
                                       .rearrange("(n p) d -> p n d", n=2), hout[:, r, :, :]).then_inc(h_st[r], 16)
            moe_pool(pool)

        @block.scalar
        def _(act):
            with act.Fori(0, LOOPS) as m:
                for r in range(EU):
                    act.wait_ge(s["ln_var"], m * EU + r + 1)
                    act.activation(sd[:, :], ve[:, :], ACT.Sqrt).then_inc(s["ln_sd"], 1)
            act.wait_ge(s["setup_done"], 1)
            act.wait_ge(s["zero_st"], ZERO_DMAS * 16)
            with act.Fori(0, LAYERS) as l:
                with act.Fori(0, PAIRS) as m:
                    for r in range(2):
                        gi = l * NBLK + m * 2 + r
                        act.wait_ge(s["tr_done"], gi + 1 + 2)
                        act.wait_ge(s["mm_done"], gi + 1)
                        act.activation(hT[:, r, :, :].rearrange("p c t -> p (c t)"), psG[:, 0:D], ACT.Copy
                                       ).then_inc(s["hT_done"], 1)

                def build_G(an, i):
                    act.wait_ge(s["agg_done"], an.n(i) + 1)
                    for j in range(J):
                        act.activation(G[:, an.par, i, j, :], iota_r[:, :], ACT.Abs,
                                       bias=ndl[:, ds(an.k(i), 1), j]).then_inc(s["g_abs"], 1)
                    act.wait_ge(s["g_abs"], (an.n(i) + 1) * J)
                    flat = G[:, an.par, i, :, :].rearrange("p j n -> p (j n)")
                    act.activation(flat, flat, ACT.Relu, bias=1.0, scale=-1.0).then_inc(s["g_ready"], 1)

                def copy_OH(an, i):
                    act.wait_ge(s["gt_done"], an.n(i) + 1)
                    act.wait_ge(s["q_ready"], an.n(i) * 2 - 2 + 2 * U)
                    act.activation(OH[:, i % 2, :, :].rearrange("p j e -> p (j e)"), psG[:, :], ACT.Copy
                                   ).then_inc(s["oh_done"], 1)

                def body(an, bn):
                    if an is not None:
                        build_G(an, 0)
                        build_G(an, 1)
                        for i in range(U - 1):
                            copy_OH(an, i)
                            if i + 2 < U:
                                build_G(an, i + 2)
                    if bn is not None:
                        act.wait_ge(s["chain_B"], bn.g * KB + 10 + START)
                        act.wait_ge(s["pb_done"], bn.g + START)
                        act.activation(pT[:, :], Dm[:, :], ACT.Exp, scale=SCALE).then_inc(s["act_B"], 1)
                        act.wait_ge(s["chain_B"], bn.g * KB + 11 + START)
                        act.activation(gx[:, :], gd[:, :], ACT.Exp, scale=SCALE).then_inc(s["act_B"], 1)
                    if an is not None:
                        copy_OH(an, U - 1)
                    if bn is not None:
                        act.wait_ge(s["pb_done"], bn.g + 1 + START)
                        act.wait_ge(s["w_dve"], bn.g * U + START)
                        act.wait_ge(s["acc_done"], bn.g * U + START)
                        act.activation(pB[:, :, :, :].rearrange("p j s h -> p (j s h)"),
                                       psB[:, 128:128 + J * PB], ACT.Copy).then_inc(s["act_B"], 1)
                        act.activation(fB[:, :, :].rearrange("p s h -> p (s h)"), psB[:, 64:64 + PB], ACT.Copy,
                                       bias=1.0).then_inc(s["act_B"], 1)
                        act.wait_ge(s["act_B"], bn.g * KACT + KACT + START)
                        for i in range(U):
                            act.wait_ge(s["agg_done"], bn.n(i) - 1 + 2 * U)
                            act.activation(W[:, i % 2, :, :, HD], pB[:, :, i, :], ACT.Copy).then_inc(s["w_act"], 1)

                edge_loop(act, l, body)
                with act.Fori(0, LOOPS) as m:
                    for r in range(EU):
                        act.wait_ge(s["z_ready"], l * PAIRS + m * EU + r + 1)
                        act.activation(ez[:, :], zc[:, :], ACT.Exp, scale=-1.0).then_inc(s["z_exp"], 1)
            moe_act(act)

        @block.tensor
        def _(pe):
            pe.wait_ge(s["steps_ready"], 1)
            for g in range(2):
                for i, arr in enumerate((srcF, dloc, ewF)):
                    bank = (psQ[:, 0, :], psQ[:, 1, :], psQ[:, 2, :], psQ[:, 3, :], psG[:, :], psA[:, :])[3 * g + i]
                    for j in range(J):
                        last = pe.transpose(bank[:, j * P:j * P + KH], arr[0:KH, g, j:SE:J], ident[0:KH, 0:KH])
                    last.then_inc(s["setup_t"], 1)
            pe.wait_ge(s["setup_done"], 1)
            with pe.Fori(0, LAYERS) as l:
                pe.wait_ge(s["w_in"], (l + 1) * (7 * 16))
                held(pe)
                with pe.Fori(0, PAIRS) as m:
                    for r in range(2):
                        gi = l * NBLK + m * 2 + r
                        pe.wait_ge(hb_in[r], (l * PAIRS + m + 1) * 16)
                        pe.wait_ge(s["hT_done"], gi + START)
                        for c in range(2):
                            last = pe.transpose(psG[:, c * P:(c + 1) * P], hb[:, r, c * P:(c + 1) * P], ident[:, :])
                        last.then_inc(s["tr_done"], 1)
                        pe.wait_ge(s["hT_done"], gi + 1 + START)
                        pe.wait_ge(s["ev_done"], gi + 1)
                        for half in range(2):
                            for c in range(2):
                                last = pe.matmul(psQ[:, 2 * r + half, :], hT[:, r, c, :],
                                                 wcat[:, c, half * 2 * D:(half + 1) * 2 * D],
                                                 start=(c == 0), stop=(c == 1))
                        last.then_inc(s["mm_done"], 1)

                def turn_G(an, i):
                    pe.wait_ge(s["g_ready"], an.n(i) + 1)
                    pe.wait_ge(s["oh_done"], an.n(i) + START)
                    for j in range(J):
                        last = pe.transpose(psG[:, j * P:(j + 1) * P], G[:, an.par, i, j, :], ident[:, :])
                    last.then_inc(s["gt_done"], 1)

                def expand_q(an, i):
                    pe.wait_ge(s["oh_done"], an.n(i) + 1 + START)
                    pe.wait_ge(q_in[i], (an.g + 1) * 16)
                    for jj in range(2):
                        pe.wait_ge(s["qb_free"], an.n(i) * 2 + jj + 1)
                        for j in (2 * jj, 2 * jj + 1):
                            last = pe.matmul(psQ[:, j, 0:QW], OH[:, i % 2, j, :], qring[:, i, :],
                                             start=True, stop=True)
                        last.then_inc(s["q_ready"], 1)

                def body(an, bn):
                    if an is not None:
                        turn_G(an, 0)
                        turn_G(an, 1)
                        expand_q(an, 0)
                    if bn is not None:
                        pe.wait_ge(s["alpha_ready"], (bn.g + 1) * U)
                        pe.wait_ge(s["chain_B"], bn.g * KB + START)
                        for j in range(J):
                            last = pe.transpose(psT[0:PB, j:SE:J], alpha[:, bn.par, j, :, :].rearrange(
                                "p s h -> p (s h)"), ident[:, :])
                        last.then_inc(s["at_done"], 1)
                    if an is not None:
                        turn_G(an, 2)
                        expand_q(an, 1)
                    if bn is not None:
                        pe.wait_ge(s["act_B"], bn.g * KACT + START)
                        pe.wait_ge(s["chain_B"], bn.g * KB + 2 + START)
                        held(pe)
                        pe.matmul(psB[0:HEADS, 0:U], selA[:, :], LB[:, :], start=True, stop=True
                                  ).then_inc(s["max_up"], 1)
                        pe.wait_ge(s["chain_B"], bn.g * KB + 5 + START)
                        held(pe)
                        pe.matmul(psB[0:PB, 32:33], lhs2[:, :, :].rearrange("a s h -> a (s h)"), ones[0:HEADS, 0:1],
                                  start=True, stop=True).then_inc(s["max_down"], 1)
                    if an is not None:
                        for i in range(2, U):
                            if i + 1 < U:
                                turn_G(an, i + 1)
                            expand_q(an, i)
                    if bn is not None:
                        pe.wait_ge(s["chain_B"], bn.g * KB + KB + START)
                        held(pe)
                        pe.matmul(psB[:, 64:64 + PB], crossOH[:, :], gm[:, :], start=True, stop=True)
                        pe.wait_ge(s["act_B"], bn.g * KACT + 1 + START)
                        held(pe)
                        for j in range(J):
                            last = pe.transpose(psB[:, 128 + j * PB:128 + (j + 1) * PB], pT[:, j:SE:J],
                                                ident[0:PB, 0:PB])
                        last.then_inc(s["pb_done"], 1)
                        for i in range(U):
                            pe.wait_ge(s["w_dve"], bn.n(i) + 1 + START)
                            pe.wait_ge(s["w_act"], bn.n(i) + 1)
                            pe.wait_ge(s["acc_done"], bn.n(i) + START)
                            for j in range(J):
                                last = pe.matmul(psA[:, 0:HEADS * AW], G[:, bn.par, i, j, :],
                                                 W[:, i % 2, j, :, :].rearrange("p h w -> p (h w)"),
                                                 start=(j == 0), stop=(j == J - 1))
                            last.then_inc(s["agg_done"], 1)

                edge_loop(pe, l, body)
            moe_pe(pe)

        @block.vector
        def _(dve):
            setup = Chain(dve, s["setup_chain"])
            dve.wait_ge(s["iotas"], 8)
            dve.tensor_copy(iota_r[:, :], iota_i[:, 0:P])
            dve.tensor_copy(iota_c[:, :], part_i[:, 0:1])
            dve.tensor_copy(kcol[:, :], part_i[:, 1:3])
            nsA, nsB = sel_i[0:PB, 0:HEADS], sel_i[0:PB, HEADS:HEADS + U]
            dve.tensor_scalar(nsA, nsA, 7, None, ALU.bitwise_and)
            setup.link(dve.tensor_scalar(nsB, nsB, 3, None, ALU.arith_shift_right))
            dve.tensor_scalar(selA[:, :], nsA, 0.0, None, ALU.is_equal)
            dve.tensor_scalar(selB[:, :], nsB, 0.0, None, ALU.is_equal)
            dve.tensor_scalar(selD[:, :, :].rearrange("a s h -> a (s h)"), sel_i[0:HEADS, HEADS + U:], 0.0, None,
                              ALU.is_equal)
            dve.tensor_scalar(ident[:, :], iota_r[:, :], iota_c[:, 0:1], None, ALU.is_equal)
            dve.tensor_scalar(tri[:, :], iota_r[:, :], iota_c[:, 0:1], None, ALU.is_ge)
            dve.tensor_scalar(e8[:, :], iota_r[:, 0:EXPERTS], -1.0, float(EXPERTS), ALU.mult, ALU.add)
            dve.wait_ge(s["last_in"], 16)
            setup.link(dve.tensor_scalar(lastI[0:KH, :], lastI[0:KH, :], 7, None, ALU.logical_shift_right))
            setup.link(dve.tensor_copy(posA[0:KH, :], lastI[0:KH, :]))
            setup.link(dve.tensor_copy(cmpT[0:KH, :], iota_i[0:KH, 0:SUPER - 1]))
            setup.link(dve.tensor_tensor(posA[0:KH, :], posA[0:KH, :], cmpT[0:KH, :], ALU.add))
            for g in range(2):
                setup.link(dve.tensor_scalar(cmpT[0:KH, :], posA[0:KH, :], kcol[0:KH, g:g + 1], None, ALU.is_lt))
                setup.link(dve.tensor_reduce(tcol[0:KH, g:g + 1], cmpT[0:KH, :], AX, ALU.add))
            setup.link(dve.tensor_copy(tI[0:KH, :], tcol[0:KH, :]))
            dve.sem_inc(s["t_ready"], 1)
            setup.link(dve.tensor_tensor(nbc[0:KH, :], kcol[0:KH, :], tcol[0:KH, :], ALU.subtract))
            setup.link(dve.tensor_scalar(small3[0:KH, :, 2], nbc[0:KH, :], float(NBLK - 1), None, ALU.min))
            setup.link(dve.tensor_scalar(nbc[0:KH, :], small3[0:KH, :, 2], -float(P), None, ALU.mult))
            dve.wait_ge(s["steps_in"], 6 * 16)
            dve.tensor_copy(dstF[0:KH, :, :], rawI[0:KH, :, :])
            setup.link(dve.tensor_copy(srcF[0:KH, :, :], srcR[0:KH, :, :]))
            for g in range(2):
                dve.tensor_copy(small3[0:KH, g, 0:1], dstF[0:KH, g, 0:1])
                dve.tensor_copy(small3[0:KH, g, 1:2], dstF[0:KH, g, SE - 1:SE])
                setup.link(dve.tensor_scalar(dloc[0:KH, g, :], dstF[0:KH, g, :], nbc[0:KH, g:g + 1], -1.0,
                                             ALU.add, ALU.max))
                setup.link(dve.tensor_scalar(dloc[0:KH, g, :], dloc[0:KH, g, :], float(P), None, ALU.min))
                dve.memset(res2[0:KH, g, 0:1], 0.0)
                dve.memset(res2[0:KH, g, SE:SE + 1], 0.0)
                setup.link(dve.tensor_tensor(res2[0:KH, g, 1:SE], dloc[0:KH, g, 1:SE], dloc[0:KH, g, 0:SE - 1],
                                             ALU.not_equal))
                setup.link(dve.tensor_scalar(res2[0:KH, g, 1:SE], res2[0:KH, g, 1:SE], -BIG, None, ALU.mult))
            dve.sem_inc(s["steps_ready"], 1)
            for g in range(2):
                for i, dst in enumerate((srcI, ndl, ewT)):
                    bank = (psQ[:, 0, :], psQ[:, 1, :], psQ[:, 2, :], psQ[:, 3, :], psG[:, :], psA[:, :])[3 * g + i]
                    dve.wait_ge(s["setup_t"], 3 * g + i + 1)
                    o_ = dst[:, g * KH:(g + 1) * KH, :].rearrange("p k j -> p j k")
                    b_ = bank.rearrange("p (j k) -> p j k", j=J)[:, :, 0:KH]
                    if i == 1:
                        dve.tensor_scalar(o_, b_, -1.0, None, ALU.mult)
                    else:
                        dve.tensor_copy(o_, b_)
            r_first, r_last, r_blk, cont, whole, t0, t1, t2, t3, crs = [x[0:HEADS, :] for x in row]
            dve.wait_ge(s["rows_in"], 3 * 16)
            dve.tensor_copy(blkI[:, :], r_blk[0:1, :])
            dve.memset(cont[:, 0:1], 0.0)
            setup.link(dve.tensor_tensor(cont[:, 1:], r_blk[:, 1:], r_blk[:, :STEPS - 1], ALU.is_equal))
            setup.link(dve.tensor_tensor(t0[:, 1:], r_first[:, 1:], r_last[:, :STEPS - 1], ALU.is_equal))
            setup.link(dve.tensor_tensor(cont[:, 1:], cont[:, 1:], t0[:, 1:], ALU.mult))
            setup.link(dve.tensor_tensor(whole, r_first, r_last, ALU.is_equal))
            setup.link(dve.tensor_tensor(whole, whole, cont, ALU.mult))
            dve.tensor_scalar(dn8[:, :], cont, 1.0, BIG, ALU.subtract, ALU.mult)
            dve.tensor_scalar(dd8[:, :], whole, 1.0, BIG, ALU.subtract, ALU.mult)
            setup.link(dve.tensor_scalar(t1, r_blk, -float(P), 1.0, ALU.mult, ALU.add))
            setup.link(dve.tensor_tensor(t1, t1, r_first, ALU.add))
            setup.link(dve.tensor_tensor(t1, t1, cont, ALU.mult))
            setup.link(dve.tensor_scalar(crs, t1, 1.0, None, ALU.subtract))
            dve.sem_inc(s["rows_ready"], 1)
            dve.wait_ge(s["setup_st"], 2 * (HEADS + 3) * 16 + 16)
            dve.sem_inc(s["rows_used"], 1)
            dve.sem_inc(s["setup_done"], 1)

            ln = Chain(dve, s["ln_chain"], 3)

            def layer_norm(x, y, it, free, n_free):
                ln.at(it)
                for n in range(2):
                    last = dve.bn_stats(stats[:, n, :], x[:, n, :])
                ln.link(last)
                held(dve)
                for n in range(2):
                    last = dve.bn_aggr(mv[:, n, :], stats[:, n, :])
                ln.link(last)
                dve.tensor_scalar(ve[:, :], mv[:, :, 1], 1e-5, None, ALU.add).then_inc(s["ln_var"], 1)
                dve.wait_ge(s["ln_sd"], it + 1)
                ln.link(dve.reciprocal(rstd[:, :], sd[:, :]))
                if free is not None:
                    dve.wait_ge(free, n_free)
                for n in range(2):
                    last = dve.tensor_scalar(y[:, n, :], x[:, n, :], mv[:, n, 0:1], rstd[:, n:n + 1],
                                             ALU.subtract, ALU.mult)
                last.then_inc(s["ln_done"], 1)

            def input_norm(m, first):
                for r in range(EU):
                    dve.wait_ge(x_in[r], (m + 1) * 16)
                    layer_norm(lx[:, r, :, :], ly[:, r, :, :], m * EU + r, None if first else h_st[r], m * 16)

            rounds(dve, LOOPS, input_norm)

            with dve.Fori(0, LAYERS) as l:
                dve.wait_ge(s["w_in"], (l + 1) * (7 * 16))
                dve.tensor_tensor(wA[:, :], wb_bc[:, 0, :], wb_bc[:, 2, :], ALU.add)
                dve.tensor_tensor(wB[:, :], wb_bc[:, 1, :], wb_bc[:, 2, :], ALU.subtract)
                held(dve)
                pc = Chain(dve, s["proj_chain"], 1)
                def project(m, first):
                    for r in range(2):
                        gi = l * NBLK + m * 2 + r
                        pc.at(gi)
                        dve.wait_ge(s["mm_done"], gi + 1 + 2)
                        if not first:
                            dve.wait_ge(pst[r], (l * PAIRS + m) * 32)
                        dve.tensor_tensor(kvb[:, r, :], psQ[:, 2 * r, :], bias_bc[:, 0:2 * D], ALU.add)
                        dve.tensor_tensor(qxb[:, r, 0:2 * D], psQ[:, 2 * r + 1, :], bias_bc[:, 2 * D:],
                                          ALU.add).then_inc(s["ev_done"], 1)
                        dve.wait_ge(s["ev_done"], gi + 1 + 2)
                        pc.link(dve.tensor_tensor(qprod, qxb[:, r, D:2 * D], we_bc[:, :], ALU.mult))
                        dve.tensor_reduce(qxb[:, r, 2 * D:QX], qprod.rearrange("p (h d) -> p h d", h=HEADS),
                                          AX, ALU.add).then_inc(s["pout"], 1)

                rounds(dve, PAIRS, project)
                dve.wait_ge(s["acc_zero"], l + 1)
                dve.wait_ge(s["cross_in"], U * 16)

                def scores(an, i):
                    for jj in range(2):
                        dve.wait_ge(s["q_ready"], an.n(i) * 2 + jj + 1 + 2 * U)
                        if jj == 0:
                            dve.wait_ge(kv_in[an.par][i], (an.use + 1) * (16 * J))
                        jr = slice(2 * jj, 2 * jj + 2)
                        dve.tensor_tensor(prod[:, i % 2, jr, :], psQ[:, jr, 0:D], kv[:, an.par, i, jr, 0:D], ALU.mult)
                        dve.tensor_tensor(al2[:, i % 2, jr, :], psQ[:, jr, D:QW],
                                          ewT[:, ds(an.k(i), 1), jr].rearrange("p k j -> p (k j)").unsqueeze(2)
                                          .to_broadcast([P, 2, HEADS]), ALU.mult).then_inc(s["qb_free"], 1)
                    dve.wait_ge(s["qb_free"], (an.n(i) + 1) * 2 + 2)
                    dve.tensor_reduce(al1[:, i % 2, :, :], prod[:, i % 2, :, :].rearrange("p j (h d) -> p j h d", h=HEADS),
                                      AX, ALU.add).then_inc(s["chain_A"], 1)
                    dve.wait_ge(s["chain_A"], an.n(i) + 1)
                    dve.tensor_tensor(alpha[:, an.par, :, i, :], al1[:, i % 2, :, :], al2[:, i % 2, :, :], ALU.add
                                      ).then_inc(s["alpha_ready"], 1)

                cb = Chain(dve, s["chain_B"], KB, START)

                def maxima_1(bn):
                    cb.at(bn.g)
                    dve.wait_ge(s["res_in"], (bn.g + 1) * 16)
                    dve.wait_ge(s["at_done"], bn.g + 1)
                    cb.link(dve.tensor_tensor_scan(F1[:, :], res[:, 0:SE], psT[0:PB, :], -BIG, ALU.add, ALU.max))
                    cb.inc(dve.tensor_scalar(LB[:, :], selB[:, :], F1[:, SE - 1:SE], None, ALU.mult))

                def maxima_2(bn):
                    dve.wait_ge(s["max_up"], bn.g + 1)
                    cb.link(dve.tensor_tensor_scan(Us[:, 1:], dd8[:, ds(bn.k(0), U)], psB[0:HEADS, 0:U], Us[:, 0:1],
                                                   ALU.add, ALU.max))
                    cb.link(dve.tensor_tensor(cc[:, :], Us[:, 0:U], dn8[:, ds(bn.k(0), U)], ALU.add))
                    cb.inc(dve.tensor_tensor(lhs2[:, :, :], selD[:, :, :],
                                             cc[:, :].unsqueeze(2).to_broadcast([HEADS, U, HEADS]), ALU.mult))
                    cb.inc(dve.tensor_copy(Us[:, 0:1], Us[:, U:U + 1]))

                def maxima_3(bn):
                    dve.wait_ge(s["max_down"], bn.g + 1)
                    cb.link(dve.tensor_copy(ccol[:, :], psB[0:PB, 32:33]))
                    cb.link(dve.tensor_tensor_scan(F2[:, :], res[:, 0:SE], psT[0:PB, :], ccol[:, 0:1],
                                                   ALU.add, ALU.max))
                    cb.inc(dve.tensor_tensor_scan(M[:, ::-1], res[:, SE:0:-1], F2[:, ::-1], -BIG,
                                                  ALU.add, ALU.max))
                    cb.wait()
                    dve.sem_inc(s["scanned"], 1)
                    cb.inc(dve.tensor_tensor(Dm[:, :], psT[0:PB, :], M[:, :], ALU.subtract))
                    cb.inc(dve.tensor_tensor(gd[:, :], ccol[:, :], M[:, 0:1], ALU.subtract))

                def maxima_4(bn):
                    cb.inc(dve.tensor_scalar(crossOH[:, :], iota_r[0:PB, :], crossc[:, ds(bn.B, 1)], None,
                                             ALU.is_equal))
                    dve.wait_ge(s["act_B"], bn.g * KACT + 2 + START)
                    cb.inc(dve.scalar_tensor_tensor(gm[:, :], ident[0:PB, 0:PB], gx[:, 0:1], ident[0:PB, 0:PB],
                                                    ALU.mult, ALU.subtract))

                def weigh(bn, i):
                    dve.wait_ge(s["act_B"], bn.g * KACT + 3 + START)
                    dve.wait_ge(s["agg_done"], bn.n(i) - 1 + 2 * U)
                    dve.tensor_tensor(W[:, i % 2, :, :, 0:HD],
                                      kv[:, bn.par, i, :, D:2 * D].rearrange("p j (h d) -> p j h d", h=HEADS),
                                      pB[:, :, i, :].unsqueeze(3).to_broadcast([P, J, HEADS, HD]), ALU.mult
                                      ).then_inc(s["v_used"], 1)
                    dve.tensor_tensor(W[:, i % 2, :, :, HD + 1], pB[:, :, i, :],
                                      ewT[:, ds(bn.k(i), 1), :].rearrange("p k j -> p (k j)").unsqueeze(2)
                                      .to_broadcast([P, J, HEADS]), ALU.mult).then_inc(s["w_dve"], 1)

                def add_up(bn, i):
                    b = dve.value_load(blkI[0:1, ds(bn.k(i), 1)], min_val=0, max_val=NBLK - 1)
                    here = acc[:, ds(b, 1), :, :].rearrange("p b h w -> p (b h) w")
                    dve.wait_ge(s["act_B"], bn.g * KACT + 4 + START)
                    dve.wait_ge(s["acc_done"], bn.n(i) + START)
                    dve.tensor_tensor(here, here, fB[:, i, :].unsqueeze(2).to_broadcast([P, HEADS, AW]), ALU.mult
                                      ).then_inc(s["scaled"], 1)
                    dve.wait_ge(s["scaled"], bn.n(i) + 1)
                    dve.wait_ge(s["agg_done"], bn.n(i) + 1 + 2 * U)
                    dve.tensor_tensor(here, here, psA[:, 0:HEADS * AW].rearrange("p (h w) -> p h w", h=HEADS),
                                      ALU.add).then_inc(s["acc_done"], 1)

                def body(an, bn):
                    if an is not None:
                        scores(an, 0)
                    if bn is not None:
                        maxima_1(bn)
                    if an is not None:
                        scores(an, 1)
                    if bn is not None:
                        maxima_2(bn)
                    if an is not None:
                        for i in range(2, U - 1):
                            scores(an, i)
                    if bn is not None:
                        maxima_3(bn)
                    if an is not None:
                        scores(an, U - 1)
                    if bn is not None:
                        maxima_4(bn)
                        weigh(bn, 0)
                        for i in range(U):
                            if i + 1 < U:
                                weigh(bn, i + 1)
                            add_up(bn, i)

                edge_loop(dve, l, body)

                dve.wait_ge(s["acc_done"], (l + 1) * STEPS + START)
                held(dve)
                ep = Chain(dve, s["ep_chain"], 12)
                with dve.Fori(0, LOOPS) as m:
                    for r in range(EU):
                        it = l * PAIRS + m * EU + r
                        ep.at(it)
                        two = acc[:, ds((m * EU + r) * 2, 2), :, :]
                        bc = lambda x: x.unsqueeze(3).to_broadcast([P, 2, HEADS, HD])
                        split = lambda x: x.rearrange("p n (h d) -> p n h d", h=HEADS)
                        over = lambda w: w[:, :].unsqueeze(1).to_broadcast([P, 2, D])
                        ep.link(dve.tensor_scalar(den[:, :, :], two[:, :, :, HD], 1e-16, None, ALU.add))
                        ep.link(dve.reciprocal(rden[:, :, :], den[:, :, :]))
                        ep.inc(dve.tensor_tensor(tew[:, :, :], two[:, :, :, HD + 1], rden[:, :, :], ALU.mult))
                        ep.link(dve.tensor_tensor(split(ov), two[:, :, :, 0:HD], bc(rden[:, :, :]), ALU.mult))
                        ep.link(dve.tensor_tensor(split(tw), split(over(we_bc)), bc(tew[:, :, :]), ALU.mult))
                        ep.link(dve.tensor_tensor(ov, ov, tw, ALU.add))
                        dve.wait_ge(xr_in[r], (l * LOOPS + m + 1) * 16)
                        ep.inc(dve.tensor_tensor(q1, ov, over(wA), ALU.mult))
                        ep.link(dve.tensor_tensor(tw, xr[:, r, :, :], over(wB), ALU.mult))
                        ep.link(dve.tensor_tensor(q1, q1, tw, ALU.add))
                        dve.tensor_reduce(zc[:, :], q1, AX, ALU.add).then_inc(s["z_ready"], 1)
                        ep.inc(dve.tensor_tensor(tw, xr[:, r, :, :], ov, ALU.subtract))
                        dve.wait_ge(s["z_exp"], it + 1)
                        ep.link(dve.tensor_scalar(zc[:, :], ez[:, :], 1.0, None, ALU.add))
                        ep.link(dve.reciprocal(beta[:, :], zc[:, :]))
                        dve.wait_ge(h_st[r], ((l + 1) * LOOPS + m) * 16)
                        for n in range(2):
                            last = dve.scalar_tensor_tensor(hout[:, r, n, :], tw[:, n, :], beta[:, n:n + 1],
                                                            ov[:, n, :], ALU.mult, ALU.add)
                        last.then_inc(s["hout_ready"], 1)
                        dve.wait_ge(s["hout_ready"], it + 1 + EU)
            moe_dve(dve, layer_norm)


def kernel(**inputs):
    import concourse.bacc as bacc
    from concourse.bass_utils import run_bass_kernel_spmd

    g = {k: np.asarray(v) for k, v in inputs.items()}
    gnn = lambda name, layer: g[f"L0_gnn_{name}{min(layer, 1) + 1}"]
    pad = SUPER * SE - EDGES
    dst = np.concatenate([g["dst"], np.full(pad, FAR, np.int32)]).reshape(SUPER, SE)
    arrays = {
        "x": np.concatenate([g["x"], np.zeros((NPAD - NODES, D), np.float32)]),
        "dst": dst,
        "last": np.ascontiguousarray(dst[:SUPER - 1, SE - 1]).reshape(1, -1),
        "src": np.concatenate([g["src"], np.zeros(pad, np.int32)]).reshape(SUPER, SE),
        "ew": np.concatenate([g["edge_weight"], np.zeros(pad, np.float32)]).reshape(SUPER, SE),
        "wcat": np.concatenate([np.concatenate([gnn(n, l) for n in ("Wk", "Wv", "Wskip", "Wq")], axis=1)
                                for l in range(LAYERS)]),
        "bcat": np.stack([np.concatenate([gnn(n, l) for n in ("bk", "bv", "bskip", "bq")])
                          for l in range(LAYERS)]),
        "we": np.concatenate([gnn("We", l) for l in range(LAYERS)]),
        "wbeta": np.concatenate([gnn("Wbeta", l).reshape(3, D) for l in range(LAYERS)]),
        "gate_w": g["L0_ffn_gate_w"],
        "gate_b": g["L0_ffn_gate_b"].reshape(1, EXPERTS),
        "w1": g["L0_ffn_w1"].reshape(EXPERTS * D, FF),
        "b1": np.ascontiguousarray(g["L0_ffn_b1"].reshape(EXPERTS, FF // P, P).transpose(0, 2, 1)
                                   ).reshape(EXPERTS * P, FF // P),
        "w2": g["L0_ffn_w2"].reshape(EXPERTS * FF, D),
        "b2": g["L0_ffn_b2"],
    }
    arrays = {f"in_{k}": np.ascontiguousarray(v) for k, v in arrays.items()}
    nc = bacc.Bacc("TRN2", target_bir_lowering=False, num_devices=1)
    a = {k[3:]: nc.dram_tensor(k, v.shape, mybir.dt.from_np(v.dtype), kind="ExternalInput").ap()
         for k, v in arrays.items()}
    out = nc.dram_tensor("out", (NPAD, D), F32, kind="ExternalOutput").ap()
    build(nc, a, out)
    r = run_bass_kernel_spmd(nc, [arrays], core_ids=[0])
    return r.results[0]["out"][:NODES]
```

```python
from contextlib import ExitStack

import numpy as np

import concourse.bass as bass
from concourse import mybir

F32 = mybir.dt.float32
I32 = mybir.dt.int32
ALU = mybir.AluOpType
ACT = mybir.ActivationFunctionType
AX = mybir.AxisListType.X
ds = bass.ds

P = 128
NODES, EDGES, D, HEADS = 6250, 100000, 256, 8
HD = D // HEADS
LAYERS = 3
J = 4
SE = P * J
SUPER = -(-EDGES // SE)
NBLK = 50
REAL_BLK = -(-NODES // P)
NPAD = NBLK * P
U = 5
STEPS = -(-(SUPER + REAL_BLK - 1) // U) * U
NB = STEPS // U
RS = 2 * U
LAG = 7
KH = -(-STEPS // 2)
SLOTS = 2 * KH
PB = U * HEADS
AW = HD + 2
QW = D + HEADS
QX = 2 * D + HEADS
BIG = 1e30
HUGE = 1e38
SCALE = float(HD) ** -0.5
FAR = 1 << 20

START = 1
EXPERTS, FF = 8, 1024
CAP = max(1, -(-5 * NODES // (4 * EXPERTS)))
CAPP = 1024
CT = CAPP // P
HALF = 489
assert NB % 2 == 1 and NBLK % 10 == 0 and 2 * HALF >= CAP


class Chain:

    def __init__(self, eng, sem, per=None, start=0):
        self.eng, self.sem, self.per, self.start, self.base, self.n = eng, sem, per, start, start, 0

    def at(self, iteration, done=0):
        self.base, self.n = iteration * self.per + self.start, done

    def inc(self, ins):
        self.n += 1
        ins.then_inc(self.sem, 1)

    def wait(self):
        self.eng.wait_ge(self.sem, self.base + self.n)

    def link(self, ins):
        self.inc(ins)
        self.wait()


KB = 13
KACT = 4
SEMAPHORES = ""


def build(nc, a, out):
    dram = lambda name, shape, dt=F32: nc.dram_tensor(name, shape, dt, kind="Internal").ap()
    h_dram = dram("h_dram", (NPAD, D))
    kv_dram = dram("kv_dram", (NPAD, 2 * D))
    qx_dram = dram("qx_dram", (NPAD, QX))
    res_dram = dram("res_dram", (SLOTS * HEADS, SE + 1))
    meta_dram = dram("meta_dram", (4, SLOTS))
    x2_dram = dram("x2_dram", (NPAD, D))
    xn_dram = dram("xn_dram", (NPAD, D))
    slots_dram = dram("slots_dram", (EXPERTS * CAPP, D))
    y_dram = dram("y_dram", (EXPERTS * 2 * HALF, D))

    with ExitStack() as ctx:
        def sb(name, shape, dt=F32):
            return ctx.enter_context(nc.sbuf_tensor("s_" + name, shape, dt))

        def pb(name, shape):
            return ctx.enter_context(nc.psum_tensor(name, shape, F32))

        def sem(name):
            return ctx.enter_context(nc.semaphore(name))

        psQ = pb("psQ", [P, 4, 512])
        psG = pb("psG", [P, 512])
        psA = pb("psA", [P, 512])
        psT = pb("psT", [P, 512])
        psB = pb("psB", [P, 512])

        part_i = sb("part_i", [P, 4], I32)
        sel_i = sb("sel_i", [P, HEADS + U + U * HEADS], I32)
        iota_r = sb("iota_r", [P, P])
        iota_c = sb("iota_c", [P, 1])
        ident = sb("ident", [P, P])
        tri = sb("tri", [P, P])
        ones = sb("ones", [P, P])
        selA = sb("selA", [PB, HEADS])
        selB = sb("selB", [PB, U])
        selD = sb("selD", [HEADS, U, HEADS])
        e8 = sb("e8", [P, EXPERTS])
        srcI = sb("srcI", [P, SLOTS, J], I32)
        ndl = sb("ndl", [P, SLOTS, J])
        ewT = sb("ewT", [P, SLOTS, J])
        dn8 = sb("dn8", [HEADS, SLOTS])
        dd8 = sb("dd8", [HEADS, SLOTS])
        blkI = sb("blkI", [1, SLOTS], I32)
        crossc = sb("crossc", [PB, NB])
        accT = sb("acc", [P, NBLK * HEADS * AW])
        acc = accT[:, :].rearrange("p (b h w) -> p b h w", b=NBLK, h=HEADS)
        accF = accT[:, :].rearrange("p (b w) -> p b w", b=NBLK)
        RING = 2 * U * J * 2 * D
        ringT = sb("ring", [P, RING])
        kv = ringT[:, :].rearrange("p (r s j w) -> p r s j w", r=2, s=U, j=J)
        G = sb("G", [P, 2, U, J, P])
        OH = sb("OH", [P, 2, J, P])
        qring = sb("qring", [P, U, QW])
        prod = sb("prod", [P, J, HEADS, HD + 1])
        alpha = sb("alpha", [P, 2, J, U, HEADS])
        res = sb("res", [PB, SE + 1])
        F1 = sb("F1", [PB, SE])
        F2 = sb("F2", [PB, SE])
        M = sb("M", [PB, SE])
        Dm, pT = F1, F2
        LB = sb("LB", [PB, U])
        Us = sb("Us", [HEADS, U + 1])
        cc = sb("cc", [HEADS, U])
        lhs2 = sb("lhs2", [HEADS, U, HEADS])
        ccol = sb("ccol", [PB, 1])
        gd = sb("gd", [PB, 1])
        gx = sb("gx", [PB, 1])
        gm = sb("gm", [PB, PB])
        crossOH = sb("crossOH", [PB, P])
        pB = sb("pB", [P, 2, J, U, HEADS])
        fB = sb("fB", [P, 2, U, HEADS])
        W = sb("W", [P, 2, J, HEADS, AW])
        idxb = sb("idxb", [P, 2, U, J], I32)
        we_bc = sb("we_bc", [P, D])
        wA = sb("wA", [P, D])
        wB = sb("wB", [P, D])
        den = sb("den", [P, 2, HEADS])
        rden = sb("rden", [P, 2, HEADS])
        tew = sb("tew", [P, 2, HEADS])
        zc = sb("zc", [P, 2])
        ez = sb("ez", [P, 2])
        beta = sb("beta", [P, 2])
        stats = sb("stats", [P, 2, 6])
        mv = sb("mv", [P, 2, 2])
        ve = sb("ve", [P, 2])
        sd = sb("sd", [P, 2])
        rstd = sb("rstd", [P, 2])
        tI = sb("tI", [P, 2], I32)
        small3 = sb("small3", [P, 2, 3])

        def view(at, *shape, of=ringT, room=RING, dt=None):
            n = int(np.prod(shape))
            assert at + n <= room, (at, n)
            names = " ".join(f"d{i}" for i in range(len(shape)))
            flat = of[:, at:at + n]
            if dt is not None:
                flat = flat.bitcast(dt)
            if len(shape) == 1:
                return flat, at + n
            return flat.rearrange(f"p ({names}) -> p {names}",
                                  **{f"d{i}": x for i, x in enumerate(shape)}), at + n

        o = 0
        rawI, o = view(o, 2, SE, dt=I32)
        srcR, o = view(o, 2, SE, dt=I32)
        dstF, o = view(o, 2, SE)
        srcF, o = view(o, 2, SE)
        ewF, o = view(o, 2, SE)
        dloc, o = view(o, 2, SE)
        res2, o = view(o, 2, SE + 1)
        posA, o = view(o, SUPER - 1)
        cmpT, o = view(o, SUPER - 1)
        kcol, o = view(o, 2)
        iota_i, o = view(o, SUPER, dt=I32)
        lastI, o = view(o, SUPER - 1, dt=I32)
        tcol, o = view(o, 2)
        nbc, o = view(o, 2)
        o += o % 2
        row = [None] * 10
        for i in range(10):
            row[i], _ = view(i * SLOTS, SLOTS, of=accT, room=NBLK * HEADS * AW)
        EU = 5
        ACCN = NBLK * HEADS * AW
        o = 10 * SLOTS
        lx, o = view(o, EU, 2, D, of=accT, room=ACCN)
        ly, o = view(o, EU, 2, D, of=accT, room=ACCN)
        lh, o = view(o, EU, 2, D, of=accT, room=ACCN)
        o = 0
        wcat, o = view(o, 2, 4 * D)
        bias_bc, o = view(o, 4 * D)
        wb_bc, o = view(o, 3, D)
        hb, o = view(o, 2, D)
        hT, o = view(o, 2, 2, P)
        kvb, o = view(o, 2, 2 * D)
        qxb, o = view(o, 2, QX)
        qprod, o = view(o, D)
        o = 0
        xr, o = view(o, EU, 2, D)
        hout, o = view(o, EU, 2, D)
        ov, o = view(o, 2, D)
        tw, o = view(o, 2, D)
        q1, o = view(o, 2, D)

        class Sems(dict):
            def __missing__(self, name):
                self[name] = sem(name)
                return self[name]

        s = Sems()
        for name in SEMAPHORES.split():
            s[name]
        kv_in = [[sem(f"kv_in_{r}_{i}") for i in range(U)] for r in range(2)]
        q_in = [sem(f"q_in_{i}") for i in range(U)]
        x_in = [sem(f"x_in_{i}") for i in range(EU)]
        xr_in = [sem(f"xr_in_{i}") for i in range(EU)]
        h_st = [sem(f"h_stored_{i}") for i in range(EU)]
        hb_in = [sem(f"hb_in_{i}") for i in range(2)]
        pst = [sem(f"proj_stored_{i}") for i in range(2)]
        PAIRS = NBLK // 2
        LOOPS = PAIRS // EU

        class Batch:

            def __init__(self, l, m, c):
                self.B, self.r = m * 2 + c, c % 2
                self.g = l * NB + self.B
                self.use = l * ((NB + 1 - self.r) // 2) + (m + c // 2)

        class Step:

            def __init__(self, batch, i):
                self.batch, self.i, self.r, self.use = batch, i, batch.r, batch.use
                self.k, self.n = batch.B * U + i, batch.g * U + i
                self.half = (batch.r * U + i) % 2

        def edge_loop(eng, l, body):
            def run(m, c, inside=False):
                def batch(d):
                    return Batch(l, m, c + d) if inside or 0 <= c + d < NB else None

                def step(d):
                    b = batch(d // U)
                    return None if b is None else Step(b, d % U)

                body(step, batch)

            loops = (NB - 3) // 2
            for c in range(-1, 2):
                run(0, c)
            with eng.Fori(0, loops) as m:
                for c in range(2, 4):
                    run(m, c, True)
            for c in range(2 + 2 * loops, NB + 2):
                run(0, c)

        def rounds(eng, n, body):
            body(0, True)
            with eng.Fori(1, n) as m:
                body(m, False)

        def block_of(eng, x):
            return x and eng.value_load(blkI[0:1, ds(x.k, 1)], min_val=0, max_val=NBLK - 1)

        ZERO_DMAS = 4
        ZW = EXPERTS * CAPP * D // (P * ZERO_DMAS)
        zeros = G[:, :, :, :, :].rearrange('p r i j n -> p (r i j n)')[:, 0:ZW]
        split = lambda x: x.rearrange("p n (h d) -> p n h d", h=HEADS)
        flat3 = lambda x: x.rearrange("p b e -> p (b e)")

        def held(eng):
            eng.sem_inc(s["held"], 1)

        NGATE = NBLK * EXPERTS
        o = 0
        hm, o = view(o, FF // P, 2 * HALF, of=accT, room=ACCN)
        lg, o = view(o, NBLK, EXPERTS, of=accT, room=ACCN)
        ex, o = view(o, NBLK, EXPERTS, of=accT, room=ACCN)
        eq, o = view(o, NBLK, EXPERTS, of=accT, room=ACCN)
        oh, o = view(o, NBLK, EXPERTS, of=accT, room=ACCN)
        cum, o = view(o, NBLK, EXPERTS, of=accT, room=ACCN)
        tot, o = view(o, NBLK, EXPERTS, of=accT, room=ACCN)
        run, o = view(o, NBLK, EXPERTS, of=accT, room=ACCN)
        mx, o = view(o, NBLK, of=accT, room=ACCN)
        se, o = view(o, NBLK, of=accT, room=ACCN)
        ms, o = view(o, NBLK, of=accT, room=ACCN)
        pos, o = view(o, NBLK, of=accT, room=ACCN)
        base, o = view(o, NBLK, of=accT, room=ACCN)
        kept, o = view(o, NBLK, of=accT, room=ACCN)
        wgt, o = view(o, NBLK, of=accT, room=ACCN)
        slf, o = view(o, NBLK, of=accT, room=ACCN)
        slotw, o = view(o, NBLK, of=accT, room=ACCN, dt=I32)
        slotr, o = view(o, NBLK, of=accT, room=ACCN, dt=I32)
        gb_bc, o = view(o, EXPERTS, of=accT, room=ACCN)
        gw, o = view(o, 2, EXPERTS, of=accT, room=ACCN)
        b1c, o = view(o, 2, FF // P, of=accT, room=ACCN)
        b2b, o = view(o, 2, D, of=accT, room=ACCN)
        o = 0
        w1, o = view(o, 2, 2, FF)
        w2, o = view(o, 2, FF // P, D)
        xs, o = view(o, 2, CT, D)
        xsT, o1 = view(o, 2, CAPP)
        xsc, _ = view(o, EU, D)
        yb, _ = view(o1, CT, D)
        hbg, o = view(o1, 2, D)
        hTg, o = view(o, 2, 2, P)
        o = 0
        yg, o = view(o, EU, D)
        x2b, o = view(o, EU, D)
        fo, o = view(o, EU, D)
        fin, o = view(o, D)
        nn, o = view(o, D)
        ty, o = view(o, D)
        cl, o = view(o, D)
        idx5 = sb("idx5", [P, 2 * EU], I32)
        w_ex = [sem(f"w_ex_{i}") for i in range(2)]
        xs_in = [sem(f"xs_in_{i}") for i in range(2)]
        sc_in = [sem(f"sc_in_{i}") for i in range(EU)]
        sc_done = [sem(f"sc_done_{i}") for i in range(EU)]
        yg_in = [sem(f"yg_in_{i}") for i in range(EU)]
        x2_in = [sem(f"x2_in_{i}") for i in range(EU)]
        o_st = [sem(f"o_stored_{i}") for i in range(EU)]
        H_ALL = (LAYERS + 1) * LOOPS * 16
        G_ALL = LAYERS * NBLK
        SROUNDS = NBLK // EU

        def moe_sync(sp):
            for i in range(EU):
                sp.wait_ge(h_st[i], H_ALL)
            with sp.Fori(0, LOOPS) as m:
                for r in range(EU):
                    sp.wait_ge(h_st[r], m * 32 + H_ALL)
                    for src, dst in ((a["x"], lx), (h_dram, lh)):
                        sp.dma_start(dst[:, r, :, :], src[ds((m * EU + r) * 2 * P, 2 * P), :]
                                     .rearrange("(n p) d -> p n d", n=2)).then_inc(x_in[r], 16)
            for i in range(EU):
                sp.wait_ge(h_st[i], H_ALL + 32 * LOOPS)
            for c in range(2):
                sp.dma_start(gw[:, c, :], a["gate_w"][c * P:(c + 1) * P, :]).then_inc(s["gate_in"], 16)
            sp.dma_start(gb_bc, a["gate_b"].to_broadcast([P, EXPERTS])).then_inc(s["gate_in"], 16)
            with sp.Fori(0, PAIRS) as m:
                for r in range(2):
                    sp.wait_ge(s["tr_done"], m * 2 + (G_ALL + r + 1))
                    sp.dma_start(hbg[:, r, :], xn_dram[ds((m * 2 + r) * P, P), :]).then_inc(hb_in[r], 16)
            def load_rows(m, first):
                for r in range(EU):
                    if not first:
                        sp.wait_ge(sc_done[r], m * 16)
                    sp.dma_start(xsc[:, r, :], xn_dram[ds((m * EU + r) * P, P), :]).then_inc(sc_in[r], 16)

            rounds(sp, SROUNDS, load_rows)
            for r in range(EU):
                sp.wait_ge(sc_done[r], SROUNDS * 16)
            with sp.Fori(0, EXPERTS // 2) as m:
                for r in range(2):
                    sp.wait_ge(s["y_mm"], m * (2 * CT) + (r * CT + CT))
                    for c in range(2):
                        sp.dma_start(w1[:, r, c, :], a["w1"][ds(m * (2 * D) + (r * D + c * P), P), :]
                                     ).then_inc(w_ex[r], 16)
                    sp.dma_start(w2[:, r, :, :], a["w2"][ds(m * (2 * FF) + r * FF, FF), :]
                                 .rearrange("(f p) d -> p f d", p=P)).then_inc(w_ex[r], 16)
                    sp.dma_start(b1c[:, r, :], a["b1"][ds(m * (2 * P) + r * P, P), :]).then_inc(w_ex[r], 16)
                    sp.wait_ge(s["y_ev"], m * (2 * CT) + (r * CT - CT + 2 + CT))
                    sp.dma_start(b2b[:, r, :], a["b2"][ds(m * 2 + r, 1), :].to_broadcast([P, D])
                                 ).then_inc(w_ex[r], 16)
                    sp.dma_start(xs[:, r, :, :], slots_dram[ds(m * (2 * CAPP) + r * CAPP, CAPP), :]
                                 .rearrange("(t p) d -> p t d", p=P)).then_inc(xs_in[r], 16)
            sp.wait_ge(s["y_st"], EXPERTS * 32)
            with sp.Fori(0, SROUNDS) as m:
                for r in range(EU):
                    sp.wait_ge(s["fo_done"], m * EU + r + 1)
                    sp.dma_start(x2b[:, r, :], x2_dram[ds((m * EU + r) * P, P), :]).then_inc(x2_in[r], 16)

        def moe_pool(pool):
            with pool.Fori(0, LOOPS) as m:
                for r in range(EU):
                    pool.wait_ge(s["ln_done"], m * EU + (PAIRS + r + 1 + EU))
                    for dst, src in ((xn_dram, ly), (x2_dram, lh)):
                        pool.dma_start(dst[ds((m * EU + r) * 2 * P, 2 * P), :].rearrange("(n p) d -> p n d", n=2),
                                       src[:, r, :, :]).then_inc(h_st[r], 16)
            pool.wait_ge(s["slots_ready"], 1)
            def scatter(m, first):
                for r in range(EU):
                    if not first:
                        pool.wait_ge(sc_done[r], m * 16)
                        held(pool)
                    pool.tensor_copy(idx5[:, r:r + 1], slotw[:, ds(m * EU + r, 1)]).then_inc(s["sidx"], 1)
                    pool.wait_ge(s["sidx"], m * EU + r + 1)
                    pool.wait_ge(sc_in[r], m * 16 + 16)
                    held(pool)
                    pool.indirect_dma_start(slots_dram, bass.IndirectOffsetOnAxis(ap=idx5[:, r:r + 1], axis=0),
                                            xsc[:, r, :], None, bounds_check=EXPERTS * CAPP - 1,
                                            oob_is_err=False).then_inc(sc_done[r], 16)

            rounds(pool, SROUNDS, scatter)
            with pool.Fori(0, EXPERTS // 2) as m:
                for r in range(2):
                    pool.wait_ge(s["y_ev"], m * (2 * CT) + (r * CT + CT + 2))
                    full = 2 * HALF // P
                    rest = 2 * HALF - full * P
                    pool.dma_start(y_dram[ds(m * (4 * HALF) + r * 2 * HALF, full * P), :]
                                   .rearrange("(t p) d -> p t d", p=P), yb[:, 0:full, :]).then_inc(s["y_st"], 16)
                    pool.dma_start(y_dram[ds(m * (4 * HALF) + (r * 2 * HALF + full * P), rest), :],
                                   yb[0:rest, full, :]).then_inc(s["y_st"], 16)
            pool.wait_ge(s["y_st"], EXPERTS * 32)
            with pool.Fori(0, SROUNDS) as m:
                for r in range(EU):
                    pool.wait_ge(s["fo_done"], m * EU + r + 1)
                    held(pool)
                    pool.tensor_copy(idx5[:, EU + r:EU + r + 1], slotr[:, ds(m * EU + r, 1)]).then_inc(s["gidx"], 1)
                    pool.wait_ge(s["gidx"], m * EU + r + 1)
                    held(pool)
                    pool.indirect_dma_start(yg[:, r, :], None, y_dram,
                                            bass.IndirectOffsetOnAxis(ap=idx5[:, EU + r:EU + r + 1], axis=0)
                                            ).then_inc(yg_in[r], 16)

        def moe_act(act):
            with act.Fori(0, LOOPS) as m:
                for r in range(EU):
                    act.wait_ge(s["ln_var"], m * EU + (PAIRS + r + 1))
                    act.activation(sd[:, :], ve[:, :], ACT.Sqrt).then_inc(s["ln_sd"], 1)
            with act.Fori(0, PAIRS) as m:
                for r in range(2):
                    act.wait_ge(s["tr_done"], m * 2 + (G_ALL + r + 1 + 2))
                    act.wait_ge(s["mm_done"], m * 2 + (G_ALL + r + 1))
                    act.activation(hTg[:, r, :, :].rearrange("p c t -> p (c t)"), psG[:, 0:D], ACT.Copy
                                   ).then_inc(s["hT_done"], 1)
            act.wait_ge(s["lm_ready"], 1)
            act.activation(flat3(ex), flat3(eq), ACT.Exp).then_inc(s["ex_ready"], 1)
            with act.Fori(0, EXPERTS // 2) as m:
                for r in range(2):
                    e16 = m * 32 + r * 16
                    for b in range(4):
                        act.wait_ge(s["xt_ps"], m * 8 + (r * 4 + b + 1))
                        act.activation(xsT[:, :, b * 2 * P:(b + 1) * 2 * P].rearrange("p c (t e) -> p t c e", t=2),
                                       psQ[:, b, :].rearrange("p (t c e) -> p t c e", t=2, c=2), ACT.Copy
                                       ).then_inc(s["xt_cp"], 1)
                    act.wait_ge(w_ex[r], m * (5 * 16) + 5 * 16)
                    act.wait_ge(s["y_mm"], m * (2 * CT) + (r * CT + 2 * CT))
                    for q in range(2 * (FF // P)):
                        f, half = q // 2, q % 2
                        act.wait_ge(s["h_mm"], e16 + (q + 1))
                        act.activation(hm[:, f, half * HALF:(half + 1) * HALF], psQ[:, q % 4, 0:HALF], ACT.Relu,
                                       bias=b1c[:, r, f:f + 1]).then_inc(s["h_cp"], 1)
            with act.Fori(0, SROUNDS) as m:
                for r in range(EU):
                    act.wait_ge(s["fo_done"], m * EU + (r + 1 + EU))
                    act.dma_start(out[ds((m * EU + r) * P, P), :], fo[:, r, :]).then_inc(o_st[r], 16)
            for r in range(EU):
                act.wait_ge(o_st[r], SROUNDS * 16)

        def moe_pe(pe):
            pe.wait_ge(s["gate_in"], 3 * 16)
            with pe.Fori(0, PAIRS) as m:
                for r in range(2):
                    pe.wait_ge(hb_in[r], m * 16 + (LAYERS * PAIRS + 1) * 16)
                    pe.wait_ge(s["hT_done"], m * 2 + (G_ALL + r) + START)
                    for c in range(2):
                        last = pe.transpose(psG[:, c * P:(c + 1) * P], hbg[:, r, c * P:(c + 1) * P], ident[:, :])
                    last.then_inc(s["tr_done"], 1)
                    pe.wait_ge(s["hT_done"], m * 2 + (G_ALL + r + 1) + START)
                    pe.wait_ge(s["ev_done"], m * 2 + (G_ALL + r + 1))
                    for c in range(2):
                        last = pe.matmul(psQ[:, r, 0:EXPERTS], hTg[:, r, c, :], gw[:, c, :],
                                         start=(c == 0), stop=(c == 1))
                    last.then_inc(s["mm_done"], 1)
            pe.wait_ge(s["oh_ready"], 1)
            pe.matmul(psT[:, 0:NGATE], tri[:, :], flat3(oh), start=True, stop=True)
            pe.matmul(psB[:, 0:NGATE], ones[:, :], flat3(oh), start=True, stop=True).then_inc(s["cnt_mm"], 1)
            with pe.Fori(0, EXPERTS // 2) as m:
                for r in range(2):
                    e16 = m * 32 + r * 16
                    pe.wait_ge(xs_in[r], m * 16 + 16)
                    pe.wait_ge(s["h_cp"], e16 + START)
                    for b in range(4):
                        for t in range(2):
                            for c in range(2):
                                last = pe.transpose(psQ[:, b, (2 * t + c) * P:(2 * t + c + 1) * P],
                                                    xs[:, r, 2 * b + t, c * P:(c + 1) * P], ident[:, :])
                        last.then_inc(s["xt_ps"], 1)
                    pe.wait_ge(s["xt_cp"], m * 8 + (r * 4 + 4))
                    pe.wait_ge(w_ex[r], m * (5 * 16) + 5 * 16)
                    for q in range(2 * (FF // P)):
                        f, half = q // 2, q % 2
                        if q >= 4:
                            pe.wait_ge(s["h_cp"], e16 + (q - 3) + START)
                        for c in range(2):
                            last = pe.matmul(psQ[:, q % 4, 0:HALF], w1[:, r, c, f * P:(f + 1) * P],
                                             xsT[:, c, half * HALF:(half + 1) * HALF],
                                             start=(c == 0), stop=(c == 1))
                        last.then_inc(s["h_mm"], 1)
                    pe.wait_ge(s["h_cp"], e16 + 16 + START)
                    for t in range(CT):
                        n = min(P, 2 * HALF - t * P)
                        bank = (psA, psT)[t % 2]
                        pe.wait_ge(s["y_ev"], m * (2 * CT) + (r * CT + t + 1))
                        for f in range(FF // P):
                            last = pe.matmul(bank[0:n, 0:D], hm[:, f, t * P:t * P + n], w2[:, r, f, :],
                                             start=(f == 0), stop=(f == FF // P - 1))
                        last.then_inc(s["y_mm"], 1)

        def moe_dve(dve, layer_norm):
            mc = Chain(dve, s["moe_add"], 1)
            with dve.Fori(0, LOOPS) as m:
                for r in range(EU):
                    mc.at(m * EU + r)
                    dve.wait_ge(x_in[r], m * 32 + (LOOPS + 2) * 16)
                    mc.link(dve.tensor_tensor(lh[:, r, :, :], lh[:, r, :, :], lx[:, r, :, :], ALU.add))
                    layer_norm(lh[:, r, :, :], ly[:, r, :, :], m * EU + r + PAIRS, h_st[r], m * 32 + (H_ALL))
            dve.wait_ge(s["gate_in"], 3 * 16)
            with dve.Fori(0, PAIRS) as m:
                for r in range(2):
                    dve.wait_ge(s["mm_done"], m * 2 + (G_ALL + r + 1 + 2))
                    dve.tensor_tensor(lg[:, ds(m * 2 + r, 1), :].rearrange("p b e -> p (b e)"),
                                      psQ[:, r, 0:EXPERTS], gb_bc, ALU.add).then_inc(s["ev_done"], 1)
            dve.wait_ge(s["ev_done"], G_ALL + NBLK + 2)
            c = Chain(dve, s["route"])
            per_token = lambda v: v.unsqueeze(2).to_broadcast([P, NBLK, EXPERTS])
            e8_bc = e8[:, :].unsqueeze(1).to_broadcast([P, NBLK, EXPERTS])
            c.link(dve.tensor_reduce(mx, lg, AX, ALU.max))
            c.link(dve.tensor_tensor(eq, lg, per_token(mx), ALU.subtract))
            dve.sem_inc(s["lm_ready"], 1)
            c.link(dve.tensor_scalar(oh, eq, 0.0, None, ALU.is_equal))
            c.link(dve.tensor_tensor(oh, oh, e8_bc, ALU.mult))
            c.link(dve.tensor_reduce(ms, oh, AX, ALU.max))
            c.link(dve.tensor_tensor(oh, e8_bc, per_token(ms), ALU.is_equal))
            dve.sem_inc(s["oh_ready"], 1)
            dve.wait_ge(s["ex_ready"], 1)
            c.link(dve.tensor_reduce(se, ex, AX, ALU.add))
            c.link(dve.reciprocal(wgt, se))
            dve.wait_ge(s["cnt_mm"], 1)
            for e in range(EXPERTS):
                last = dve.tensor_tensor_scan(run[:, :, e], ones[:, 0:NBLK], psB[:, e:NGATE:EXPERTS], 0.0,
                                              ALU.mult, ALU.add)
            c.link(last)
            c.link(dve.tensor_tensor(flat3(run), flat3(run), psB[:, 0:NGATE], ALU.subtract))
            c.link(dve.tensor_tensor(flat3(run), flat3(run), psT[:, 0:NGATE], ALU.add))
            c.link(dve.tensor_tensor(run, run, oh, ALU.mult))
            c.link(dve.tensor_reduce(pos, run, AX, ALU.add))
            c.link(dve.tensor_scalar(kept, pos, float(CAP), None, ALU.is_le))
            c.link(dve.tensor_tensor(wgt, wgt, kept, ALU.mult))
            c.link(dve.tensor_scalar(base, ms, -float(CAPP), float(EXPERTS * CAPP - 1), ALU.mult, ALU.add))
            c.link(dve.tensor_scalar(kept, kept, -float(1 << 20), float(1 << 20), ALU.mult, ALU.add))
            c.link(dve.tensor_tensor(slf, base, pos, ALU.add))
            c.link(dve.tensor_tensor(slf, slf, kept, ALU.add))
            c.link(dve.tensor_copy(slotw, slf))
            c.link(dve.tensor_scalar(pos, pos, float(CAP), None, ALU.min))
            c.link(dve.tensor_scalar(base, ms, -float(2 * HALF), float(EXPERTS * 2 * HALF - 1), ALU.mult, ALU.add))
            c.link(dve.tensor_tensor(slf, base, pos, ALU.add))
            c.link(dve.tensor_copy(slotr, slf))
            dve.sem_inc(s["slots_ready"], 1)
            def add_bias(m, first):
                for r in range(2):
                    dve.wait_ge(w_ex[r], m * (5 * 16) + 5 * 16)
                    if r or not first:
                        dve.wait_ge(s["y_st"], m * 64 + r * 32)
                    for t in range(CT):
                        n = min(P, 2 * HALF - t * P)
                        bank = (psA, psT)[t % 2]
                        dve.wait_ge(s["y_mm"], m * (2 * CT) + (r * CT + t + 1 + 2 * CT))
                        dve.tensor_tensor(yb[0:n, t, :], bank[0:n, 0:D], b2b[0:n, r, :], ALU.add
                                          ).then_inc(s["y_ev"], 1)

            rounds(dve, EXPERTS // 2, add_bias)
            fc = Chain(dve, s["final"], 6)
            def combine(m, first):
                for r in range(EU):
                    fc.at(m * EU + r)
                    dve.wait_ge(yg_in[r], m * 16 + 16)
                    fc.link(dve.tensor_scalar(ty, yg[:, r, :], wgt[:, ds(m * EU + r, 1)], None, ALU.mult))
                    fc.inc(dve.tensor_scalar(fin, ty, 0.0, 0.0, ALU.mult, ALU.is_equal))
                    fc.inc(dve.tensor_scalar(cl, ty, HUGE, 10000.0, ALU.is_ge, ALU.mult))
                    fc.link(dve.tensor_scalar(nn, ty, -HUGE, -10000.0, ALU.is_le, ALU.mult))
                    fc.link(dve.tensor_tensor(cl, cl, nn, ALU.add))
                    held(dve)
                    fc.link(dve.copy_predicated(cl, fin.bitcast(I32), ty))
                    dve.wait_ge(x2_in[r], m * 16 + 16)
                    if not first:
                        dve.wait_ge(o_st[r], m * 16)
                    dve.tensor_tensor(fo[:, r, :], cl, x2b[:, r, :], ALU.add).then_inc(s["fo_done"], 1)
                    dve.wait_ge(s["fo_done"], m * EU + (r + 1 + EU))

            rounds(dve, SROUNDS, combine)

        block = ctx.enter_context(nc.Block())

        @block.sync
        def _(sp):
            sp.dma_start(lastI[0:KH, :], a["last"].to_broadcast([KH, SUPER - 1])).then_inc(s["last_in"], 16)
            sp.wait_ge(s["steps_ready"], 1)
            for g in range(2):
                for h in range(HEADS):
                    sp.dma_start(res_dram[g * KH * HEADS + h:(g + 1) * KH * HEADS:HEADS, :],
                                 res2[0:KH, g, :]).then_inc(s["setup_st"], 16)
                for i in range(3):
                    sp.dma_start(meta_dram[i:i + 1, g * KH:(g + 1) * KH].rearrange("a k -> k a"),
                                 small3[0:KH, g, i:i + 1], allow_slow_non_contiguous=True).then_inc(s["setup_st"], 16)
            sp.wait_ge(s["setup_st"], 2 * (HEADS + 3) * 16)
            for i in range(3):
                sp.dma_start(row[i][0:HEADS, :], meta_dram[i:i + 1, :].to_broadcast([HEADS, SLOTS])
                             ).then_inc(s["rows_in"], 16)
            sp.wait_ge(s["rows_ready"], 1)
            sp.dma_start(meta_dram[3:4, :], row[9][0:1, :]).then_inc(s["setup_st"], 16)
            sp.wait_ge(s["setup_st"], 2 * (HEADS + 3) * 16 + 16)
            for i in range(U):
                sp.dma_start(crossc[i * HEADS:(i + 1) * HEADS, :],
                             meta_dram[3:4, i:STEPS:U].to_broadcast([HEADS, NB]),
                             allow_slow_non_contiguous=True).then_inc(s["cross_in"], 16)
            with sp.Fori(0, LOOPS) as m:
                for r in range(EU):
                    sp.wait_ge(s["ln_done"], m * EU + r + 1)
                    sp.dma_start(lx[:, r, :, :], a["x"][ds((m * EU + r) * 2 * P, 2 * P), :]
                                 .rearrange("(n p) d -> p n d", n=2)).then_inc(x_in[r], 16)
            with sp.Fori(0, LAYERS) as l:
                for i in range(EU):
                    sp.wait_ge(h_st[i], (l + 1) * (16 * LOOPS))
                for c in range(2):
                    sp.dma_start(wcat[:, c, :], a["wcat"][ds(l * D + c * P, P), :]).then_inc(s["w_in"], 16)
                sp.dma_start(bias_bc[:, :], a["bcat"][ds(l, 1), :].to_broadcast([P, 4 * D])).then_inc(s["w_in"], 16)
                sp.dma_start(we_bc[:, :], a["we"][ds(l, 1), :].to_broadcast([P, D])).then_inc(s["w_in"], 16)
                for i in range(3):
                    sp.dma_start(wb_bc[:, i, :], a["wbeta"][ds(l * 3 + i, 1), :].to_broadcast([P, D])
                                 ).then_inc(s["w_in"], 16)
                with sp.Fori(0, PAIRS) as m:
                    for r in range(2):
                        sp.wait_ge(s["tr_done"], l * NBLK + m * 2 + r + 1)
                        sp.dma_start(hb[:, r, :], h_dram[ds((m * 2 + r) * P, P), :]).then_inc(hb_in[r], 16)
                for r in range(2):
                    sp.wait_ge(pst[r], (l + 1) * (PAIRS * 32))
                held(sp)

                def body(step, batch):
                    an = batch(0)
                    if an is None:
                        return
                    steps = [step(i) for i in range(U)]
                    blocks = [sp.value_load(blkI[0:1, ds(x.k, 1)], min_val=0, max_val=NBLK - 1) for x in steps]
                    for x, b in zip(steps, blocks):
                        sp.wait_ge(s["q_ready"], (x.n + 1) * 2)
                        sp.dma_start(qring[:, x.i, :], qx_dram[ds(b * P, P), D:QX]).then_inc(q_in[x.i], 16)
                    sp.wait_ge(s["scanned"], an.g + START)
                    sp.dma_start(res[:, :], res_dram[ds(steps[0].k * HEADS, PB), :]).then_inc(s["res_in"], 16)

                edge_loop(sp, l, body)
                sp.wait_ge(s["acc_done"], (l + 1) * STEPS + START)
                held(sp)
                with sp.Fori(0, LOOPS) as m:
                    for r in range(EU):
                        sp.wait_ge(s["hout_ready"], l * PAIRS + m * EU + r + 1)
                        sp.dma_start(xr[:, r, :, :], qx_dram[ds((m * EU + r) * 2 * P, 2 * P), 0:D]
                                     .rearrange("(n p) d -> p n d", n=2)).then_inc(xr_in[r], 16)
            moe_sync(sp)

        @block.gpsimd
        def _(pool):
            for name, n in (("q_ready", 2 * U), ("agg_done", RS), ("v_used", RS), ("k_used", 2), ("et_done", 2),
                            ("w_dve", RS), ("w_act", RS), ("scaled", RS), ("tr_done", 2),
                            ("mm_done", 2), ("ev_done", 2), ("hout_ready", EU), ("ln_done", EU), ("y_mm", 2 * CT),
                            ("y_ev", 2), ("fo_done", EU)):
                pool.sem_inc(s[name], n)
            for name in ("scanned", "hT_done", "pb_done", "alpha_ready", "acc_done", "oh_done", "chain_B", "act_B",
                         "h_cp"):
                pool.sem_inc(s[name], START)
            pool.iota(iota_i[:, :], [[1, SUPER]], base=0, channel_multiplier=0).then_inc(s["iotas"], 1)
            pool.iota(part_i[:, 0:1], [[1, 1]], base=0, channel_multiplier=1).then_inc(s["iotas"], 1)
            pool.iota(part_i[:, 1:3], [[KH, 2]], base=0, channel_multiplier=1).then_inc(s["iotas"], 1)
            pool.iota(sel_i[0:PB, 0:HEADS], [[-1, HEADS]], base=0, channel_multiplier=1).then_inc(s["iotas"], 1)
            pool.iota(sel_i[0:PB, HEADS:HEADS + U], [[-HEADS, U]], base=0, channel_multiplier=1
                      ).then_inc(s["iotas"], 1)
            pool.iota(sel_i[0:HEADS, HEADS + U:], [[0, U], [1, HEADS]], base=0, channel_multiplier=-1
                      ).then_inc(s["iotas"], 1)
            pool.memset(ones[:, :], 1.0).then_inc(s["iotas"], 1)
            pool.memset(Us[:, :], 0.0).then_inc(s["iotas"], 1)
            pool.memset(zeros, 0.0).then_inc(s["zeros"], 1)
            pool.wait_ge(s["zeros"], 1)
            flat_slots = slots_dram.rearrange("(p r) d -> p (r d)", p=P)
            for i in range(ZERO_DMAS):
                pool.dma_start(flat_slots[:, i * ZW:(i + 1) * ZW], zeros).then_inc(s["zero_st"], 16)
            pool.wait_ge(s["t_ready"], 1)
            for g in range(2):
                for name, dst in (("dst", rawI), ("src", srcR), ("ew", ewF)):
                    pool.indirect_dma_start(dst[0:KH, g, :], None, a[name],
                                            bass.IndirectOffsetOnAxis(ap=tI[0:KH, g:g + 1], axis=0)
                                            ).then_inc(s["steps_in"], 16)
            with pool.Fori(0, LOOPS) as m:
                for r in range(EU):
                    pool.wait_ge(s["ln_done"], m * EU + r + 1 + EU)
                    pool.dma_start(h_dram[ds((m * EU + r) * 2 * P, 2 * P), :].rearrange("(n p) d -> p n d", n=2),
                                   ly[:, r, :, :]).then_inc(h_st[r], 16)
            with pool.Fori(0, LAYERS) as l:
                pool.wait_ge(s["hout_ready"], l * PAIRS + EU)
                for i in range(EU):
                    pool.wait_ge(h_st[i], (l + 1) * (16 * LOOPS))
                pool.wait_ge(s["rows_used"], 1)
                held(pool)
                pool.memset(accT[:, :], 0.0).then_inc(s["acc_zero"], 1)
                with pool.Fori(0, PAIRS) as m:
                    for r in range(2):
                        pool.wait_ge(s["pout"], l * NBLK + m * 2 + r + 1)
                        pool.dma_start(kv_dram[ds((m * 2 + r) * P, P), :], kvb[:, r, :]).then_inc(pst[r], 16)
                        pool.dma_start(qx_dram[ds((m * 2 + r) * P, P), :], qxb[:, r, :]).then_inc(pst[r], 16)
                for r in range(2):
                    pool.wait_ge(pst[r], (l + 1) * (PAIRS * 32))
                held(pool)

                def body(step, batch):
                    an = batch(0)
                    if an is None:
                        return
                    for i in range(U):
                        x = step(i)
                        pool.wait_ge(s["v_used"], x.n + 1)
                        if i == 0:
                            held(pool)
                            pool.tensor_copy(idxb[:, an.r, :, :], srcI[:, ds(x.k, U), :]).then_inc(s["idx_done"], 1)
                            pool.wait_ge(s["idx_done"], an.g + 1)
                        held(pool)
                        for j in range(J):
                            pool.indirect_dma_start(
                                kv[:, an.r, i, j, :], None, kv_dram,
                                bass.IndirectOffsetOnAxis(ap=idxb[:, an.r, i, j:j + 1], axis=0)
                            ).then_inc(kv_in[an.r][i], 16)

                edge_loop(pool, l, body)
                with pool.Fori(0, LOOPS) as m:
                    for r in range(EU):
                        pool.wait_ge(s["hout_ready"], l * PAIRS + m * EU + r + 1 + EU)
                        pool.dma_start(h_dram[ds((m * EU + r) * 2 * P, 2 * P), :]
                                       .rearrange("(n p) d -> p n d", n=2), hout[:, r, :, :]).then_inc(h_st[r], 16)
            moe_pool(pool)

        @block.scalar
        def _(act):
            with act.Fori(0, LOOPS) as m:
                for r in range(EU):
                    act.wait_ge(s["ln_var"], m * EU + r + 1)
                    act.activation(sd[:, :], ve[:, :], ACT.Sqrt).then_inc(s["ln_sd"], 1)
            act.wait_ge(s["setup_done"], 1)
            act.wait_ge(s["zero_st"], ZERO_DMAS * 16)
            with act.Fori(0, LAYERS) as l:
                with act.Fori(0, PAIRS) as m:
                    for r in range(2):
                        gi = l * NBLK + m * 2 + r
                        act.wait_ge(s["tr_done"], gi + 1 + 2)
                        act.wait_ge(s["mm_done"], gi + 1)
                        act.activation(hT[:, r, :, :].rearrange("p c t -> p (c t)"), psG[:, 0:D], ACT.Copy
                                       ).then_inc(s["hT_done"], 1)

                def build_G(x):
                    act.wait_ge(s["agg_done"], x.n + 1)
                    for j in range(J):
                        act.activation(G[:, x.r, x.i, j, :], iota_r[:, :], ACT.Abs,
                                       bias=ndl[:, ds(x.k, 1), j]).then_inc(s["g_abs"], 1)
                    act.wait_ge(s["g_abs"], (x.n + 1) * J)
                    flat = G[:, x.r, x.i, :, :].rearrange("p j n -> p (j n)")
                    act.activation(flat, flat, ACT.Relu, bias=1.0, scale=-1.0).then_inc(s["g_ready"], 1)

                def copy_OH(x):
                    act.wait_ge(s["gt_done"], x.n + 1)
                    act.wait_ge(s["q_ready"], x.n * 2 - 2 + 2 * U)
                    act.activation(OH[:, x.half, :, :].rearrange("p j e -> p (j e)"), psG[:, :], ACT.Copy
                                   ).then_inc(s["oh_done"], 1)

                def edge_term(x):
                    act.wait_ge(s["alpha_ready"], x.n + START)
                    for jj in range(2):
                        act.wait_ge(s["k_used"], x.n * 2 + jj + 1 + 2)
                        for j in (2 * jj, 2 * jj + 1):
                            last = act.activation(prod[:, j, :, HD], psQ[:, j, D:QW], ACT.Copy,
                                                  scale=ewT[:, ds(x.k, 1), j])
                        last.then_inc(s["et_done"], 1)

                def exponentials(bn):
                    act.wait_ge(s["chain_B"], bn.g * KB + 10 + START)
                    act.wait_ge(s["pb_done"], bn.g + START)
                    act.activation(pT[:, :], Dm[:, :], ACT.Exp, scale=SCALE).then_inc(s["act_B"], 1)
                    act.wait_ge(s["chain_B"], bn.g * KB + 11 + START)
                    act.activation(gx[:, :], gd[:, :], ACT.Exp, scale=SCALE).then_inc(s["act_B"], 1)

                def copy_weights(bn):
                    act.wait_ge(s["pb_done"], bn.g + 1 + START)
                    for name in ("w_dve", "w_act", "scaled"):
                        act.wait_ge(s[name], bn.g * U - U + RS)
                    act.activation(pB[:, bn.r, :, :, :].rearrange("p j s h -> p (j s h)"),
                                   psB[:, 128:128 + J * PB], ACT.Copy).then_inc(s["act_B"], 1)
                    act.activation(fB[:, bn.r, :, :].rearrange("p s h -> p (s h)"), psB[:, 64:64 + PB], ACT.Copy,
                                   bias=1.0).then_inc(s["act_B"], 1)

                def weight_column(x):
                    act.wait_ge(s["act_B"], x.batch.g * KACT + 3 + START)
                    act.wait_ge(s["agg_done"], x.n - 1 + RS)
                    act.activation(W[:, x.half, :, :, HD], pB[:, x.r, :, x.i, :], ACT.Copy).then_inc(s["w_act"], 1)

                def keep_sums(x, b):
                    here = accF[:, ds(b, 1), :].rearrange("p b w -> p (b w)")
                    act.wait_ge(s["agg_done"], x.n + 1 + RS)
                    held(act)
                    act.activation(here, psA[:, 0:HEADS * AW], ACT.Copy).then_inc(s["acc_done"], 1)

                def body(step, batch):
                    for i in range(U):
                        b = block_of(act, step(i - LAG - 1))
                        if step(i + 1):
                            copy_OH(step(i + 1))
                        if i == 1 and batch(-1):
                            exponentials(batch(-1))
                        if step(i):
                            edge_term(step(i))
                        if step(i - LAG):
                            weight_column(step(i - LAG))
                        if step(i - LAG - 1):
                            keep_sums(step(i - LAG - 1), b)
                        if step(i + 2):
                            build_G(step(i + 2))
                        if i == 1 and batch(-1):
                            copy_weights(batch(-1))

                edge_loop(act, l, body)
                with act.Fori(0, LOOPS) as m:
                    for r in range(EU):
                        act.wait_ge(s["z_ready"], l * PAIRS + m * EU + r + 1)
                        act.activation(ez[:, :], zc[:, :], ACT.Exp, scale=-1.0).then_inc(s["z_exp"], 1)
            moe_act(act)

        @block.tensor
        def _(pe):
            pe.wait_ge(s["steps_ready"], 1)
            for g in range(2):
                for i, arr in enumerate((srcF, dloc, ewF)):
                    bank = (psQ[:, 0, :], psQ[:, 1, :], psQ[:, 2, :], psQ[:, 3, :], psG[:, :], psA[:, :])[3 * g + i]
                    for j in range(J):
                        last = pe.transpose(bank[:, j * P:j * P + KH], arr[0:KH, g, j:SE:J], ident[0:KH, 0:KH])
                    last.then_inc(s["setup_t"], 1)
            pe.wait_ge(s["setup_done"], 1)
            with pe.Fori(0, LAYERS) as l:
                pe.wait_ge(s["w_in"], (l + 1) * (7 * 16))
                held(pe)
                with pe.Fori(0, PAIRS) as m:
                    for r in range(2):
                        gi = l * NBLK + m * 2 + r
                        pe.wait_ge(hb_in[r], (l * PAIRS + m + 1) * 16)
                        pe.wait_ge(s["hT_done"], gi + START)
                        for c in range(2):
                            last = pe.transpose(psG[:, c * P:(c + 1) * P], hb[:, r, c * P:(c + 1) * P], ident[:, :])
                        last.then_inc(s["tr_done"], 1)
                        pe.wait_ge(s["hT_done"], gi + 1 + START)
                        pe.wait_ge(s["ev_done"], gi + 1)
                        for half in range(2):
                            for c in range(2):
                                last = pe.matmul(psQ[:, 2 * r + half, :], hT[:, r, c, :],
                                                 wcat[:, c, half * 2 * D:(half + 1) * 2 * D],
                                                 start=(c == 0), stop=(c == 1))
                        last.then_inc(s["mm_done"], 1)

                def turn_G(x):
                    pe.wait_ge(s["g_ready"], x.n + 1)
                    pe.wait_ge(s["oh_done"], x.n + START)
                    for j in range(J):
                        last = pe.transpose(psG[:, j * P:(j + 1) * P], G[:, x.r, x.i, j, :], ident[:, :])
                    last.then_inc(s["gt_done"], 1)

                def expand_q(x):
                    pe.wait_ge(s["oh_done"], x.n + 1 + START)
                    pe.wait_ge(q_in[x.i], (x.batch.g + 1) * 16)
                    for jj in range(2):
                        pe.wait_ge(s["et_done"], x.n * 2 + jj + 1)
                        for j in (2 * jj, 2 * jj + 1):
                            last = pe.matmul(psQ[:, j, 0:QW], OH[:, x.half, j, :], qring[:, x.i, :],
                                             start=True, stop=True)
                        last.then_inc(s["q_ready"], 1)

                def turn_scores(bn):
                    pe.wait_ge(s["alpha_ready"], (bn.g + 1) * U + START)
                    pe.wait_ge(s["chain_B"], bn.g * KB + START)
                    held(pe)
                    for j in range(J):
                        last = pe.transpose(psT[0:PB, j:SE:J], alpha[:, bn.r, j, :, :].rearrange(
                            "p s h -> p (s h)"), ident[:, :])
                    last.then_inc(s["at_done"], 1)

                def maxima_up(bn):
                    pe.wait_ge(s["act_B"], bn.g * KACT + START)
                    pe.wait_ge(s["chain_B"], bn.g * KB + 2 + START)
                    held(pe)
                    pe.matmul(psB[0:HEADS, 0:U], selA[:, :], LB[:, :], start=True, stop=True
                              ).then_inc(s["max_up"], 1)

                def maxima_down(bn):
                    pe.wait_ge(s["chain_B"], bn.g * KB + 5 + START)
                    held(pe)
                    pe.matmul(psB[0:PB, 32:33], lhs2[:, :, :].rearrange("a s h -> a (s h)"), ones[0:HEADS, 0:1],
                              start=True, stop=True).then_inc(s["max_down"], 1)

                def turn_weights(bn):
                    pe.wait_ge(s["chain_B"], bn.g * KB + KB + START)
                    held(pe)
                    pe.matmul(psB[:, 64:64 + PB], crossOH[:, :], gm[:, :], start=True, stop=True)
                    pe.wait_ge(s["act_B"], bn.g * KACT + 1 + START)
                    held(pe)
                    for j in range(J):
                        last = pe.transpose(psB[:, 128 + j * PB:128 + (j + 1) * PB], pT[:, j:SE:J],
                                            ident[0:PB, 0:PB])
                    last.then_inc(s["pb_done"], 1)

                def add_up(x):
                    pe.wait_ge(s["w_dve"], x.n + 1 + RS)
                    pe.wait_ge(s["w_act"], x.n + 1 + RS)
                    pe.wait_ge(s["acc_done"], x.n + START)
                    for j in range(J):
                        pe.matmul(psA[:, 0:HEADS * AW], G[:, x.r, x.i, j, :],
                                  W[:, x.half, j, :, :].rearrange("p h w -> p (h w)"), start=(j == 0), stop=False)

                def add_before(x, b):
                    here = accF[:, ds(b, 1), :].rearrange("p b w -> p (b w)")
                    pe.wait_ge(s["scaled"], x.n + 1 + RS)
                    held(pe)
                    pe.matmul(psA[:, 0:HEADS * AW], ident[:, :], here, start=False, stop=True
                              ).then_inc(s["agg_done"], 1)

                def body(step, batch):
                    for i in range(U):
                        b = block_of(pe, step(i - LAG - 1))
                        if step(i + 1):
                            turn_G(step(i + 1))
                        if step(i - LAG - 1):
                            add_up(step(i - LAG - 1))
                            add_before(step(i - LAG - 1), b)
                        if i == 0 and batch(-1):
                            maxima_up(batch(-1))
                        if step(i + 1):
                            expand_q(step(i + 1))
                        if i == 0 and batch(-1):
                            maxima_down(batch(-1))
                        if i == 1 and batch(-1):
                            turn_weights(batch(-1))
                        if i == U - 1 and batch(0):
                            turn_scores(batch(0))

                edge_loop(pe, l, body)
            moe_pe(pe)

        @block.vector
        def _(dve):
            setup = Chain(dve, s["setup_chain"])
            dve.wait_ge(s["iotas"], 8)
            dve.tensor_copy(iota_r[:, :], iota_i[:, 0:P])
            dve.tensor_copy(iota_c[:, :], part_i[:, 0:1])
            dve.tensor_copy(kcol[:, :], part_i[:, 1:3])
            nsA, nsB = sel_i[0:PB, 0:HEADS], sel_i[0:PB, HEADS:HEADS + U]
            dve.tensor_scalar(nsA, nsA, 7, None, ALU.bitwise_and)
            setup.link(dve.tensor_scalar(nsB, nsB, 3, None, ALU.arith_shift_right))
            dve.tensor_scalar(selA[:, :], nsA, 0.0, None, ALU.is_equal)
            dve.tensor_scalar(selB[:, :], nsB, 0.0, None, ALU.is_equal)
            dve.tensor_scalar(selD[:, :, :].rearrange("a s h -> a (s h)"), sel_i[0:HEADS, HEADS + U:], 0.0, None,
                              ALU.is_equal)
            dve.tensor_scalar(ident[:, :], iota_r[:, :], iota_c[:, 0:1], None, ALU.is_equal)
            dve.tensor_scalar(tri[:, :], iota_r[:, :], iota_c[:, 0:1], None, ALU.is_ge)
            dve.tensor_scalar(e8[:, :], iota_r[:, 0:EXPERTS], -1.0, float(EXPERTS), ALU.mult, ALU.add)
            dve.wait_ge(s["last_in"], 16)
            setup.link(dve.tensor_scalar(lastI[0:KH, :], lastI[0:KH, :], 7, None, ALU.logical_shift_right))
            setup.link(dve.tensor_copy(posA[0:KH, :], lastI[0:KH, :]))
            setup.link(dve.tensor_copy(cmpT[0:KH, :], iota_i[0:KH, 0:SUPER - 1]))
            setup.link(dve.tensor_tensor(posA[0:KH, :], posA[0:KH, :], cmpT[0:KH, :], ALU.add))
            for g in range(2):
                setup.link(dve.tensor_scalar(cmpT[0:KH, :], posA[0:KH, :], kcol[0:KH, g:g + 1], None, ALU.is_lt))
                setup.link(dve.tensor_reduce(tcol[0:KH, g:g + 1], cmpT[0:KH, :], AX, ALU.add))
            setup.link(dve.tensor_copy(tI[0:KH, :], tcol[0:KH, :]))
            dve.sem_inc(s["t_ready"], 1)
            setup.link(dve.tensor_tensor(nbc[0:KH, :], kcol[0:KH, :], tcol[0:KH, :], ALU.subtract))
            setup.link(dve.tensor_scalar(small3[0:KH, :, 2], nbc[0:KH, :], float(NBLK - 1), None, ALU.min))
            setup.link(dve.tensor_scalar(nbc[0:KH, :], small3[0:KH, :, 2], -float(P), None, ALU.mult))
            dve.wait_ge(s["steps_in"], 6 * 16)
            dve.tensor_copy(dstF[0:KH, :, :], rawI[0:KH, :, :])
            setup.link(dve.tensor_copy(srcF[0:KH, :, :], srcR[0:KH, :, :]))
            for g in range(2):
                dve.tensor_copy(small3[0:KH, g, 0:1], dstF[0:KH, g, 0:1])
                dve.tensor_copy(small3[0:KH, g, 1:2], dstF[0:KH, g, SE - 1:SE])
                setup.link(dve.tensor_scalar(dloc[0:KH, g, :], dstF[0:KH, g, :], nbc[0:KH, g:g + 1], -1.0,
                                             ALU.add, ALU.max))
                setup.link(dve.tensor_scalar(dloc[0:KH, g, :], dloc[0:KH, g, :], float(P), None, ALU.min))
                dve.memset(res2[0:KH, g, 0:1], 0.0)
                dve.memset(res2[0:KH, g, SE:SE + 1], 0.0)
                setup.link(dve.tensor_tensor(res2[0:KH, g, 1:SE], dloc[0:KH, g, 1:SE], dloc[0:KH, g, 0:SE - 1],
                                             ALU.not_equal))
                setup.link(dve.tensor_scalar(res2[0:KH, g, 1:SE], res2[0:KH, g, 1:SE], -BIG, None, ALU.mult))
            dve.sem_inc(s["steps_ready"], 1)
            for g in range(2):
                for i, dst in enumerate((srcI, ndl, ewT)):
                    bank = (psQ[:, 0, :], psQ[:, 1, :], psQ[:, 2, :], psQ[:, 3, :], psG[:, :], psA[:, :])[3 * g + i]
                    dve.wait_ge(s["setup_t"], 3 * g + i + 1)
                    o_ = dst[:, g * KH:(g + 1) * KH, :].rearrange("p k j -> p j k")
                    b_ = bank.rearrange("p (j k) -> p j k", j=J)[:, :, 0:KH]
                    if i == 1:
                        dve.tensor_scalar(o_, b_, -1.0, None, ALU.mult)
                    else:
                        dve.tensor_copy(o_, b_)
            r_first, r_last, r_blk, cont, whole, t0, t1, t2, t3, crs = [x[0:HEADS, :] for x in row]
            dve.wait_ge(s["rows_in"], 3 * 16)
            dve.tensor_copy(blkI[:, :], r_blk[0:1, :])
            dve.memset(cont[:, 0:1], 0.0)
            setup.link(dve.tensor_tensor(cont[:, 1:], r_blk[:, 1:], r_blk[:, :SLOTS - 1], ALU.is_equal))
            setup.link(dve.tensor_tensor(t0[:, 1:], r_first[:, 1:], r_last[:, :SLOTS - 1], ALU.is_equal))
            setup.link(dve.tensor_tensor(cont[:, 1:], cont[:, 1:], t0[:, 1:], ALU.mult))
            setup.link(dve.tensor_tensor(whole, r_first, r_last, ALU.is_equal))
            setup.link(dve.tensor_tensor(whole, whole, cont, ALU.mult))
            dve.tensor_scalar(dn8[:, :], cont, 1.0, BIG, ALU.subtract, ALU.mult)
            dve.tensor_scalar(dd8[:, :], whole, 1.0, BIG, ALU.subtract, ALU.mult)
            setup.link(dve.tensor_scalar(t1, r_blk, -float(P), 1.0, ALU.mult, ALU.add))
            setup.link(dve.tensor_tensor(t1, t1, r_first, ALU.add))
            setup.link(dve.tensor_tensor(t1, t1, cont, ALU.mult))
            setup.link(dve.tensor_scalar(crs, t1, 1.0, None, ALU.subtract))
            dve.sem_inc(s["rows_ready"], 1)
            dve.wait_ge(s["setup_st"], 2 * (HEADS + 3) * 16 + 16)
            dve.sem_inc(s["rows_used"], 1)
            dve.sem_inc(s["setup_done"], 1)

            ln = Chain(dve, s["ln_chain"], 3)

            def layer_norm(x, y, it, free, n_free):
                ln.at(it)
                for n in range(2):
                    last = dve.bn_stats(stats[:, n, :], x[:, n, :])
                ln.link(last)
                held(dve)
                for n in range(2):
                    last = dve.bn_aggr(mv[:, n, :], stats[:, n, :])
                ln.link(last)
                dve.tensor_scalar(ve[:, :], mv[:, :, 1], 1e-5, None, ALU.add).then_inc(s["ln_var"], 1)
                dve.wait_ge(s["ln_sd"], it + 1)
                ln.link(dve.reciprocal(rstd[:, :], sd[:, :]))
                if free is not None:
                    dve.wait_ge(free, n_free)
                for n in range(2):
                    last = dve.tensor_scalar(y[:, n, :], x[:, n, :], mv[:, n, 0:1], rstd[:, n:n + 1],
                                             ALU.subtract, ALU.mult)
                last.then_inc(s["ln_done"], 1)

            def input_norm(m, first):
                for r in range(EU):
                    dve.wait_ge(x_in[r], (m + 1) * 16)
                    layer_norm(lx[:, r, :, :], ly[:, r, :, :], m * EU + r, None if first else h_st[r], m * 16)

            rounds(dve, LOOPS, input_norm)

            with dve.Fori(0, LAYERS) as l:
                dve.wait_ge(s["w_in"], (l + 1) * (7 * 16))
                dve.tensor_tensor(wA[:, :], wb_bc[:, 0, :], wb_bc[:, 2, :], ALU.add)
                dve.tensor_tensor(wB[:, :], wb_bc[:, 1, :], wb_bc[:, 2, :], ALU.subtract)
                held(dve)
                pc = Chain(dve, s["proj_chain"], 1)
                def project(m, first):
                    for r in range(2):
                        gi = l * NBLK + m * 2 + r
                        pc.at(gi)
                        dve.wait_ge(s["mm_done"], gi + 1 + 2)
                        if not first:
                            dve.wait_ge(pst[r], (l * PAIRS + m) * 32)
                        dve.tensor_tensor(kvb[:, r, :], psQ[:, 2 * r, :], bias_bc[:, 0:2 * D], ALU.add)
                        dve.tensor_tensor(qxb[:, r, 0:2 * D], psQ[:, 2 * r + 1, :], bias_bc[:, 2 * D:],
                                          ALU.add).then_inc(s["ev_done"], 1)
                        dve.wait_ge(s["ev_done"], gi + 1 + 2)
                        pc.link(dve.tensor_tensor(qprod, qxb[:, r, D:2 * D], we_bc[:, :], ALU.mult))
                        dve.tensor_reduce(qxb[:, r, 2 * D:QX], qprod.rearrange("p (h d) -> p h d", h=HEADS),
                                          AX, ALU.add).then_inc(s["pout"], 1)

                rounds(dve, PAIRS, project)
                dve.wait_ge(s["acc_zero"], l + 1)
                dve.wait_ge(s["cross_in"], U * 16)

                def scores(x):
                    dve.wait_ge(s["alpha_ready"], x.n + START)
                    for jj in range(2):
                        dve.wait_ge(s["q_ready"], x.n * 2 + jj + 1 + 2 * U)
                        if jj == 0:
                            dve.wait_ge(kv_in[x.r][x.i], (x.use + 1) * (16 * J))
                        jr = slice(2 * jj, 2 * jj + 2)
                        dve.tensor_tensor(prod[:, jr, :, 0:HD], split(psQ[:, jr, 0:D]),
                                          split(kv[:, x.r, x.i, jr, 0:D]), ALU.mult).then_inc(s["k_used"], 1)

                def reduce_scores(x):
                    dve.wait_ge(s["k_used"], (x.n + 1) * 2 + 2)
                    dve.wait_ge(s["et_done"], (x.n + 1) * 2 + 2)
                    dve.tensor_reduce(alpha[:, x.r, :, x.i, :], prod[:, :, :, :], AX, ALU.add
                                      ).then_inc(s["alpha_ready"], 1)

                cb = Chain(dve, s["chain_B"], KB, START)

                def maxima_1(bn):
                    cb.at(bn.g)
                    dve.wait_ge(s["res_in"], (bn.g + 1) * 16)
                    dve.wait_ge(s["at_done"], bn.g + 1)
                    cb.link(dve.tensor_tensor_scan(F1[:, :], res[:, 0:SE], psT[0:PB, :], -BIG, ALU.add, ALU.max))
                    cb.inc(dve.tensor_scalar(LB[:, :], selB[:, :], F1[:, SE - 1:SE], None, ALU.mult))

                def maxima_2(bn):
                    cb.at(bn.g, 2)
                    dve.wait_ge(s["max_up"], bn.g + 1)
                    cb.link(dve.tensor_tensor_scan(Us[:, 1:], dd8[:, ds(bn.B * U, U)], psB[0:HEADS, 0:U], Us[:, 0:1],
                                                   ALU.add, ALU.max))
                    cb.link(dve.tensor_tensor(cc[:, :], Us[:, 0:U], dn8[:, ds(bn.B * U, U)], ALU.add))
                    cb.inc(dve.tensor_tensor(lhs2[:, :, :], selD[:, :, :],
                                             cc[:, :].unsqueeze(2).to_broadcast([HEADS, U, HEADS]), ALU.mult))
                    cb.inc(dve.tensor_copy(Us[:, 0:1], Us[:, U:U + 1]))

                def maxima_3(bn):
                    cb.at(bn.g, 6)
                    dve.wait_ge(s["max_down"], bn.g + 1)
                    cb.link(dve.tensor_copy(ccol[:, :], psB[0:PB, 32:33]))
                    cb.link(dve.tensor_tensor_scan(F2[:, :], res[:, 0:SE], psT[0:PB, :], ccol[:, 0:1],
                                                   ALU.add, ALU.max))
                    cb.inc(dve.tensor_tensor_scan(M[:, ::-1], res[:, SE:0:-1], F2[:, ::-1], -BIG,
                                                  ALU.add, ALU.max))
                    cb.wait()
                    dve.sem_inc(s["scanned"], 1)
                    cb.inc(dve.tensor_tensor(Dm[:, :], psT[0:PB, :], M[:, :], ALU.subtract))
                    cb.inc(dve.tensor_tensor(gd[:, :], ccol[:, :], M[:, 0:1], ALU.subtract))

                def maxima_4(bn):
                    cb.at(bn.g, 11)
                    cb.inc(dve.tensor_scalar(crossOH[:, :], iota_r[0:PB, :], crossc[:, ds(bn.B, 1)], None,
                                             ALU.is_equal))
                    dve.wait_ge(s["act_B"], bn.g * KACT + 2 + START)
                    cb.inc(dve.scalar_tensor_tensor(gm[:, :], ident[0:PB, 0:PB], gx[:, 0:1], ident[0:PB, 0:PB],
                                                    ALU.mult, ALU.subtract))

                def weigh(x):
                    dve.wait_ge(s["act_B"], x.batch.g * KACT + 3 + START)
                    dve.wait_ge(s["agg_done"], x.n - 1 + RS)
                    dve.tensor_tensor(W[:, x.half, :, :, 0:HD], split(kv[:, x.r, x.i, :, D:2 * D]),
                                      pB[:, x.r, :, x.i, :].unsqueeze(3).to_broadcast([P, J, HEADS, HD]), ALU.mult
                                      ).then_inc(s["v_used"], 1)
                    dve.tensor_tensor(W[:, x.half, :, :, HD + 1], pB[:, x.r, :, x.i, :],
                                      ewT[:, ds(x.k, 1), :].rearrange("p k j -> p (k j)").unsqueeze(2)
                                      .to_broadcast([P, J, HEADS]), ALU.mult).then_inc(s["w_dve"], 1)

                def rescale(x, b):
                    here = acc[:, ds(b, 1), :, :].rearrange("p b h w -> p (b h) w")
                    dve.wait_ge(s["act_B"], x.batch.g * KACT + 4 + START)
                    dve.wait_ge(s["acc_done"], x.n + START)
                    dve.tensor_tensor(here, here, fB[:, x.r, x.i, :].unsqueeze(2).to_broadcast([P, HEADS, AW]),
                                      ALU.mult).then_inc(s["scaled"], 1)

                def body(step, batch):
                    for i in range(U):
                        if step(i):
                            scores(step(i))
                        if i == 0 and batch(-1):
                            maxima_1(batch(-1))
                        if step(i - LAG):
                            weigh(step(i - LAG))
                        b = block_of(dve, step(i - LAG))
                        if i == 0 and batch(-1):
                            maxima_2(batch(-1))
                        if i == 1 and batch(-1):
                            maxima_4(batch(-1))
                        if step(i):
                            reduce_scores(step(i))
                        if step(i - LAG):
                            rescale(step(i - LAG), b)
                        if i == 0 and batch(-1):
                            maxima_3(batch(-1))

                edge_loop(dve, l, body)

                dve.wait_ge(s["acc_done"], (l + 1) * STEPS + START)
                held(dve)
                ep = Chain(dve, s["ep_chain"], 12)
                with dve.Fori(0, LOOPS) as m:
                    for r in range(EU):
                        it = l * PAIRS + m * EU + r
                        ep.at(it)
                        two = acc[:, ds((m * EU + r) * 2, 2), :, :]
                        bc = lambda x: x.unsqueeze(3).to_broadcast([P, 2, HEADS, HD])
                        over = lambda w: w[:, :].unsqueeze(1).to_broadcast([P, 2, D])
                        ep.link(dve.tensor_scalar(den[:, :, :], two[:, :, :, HD], 1e-16, None, ALU.add))
                        ep.link(dve.reciprocal(rden[:, :, :], den[:, :, :]))
                        ep.inc(dve.tensor_tensor(tew[:, :, :], two[:, :, :, HD + 1], rden[:, :, :], ALU.mult))
                        ep.link(dve.tensor_tensor(split(ov), two[:, :, :, 0:HD], bc(rden[:, :, :]), ALU.mult))
                        ep.link(dve.tensor_tensor(split(tw), split(over(we_bc)), bc(tew[:, :, :]), ALU.mult))
                        ep.link(dve.tensor_tensor(ov, ov, tw, ALU.add))
                        dve.wait_ge(xr_in[r], (l * LOOPS + m + 1) * 16)
                        ep.inc(dve.tensor_tensor(q1, ov, over(wA), ALU.mult))
                        ep.link(dve.tensor_tensor(tw, xr[:, r, :, :], over(wB), ALU.mult))
                        ep.link(dve.tensor_tensor(q1, q1, tw, ALU.add))
                        dve.tensor_reduce(zc[:, :], q1, AX, ALU.add).then_inc(s["z_ready"], 1)
                        ep.inc(dve.tensor_tensor(tw, xr[:, r, :, :], ov, ALU.subtract))
                        dve.wait_ge(s["z_exp"], it + 1)
                        ep.link(dve.tensor_scalar(zc[:, :], ez[:, :], 1.0, None, ALU.add))
                        ep.link(dve.reciprocal(beta[:, :], zc[:, :]))
                        dve.wait_ge(h_st[r], ((l + 1) * LOOPS + m) * 16)
                        for n in range(2):
                            last = dve.scalar_tensor_tensor(hout[:, r, n, :], tw[:, n, :], beta[:, n:n + 1],
                                                            ov[:, n, :], ALU.mult, ALU.add)
                        last.then_inc(s["hout_ready"], 1)
                        dve.wait_ge(s["hout_ready"], it + 1 + EU)
            moe_dve(dve, layer_norm)


def kernel(**inputs):
    import concourse.bacc as bacc
    from concourse.bass_utils import run_bass_kernel_spmd

    g = {k: np.asarray(v) for k, v in inputs.items()}
    gnn = lambda name, layer: g[f"L0_gnn_{name}{min(layer, 1) + 1}"]
    pad = SUPER * SE - EDGES
    dst = np.concatenate([g["dst"], np.full(pad, FAR, np.int32)]).reshape(SUPER, SE)
    arrays = {
        "x": np.concatenate([g["x"], np.zeros((NPAD - NODES, D), np.float32)]),
        "dst": dst,
        "last": np.ascontiguousarray(dst[:SUPER - 1, SE - 1]).reshape(1, -1),
        "src": np.concatenate([g["src"], np.zeros(pad, np.int32)]).reshape(SUPER, SE),
        "ew": np.concatenate([g["edge_weight"], np.zeros(pad, np.float32)]).reshape(SUPER, SE),
        "wcat": np.concatenate([np.concatenate([gnn(n, l) for n in ("Wk", "Wv", "Wskip", "Wq")], axis=1)
                                for l in range(LAYERS)]),
        "bcat": np.stack([np.concatenate([gnn(n, l) for n in ("bk", "bv", "bskip", "bq")])
                          for l in range(LAYERS)]),
        "we": np.concatenate([gnn("We", l) for l in range(LAYERS)]),
        "wbeta": np.concatenate([gnn("Wbeta", l).reshape(3, D) for l in range(LAYERS)]),
        "gate_w": g["L0_ffn_gate_w"],
        "gate_b": g["L0_ffn_gate_b"].reshape(1, EXPERTS),
        "w1": g["L0_ffn_w1"].reshape(EXPERTS * D, FF),
        "b1": np.ascontiguousarray(g["L0_ffn_b1"].reshape(EXPERTS, FF // P, P).transpose(0, 2, 1)
                                   ).reshape(EXPERTS * P, FF // P),
        "w2": g["L0_ffn_w2"].reshape(EXPERTS * FF, D),
        "b2": g["L0_ffn_b2"],
    }
    arrays = {f"in_{k}": np.ascontiguousarray(v) for k, v in arrays.items()}
    nc = bacc.Bacc("TRN2", target_bir_lowering=False, num_devices=1)
    a = {k[3:]: nc.dram_tensor(k, v.shape, mybir.dt.from_np(v.dtype), kind="ExternalInput").ap()
         for k, v in arrays.items()}
    out = nc.dram_tensor("out", (NPAD, D), F32, kind="ExternalOutput").ap()
    build(nc, a, out)
    r = run_bass_kernel_spmd(nc, [arrays], core_ids=[0])
    return r.results[0]["out"][:NODES]
```

```python
from contextlib import ExitStack

import numpy as np

import concourse.bass as bass
from concourse import mybir

F32 = mybir.dt.float32
I32 = mybir.dt.int32
ALU = mybir.AluOpType
ACT = mybir.ActivationFunctionType
AX = mybir.AxisListType.X
ds = bass.ds

P = 128
NODES, EDGES, D, HEADS = 6250, 100000, 256, 8
HD = D // HEADS
LAYERS = 3
J = 4
SE = P * J
SUPER = -(-EDGES // SE)
NBLK = 50
REAL_BLK = -(-NODES // P)
NPAD = NBLK * P
U = 5
STEPS = -(-(SUPER + REAL_BLK - 1) // U) * U
NB = STEPS // U
RS = 2 * U
LAG = 7
KH = -(-STEPS // 2)
SLOTS = 2 * KH
PB = U * HEADS
AW = HD + 2
QW = D + HEADS
QX = QW + 1 + D
BIG = 1e30
HUGE = 1e38
SCALE = float(HD) ** -0.5
FAR = 1 << 20

START = 1
EXPERTS, FF = 8, 1024
CAP = max(1, -(-5 * NODES // (4 * EXPERTS)))
CAPP = 1024
CT = CAPP // P
HALF = 489
HALVES = ((0, 512), (512, 2 * HALF - 512))
assert NB % 2 == 1 and NBLK % 10 == 0 and 2 * HALF >= CAP

KB = 13
KACT = 4


class Chain:

    def __init__(self, eng, sem, per=None, start=0):
        self.eng, self.sem, self.per, self.start, self.base, self.n = eng, sem, per, start, start, 0

    def at(self, iteration, done=0):
        self.base, self.n = iteration * self.per + self.start, done

    def inc(self, ins):
        self.n += 1
        ins.then_inc(self.sem, 1)

    def wait(self):
        self.eng.wait_ge(self.sem, self.base + self.n)

    def link(self, ins):
        self.inc(ins)
        self.wait()




def build(nc, a, out):
    dram = lambda name, shape, dt=F32: nc.dram_tensor(name, shape, dt, kind="Internal").ap()
    kv_dram = dram("kv_dram", (NPAD, 2 * D))
    qx_dram = dram("qx_dram", (NPAD, QX))
    res_dram = dram("res_dram", (SLOTS * HEADS, SE + 1))
    meta_dram = dram("meta_dram", (4, SLOTS))
    x2_dram = dram("x2_dram", (NPAD, D))
    xn_dram = dram("xn_dram", (NPAD, D))
    slots_dram = dram("slots_dram", (EXPERTS * CAPP, D))
    y_dram = dram("y_dram", (EXPERTS * 2 * HALF, D))

    with ExitStack() as ctx:
        def sb(name, shape, dt=F32):
            return ctx.enter_context(nc.sbuf_tensor("s_" + name, shape, dt))

        def pb(name, shape):
            return ctx.enter_context(nc.psum_tensor(name, shape, F32))

        def sem(name):
            return ctx.enter_context(nc.semaphore(name))

        psQ = pb("psQ", [P, 4, 512])
        psG = pb("psG", [P, 512])
        psA = pb("psA", [P, 512])
        psT = pb("psT", [P, 512])
        psB = pb("psB", [P, 512])

        part_i = sb("part_i", [P, 4], I32)
        sel_i = sb("sel_i", [P, HEADS + U + U * HEADS], I32)
        iota_r = sb("iota_r", [P, P])
        iota_c = sb("iota_c", [P, 1])
        ident = sb("ident", [P, P])
        tri = sb("tri", [P, P])
        ones = sb("ones", [P, P])
        selA = sb("selA", [PB, HEADS])
        selB = sb("selB", [PB, U])
        selD = sb("selD", [HEADS, U, HEADS])
        e8 = sb("e8", [P, EXPERTS])
        srcI = sb("srcI", [P, SLOTS, J], I32)
        ndl = sb("ndl", [P, SLOTS, J])
        ewT = sb("ewT", [P, SLOTS, J])
        dn8 = sb("dn8", [HEADS, SLOTS])
        dd8 = sb("dd8", [HEADS, SLOTS])
        blkI = sb("blkI", [1, SLOTS], I32)
        crossc = sb("crossc", [PB, NB])
        accT = sb("acc", [P, NBLK * HEADS * AW])
        acc = accT[:, :].rearrange("p (b h w) -> p b h w", b=NBLK, h=HEADS)
        accF = accT[:, :].rearrange("p (b w) -> p b w", b=NBLK)
        RING = 2 * U * J * 2 * D
        ringT = sb("ring", [P, RING])
        kv = ringT[:, :].rearrange("p (r s j w) -> p r s j w", r=2, s=U, j=J)
        G = sb("G", [P, 2, U, J, P])
        OH = sb("OH", [P, 2, J, P])
        qring = sb("qring", [P, U, QW])
        prod = sb("prod", [P, J, HEADS, HD + 1])
        alpha = sb("alpha", [P, 2, J, U, HEADS])
        res = sb("res", [PB, SE + 1])
        F1 = sb("F1", [PB, SE])
        F2 = sb("F2", [PB, SE])
        M = sb("M", [PB, SE])
        Dm, pT = F1, F2
        LB = sb("LB", [PB, U])
        Us = sb("Us", [HEADS, U + 1])
        cc = sb("cc", [HEADS, U])
        lhs2 = sb("lhs2", [HEADS, U, HEADS])
        ccol = sb("ccol", [PB, 1])
        gd = sb("gd", [PB, 1])
        gx = sb("gx", [PB, 1])
        gm = sb("gm", [PB, PB])
        crossOH = sb("crossOH", [PB, P])
        pB = sb("pB", [P, 2, J, U, HEADS])
        fB = sb("fB", [P, 2, U, HEADS])
        W = sb("W", [P, 2, J, HEADS, AW])
        idxb = sb("idxb", [P, 2, U, J], I32)
        wx = sb("wx", [P, 3, HEADS + 1])
        wA = sb("wA", [P, D])
        wB = sb("wB", [P, D])
        den = sb("den", [P, 2, HEADS])
        rden = sb("rden", [P, 2, HEADS])
        tew = sb("tew", [P, 2, HEADS])
        zc = sb("zc", [P, 2])
        zr = sb("zr", [P, 2])
        ez = sb("ez", [P, 2])
        beta = sb("beta", [P, 2])
        stats = sb("stats", [P, 2, 6])
        mv = sb("mv", [P, 2, 2])
        ve = sb("ve", [P, 2])
        sd = sb("sd", [P, 2])
        rstd = sb("rstd", [P, 2])
        tI = sb("tI", [P, 2], I32)
        small3 = sb("small3", [P, 2, 3])

        def view(at, *shape, of=ringT, room=RING, dt=None):
            n = int(np.prod(shape))
            assert at + n <= room, (at, n)
            names = " ".join(f"d{i}" for i in range(len(shape)))
            flat = of[:, at:at + n]
            if dt is not None:
                flat = flat.bitcast(dt)
            if len(shape) == 1:
                return flat, at + n
            return flat.rearrange(f"p ({names}) -> p {names}",
                                  **{f"d{i}": x for i, x in enumerate(shape)}), at + n

        o = 0
        rawI, o = view(o, 2, SE, dt=I32)
        srcR, o = view(o, 2, SE, dt=I32)
        dstF, o = view(o, 2, SE)
        srcF, o = view(o, 2, SE)
        ewF, o = view(o, 2, SE)
        dloc, o = view(o, 2, SE)
        res2, o = view(o, 2, SE + 1)
        posA, o = view(o, SUPER - 1)
        cmpT, o = view(o, SUPER - 1)
        kcol, o = view(o, 2)
        iota_i, o = view(o, SUPER, dt=I32)
        lastI, o = view(o, SUPER - 1, dt=I32)
        tcol, o = view(o, 2)
        nbc, o = view(o, 2)
        o += o % 2
        row = [None] * 10
        for i in range(10):
            row[i], _ = view(i * SLOTS, SLOTS, of=accT, room=NBLK * HEADS * AW)
        EU = 5
        ACCN = NBLK * HEADS * AW
        o = 0
        wcat, o = view(o, 2, 4 * D)
        bias_bc, o = view(o, 4 * D)
        w_and_bias, _ = view(0, 3, 4 * D)
        we_next, o = view(o, D)
        we_bc, o = view(o, D)
        wb_bc, o = view(o, 2, D)
        wb_next, o = view(o, 2, D)
        hT, o = view(o, 2, 2, P)
        ov, o = view(o, 2, D)
        tw, o = view(o, 2, D)
        q1, o = view(o, 2, D)
        o2 = o
        kvb, o = view(o, EU, 2, 2 * D)
        qxb, o = view(o, EU, 2, 2, D + HEADS + 1)
        qx_rows = qxb.rearrange("p e n t w -> p e n (t w)")
        hin, o = view(o, EU, 2, D)
        tmp, _ = view(RING - 3 * D, 3, D)
        lx, o2 = view(o2, EU, 2, D)
        ly, o2 = view(o2, EU, 2, D)
        lh, o2 = view(o2, EU, 2, D)
        GW = 2 * U * J * P
        GT = G[:, :, :, :, :].rearrange("p r i j n -> p (r i j n)")
        xr, _ = view(0, EU, 2, D + 1, of=GT, room=GW)

        class Sems(dict):
            def __missing__(self, name):
                self[name] = sem(name)
                return self[name]

        s = Sems()
        kv_in = [[sem(f"kv_in_{r}_{i}") for i in range(U)] for r in range(2)]
        q_in = [sem(f"q_in_{i}") for i in range(U)]
        x_in = [sem(f"x_in_{i}") for i in range(EU)]
        xr_in = [sem(f"xr_in_{i}") for i in range(EU)]
        h_st = [sem(f"h_stored_{i}") for i in range(EU)]
        pst = [sem(f"proj_stored_{i}") for i in range(EU)]
        PAIRS = NBLK // 2
        LOOPS = PAIRS // EU

        class Batch:

            def __init__(self, l, m, c):
                self.B, self.r = m * 2 + c, c % 2
                self.g = l * NB + self.B
                self.use = l * ((NB + 1 - self.r) // 2) + (m + c // 2)

        class Step:

            def __init__(self, batch, i):
                self.batch, self.i, self.r, self.use = batch, i, batch.r, batch.use
                self.k, self.n = batch.B * U + i, batch.g * U + i
                self.half = (batch.r * U + i) % 2

        def edge_loop(eng, l, body):
            def run(m, c, inside=False):
                def batch(d):
                    return Batch(l, m, c + d) if inside or 0 <= c + d < NB else None

                def step(d):
                    b = batch(d // U)
                    return None if b is None else Step(b, d % U)

                body(step, batch)

            loops = (NB - 3) // 2
            for c in range(-1, 2):
                run(0, c)
            with eng.Fori(0, loops) as m:
                for c in range(2, 4):
                    run(m, c, True)
            for c in range(2 + 2 * loops, NB + 2):
                run(0, c)

        def rounds(eng, n, body):
            body(0, True)
            with eng.Fori(1, n) as m:
                body(m, False)

        def block_of(eng, x):
            return x and eng.value_load(blkI[0:1, ds(x.k, 1)], min_val=0, max_val=NBLK - 1)

        ZERO_DMAS = 4
        ZW = EXPERTS * CAPP * D // (P * ZERO_DMAS)
        zeros = accT[:, 10 * SLOTS:10 * SLOTS + ZW]
        split = lambda x: x.rearrange("p n (h d) -> p n h d", h=HEADS)
        pair_rows = lambda dram_rows, it: dram_rows[ds(it * 2 * P, 2 * P), :].rearrange("(n p) d -> p n d", n=2)
        skip_rows = qx_dram[:, QW:QX]
        STORED = LOOPS * 32
        flat3 = lambda x: x.rearrange("p b e -> p (b e)")

        def held(eng):
            eng.sem_inc(s["held"], 1)

        NGATE = NBLK * EXPERTS
        o = 0
        hm, o = view(o, FF // P, 2 * HALF, of=accT, room=ACCN)
        ex, o = view(o, NBLK, EXPERTS, of=accT, room=ACCN)
        eq, o = view(o, NBLK, EXPERTS, of=accT, room=ACCN)
        oh, o = view(o, NBLK, EXPERTS, of=accT, room=ACCN)
        run, o = view(o, NBLK, EXPERTS, of=accT, room=ACCN)
        mx, o = view(o, NBLK, of=accT, room=ACCN)
        se, o = view(o, NBLK, of=accT, room=ACCN)
        ms, o = view(o, NBLK, of=accT, room=ACCN)
        pos, o = view(o, NBLK, of=accT, room=ACCN)
        base, o = view(o, NBLK, of=accT, room=ACCN)
        kept, o = view(o, NBLK, of=accT, room=ACCN)
        wgt, o = view(o, NBLK, of=accT, room=ACCN)
        slf, o = view(o, NBLK, of=accT, room=ACCN)
        slotw, o = view(o, NBLK, of=accT, room=ACCN, dt=I32)
        slotr, o = view(o, NBLK, of=accT, room=ACCN, dt=I32)
        b1c, o = view(o, 2, FF // P, of=accT, room=ACCN)
        b2b, o = view(o, 2, D, of=accT, room=ACCN)
        o = 0
        w1, o = view(o, 2, 2, FF)
        w2, o = view(o, 2, FF // P, D)
        xs, o = view(o, 2, CT, D)
        xsT, o1 = view(o, 2, CAPP)
        xsc, _ = view(o, EU, D)
        yb, _ = view(o1, CT, D)
        o = RING - (NBLK + 3) * EXPERTS
        lg, o = view(o, NBLK, EXPERTS)
        gb_bc, o = view(o, EXPERTS)
        gw, o = view(o, 2, EXPERTS)
        o = 0
        yg, o = view(o, EU, D)
        x2b, o = view(o, EU, D)
        fo, o = view(o, EU, D)
        fin, o = view(o, D)
        nn, o = view(o, D)
        ty, o = view(o, D)
        cl, o = view(o, D)
        slot_idx = sb("slot_idx", [P, 2 * EU], I32)
        w_ex = [sem(f"w_ex_{i}") for i in range(2)]
        xs_in = [sem(f"xs_in_{i}") for i in range(2)]
        sc_in = [sem(f"sc_in_{i}") for i in range(EU)]
        sc_done = [sem(f"sc_done_{i}") for i in range(EU)]
        yg_in = [sem(f"yg_in_{i}") for i in range(EU)]
        x2_in = [sem(f"x2_in_{i}") for i in range(EU)]
        o_st = [sem(f"o_stored_{i}") for i in range(EU)]
        G_ALL = LAYERS * NBLK
        SROUNDS = NBLK // EU

        def slot_of(m, r, ahead):
            return (m, r) if not ahead else (m, 1) if r == 0 else (m + 1, 0)

        def experts(eng, body):
            with eng.Fori(0, EXPERTS // 2 - 1) as m:
                for r in range(2):
                    body(m, r, True)
            for r in range(2):
                body(EXPERTS // 2 - 1, r, r == 0)

        def moe_sync(sp):
            for i in range(EU):
                sp.wait_ge(h_st[i], LOOPS * 32)

            def weights(m, r):
                sp.wait_ge(s["y_mm"], m * (2 * CT) + (r * CT + CT))
                for c in range(2):
                    sp.dma_start(w1[:, r, c, :], a["w1"][ds(m * (2 * D) + (r * D + c * P), P), :]
                                 ).then_inc(w_ex[r], 16)
                sp.dma_start(w2[:, r, :, :], a["w2"][ds(m * (2 * FF) + r * FF, FF), :]
                             .rearrange("(f p) d -> p f d", p=P)).then_inc(w_ex[r], 16)
                sp.dma_start(b1c[:, r, :], a["b1"][ds(m * (2 * P) + r * P, P), :]).then_inc(w_ex[r], 16)
                if not isinstance(m, int):
                    sp.wait_ge(s["y_ev"], m * (2 * CT) + (r * CT - CT + 2))
                sp.dma_start(b2b[:, r, :], a["b2"][ds(m * 2 + r, 1), :].to_broadcast([P, D])
                             ).then_inc(w_ex[r], 16)

            def slots(m, r):
                sp.dma_start(xs[:, r, :, :], slots_dram[ds(m * (2 * CAPP) + r * CAPP, CAPP), :]
                             .rearrange("(t p) d -> p t d", p=P)).then_inc(xs_in[r], 16)

            sp.wait_ge(s["mm_done"], G_ALL + NBLK + 2)
            for r in range(2):
                weights(0, r)
            def load_rows(m, first):
                for r in range(EU):
                    if not first:
                        sp.wait_ge(sc_done[r], m * 16)
                    sp.dma_start(xsc[:, r, :], xn_dram[ds((m * EU + r) * P, P), :]).then_inc(sc_in[r], 16)

            rounds(sp, SROUNDS, load_rows)
            for r in range(EU):
                sp.wait_ge(sc_done[r], SROUNDS * 16)
            for r in range(2):
                slots(0, r)
            with sp.Fori(1, EXPERTS // 2) as m:
                for r in range(2):
                    weights(m, r)
                    slots(m, r)
            sp.wait_ge(s["y_st"], EXPERTS * 32)
            with sp.Fori(0, SROUNDS) as m:
                for r in range(EU):
                    sp.wait_ge(s["fo_done"], m * EU + r + 1)
                    sp.dma_start(x2b[:, r, :], x2_dram[ds((m * EU + r) * P, P), :]).then_inc(x2_in[r], 16)

        def moe_pool(pool):
            with pool.Fori(0, LOOPS) as m:
                for r in range(EU):
                    pool.wait_ge(s["h_ready"], m * EU + (LAYERS * PAIRS + r + 1 + EU))
                    for dst, src in ((xn_dram, ly), (x2_dram, lh)):
                        pool.dma_start(pair_rows(dst, m * EU + r), src[:, r, :, :]).then_inc(h_st[r], 16)
            pool.wait_ge(s["slots_ready"], 1)
            def scatter(m, first):
                for r in range(EU):
                    if not first:
                        pool.wait_ge(sc_done[r], m * 16)
                        held(pool)
                    pool.tensor_copy(slot_idx[:, r:r + 1], slotw[:, ds(m * EU + r, 1)]).then_inc(s["sidx"], 1)
                    pool.wait_ge(s["sidx"], m * EU + r + 1)
                    pool.wait_ge(sc_in[r], m * 16 + 16)
                    held(pool)
                    pool.indirect_dma_start(slots_dram, bass.IndirectOffsetOnAxis(ap=slot_idx[:, r:r + 1], axis=0),
                                            xsc[:, r, :], None, bounds_check=EXPERTS * CAPP - 1,
                                            oob_is_err=False).then_inc(sc_done[r], 16)

            rounds(pool, SROUNDS, scatter)
            with pool.Fori(0, EXPERTS // 2) as m:
                for r in range(2):
                    pool.wait_ge(s["y_ev"], m * (2 * CT) + (r * CT + CT + 2))
                    full = 2 * HALF // P
                    rest = 2 * HALF - full * P
                    pool.dma_start(y_dram[ds(m * (4 * HALF) + r * 2 * HALF, full * P), :]
                                   .rearrange("(t p) d -> p t d", p=P), yb[:, 0:full, :]).then_inc(s["y_st"], 16)
                    pool.dma_start(y_dram[ds(m * (4 * HALF) + (r * 2 * HALF + full * P), rest), :],
                                   yb[0:rest, full, :]).then_inc(s["y_st"], 16)
            pool.wait_ge(s["y_st"], EXPERTS * 32)
            with pool.Fori(0, SROUNDS) as m:
                for r in range(EU):
                    pool.wait_ge(s["fo_done"], m * EU + r + 1)
                    held(pool)
                    pool.tensor_copy(slot_idx[:, EU + r:EU + r + 1], slotr[:, ds(m * EU + r, 1)]).then_inc(s["gidx"], 1)
                    pool.wait_ge(s["gidx"], m * EU + r + 1)
                    held(pool)
                    pool.indirect_dma_start(yg[:, r, :], None, y_dram,
                                            bass.IndirectOffsetOnAxis(ap=slot_idx[:, EU + r:EU + r + 1], axis=0)
                                            ).then_inc(yg_in[r], 16)

        def moe_act(act):
            act.wait_ge(s["lm_ready"], 1)
            act.activation(flat3(ex), flat3(eq), ACT.Exp).then_inc(s["ex_ready"], 1)

            def take_slots(m, r):
                for b in range(4):
                    act.wait_ge(s["xt_ps"], m * 8 + (r * 4 + b + 1))
                    act.activation(xsT[:, :, b * 2 * P:(b + 1) * 2 * P].rearrange("p c (t e) -> p t c e", t=2),
                                   psQ[:, b, :].rearrange("p (t c e) -> p t c e", t=2, c=2), ACT.Copy
                                   ).then_inc(s["xt_cp"], 1)

            def hidden(m, r, more):
                act.wait_ge(w_ex[r], m * (5 * 16) + 5 * 16)
                act.wait_ge(s["y_mm"], m * (2 * CT) + (r * CT + 2 * CT))
                for q in range(2 * (FF // P)):
                    half, f = divmod(q, FF // P)
                    at, n = HALVES[half]
                    act.wait_ge(s["h_mm"], m * 32 + (r * 16 + q + 1))
                    act.activation(hm[:, f, at:at + n], psQ[:, q % 4, 0:n], ACT.Relu,
                                   bias=b1c[:, r, f:f + 1]).then_inc(s["h_cp"], 1)
                if more:
                    take_slots(*slot_of(m, r, 1))

            take_slots(0, 0)
            experts(act, hidden)
            with act.Fori(0, SROUNDS) as m:
                for r in range(EU):
                    act.wait_ge(s["fo_done"], m * EU + (r + 1 + EU))
                    act.dma_start(out[ds((m * EU + r) * P, P), :], fo[:, r, :]).then_inc(o_st[r], 16)
            for r in range(EU):
                act.wait_ge(o_st[r], SROUNDS * 16)

        def moe_pe(pe):
            pe.wait_ge(s["oh_ready"], 1)
            pe.matmul(psT[:, 0:NGATE], tri[:, :], flat3(oh), start=True, stop=True)
            pe.matmul(psB[:, 0:NGATE], ones[:, :], flat3(oh), start=True, stop=True).then_inc(s["cnt_mm"], 1)

            def turn_slots(m, r):
                pe.wait_ge(xs_in[r], m * 16 + 16)
                pe.wait_ge(s["h_cp"], m * 32 + r * 16 + START)
                for b in range(4):
                    for t in range(2):
                        for c in range(2):
                            last = pe.transpose(psQ[:, b, (2 * t + c) * P:(2 * t + c + 1) * P],
                                                xs[:, r, 2 * b + t, c * P:(c + 1) * P], ident[:, :])
                    last.then_inc(s["xt_ps"], 1)

            def expert(m, r, more):
                e16 = m * 32 + r * 16
                pe.wait_ge(s["xt_cp"], m * 8 + (r * 4 + 4))
                pe.wait_ge(w_ex[r], m * (5 * 16) + 5 * 16)
                for q in range(2 * (FF // P)):
                    half, f = divmod(q, FF // P)
                    at, n = HALVES[half]
                    if q >= 4:
                        pe.wait_ge(s["h_cp"], e16 + (q - 3) + START)
                    for c in range(2):
                        last = pe.matmul(psQ[:, q % 4, 0:n], w1[:, r, c, f * P:(f + 1) * P],
                                         xsT[:, c, at:at + n], start=(c == 0), stop=(c == 1))
                    last.then_inc(s["h_mm"], 1)
                for t in range(CT):
                    if t % (CT // 2) == 0:
                        pe.wait_ge(s["h_cp"], e16 + (8 if t == 0 else 16) + START)
                        if t and more:
                            turn_slots(*slot_of(m, r, 1))
                    n = min(P, 2 * HALF - t * P)
                    bank = (psA, psT)[t % 2]
                    pe.wait_ge(s["y_ev"], m * (2 * CT) + (r * CT + t + 1))
                    for f in range(FF // P):
                        last = pe.matmul(bank[0:n, 0:D], hm[:, f, t * P:t * P + n], w2[:, r, f, :],
                                         start=(f == 0), stop=(f == FF // P - 1))
                    last.then_inc(s["y_mm"], 1)

            turn_slots(0, 0)
            experts(pe, expert)

        def moe_dve(dve):
            dve.wait_ge(s["ev_done"], G_ALL + NBLK + 2)
            c = Chain(dve, s["route"])
            per_token = lambda v: v.unsqueeze(2).to_broadcast([P, NBLK, EXPERTS])
            e8_bc = e8[:, :].unsqueeze(1).to_broadcast([P, NBLK, EXPERTS])
            c.link(dve.tensor_reduce(mx, lg, AX, ALU.max))
            c.link(dve.tensor_tensor(eq, lg, per_token(mx), ALU.subtract))
            dve.sem_inc(s["lm_ready"], 1)
            c.link(dve.tensor_scalar(oh, eq, 0.0, None, ALU.is_equal))
            c.link(dve.tensor_tensor(oh, oh, e8_bc, ALU.mult))
            c.link(dve.tensor_reduce(ms, oh, AX, ALU.max))
            c.link(dve.tensor_tensor(oh, e8_bc, per_token(ms), ALU.is_equal))
            dve.sem_inc(s["oh_ready"], 1)
            dve.wait_ge(s["ex_ready"], 1)
            c.link(dve.tensor_reduce(se, ex, AX, ALU.add))
            c.link(dve.reciprocal(wgt, se))
            dve.wait_ge(s["cnt_mm"], 1)
            for e in range(EXPERTS):
                last = dve.tensor_tensor_scan(run[:, :, e], ones[:, 0:NBLK], psB[:, e:NGATE:EXPERTS], 0.0,
                                              ALU.mult, ALU.add)
            c.link(last)
            c.link(dve.tensor_tensor(flat3(run), flat3(run), psB[:, 0:NGATE], ALU.subtract))
            c.link(dve.tensor_tensor(flat3(run), flat3(run), psT[:, 0:NGATE], ALU.add))
            c.link(dve.tensor_tensor(run, run, oh, ALU.mult))
            c.link(dve.tensor_reduce(pos, run, AX, ALU.add))
            c.link(dve.tensor_scalar(kept, pos, float(CAP), None, ALU.is_le))
            c.link(dve.tensor_tensor(wgt, wgt, kept, ALU.mult))
            c.link(dve.tensor_scalar(base, ms, -float(CAPP), float(EXPERTS * CAPP - 1), ALU.mult, ALU.add))
            c.link(dve.tensor_scalar(kept, kept, -float(1 << 20), float(1 << 20), ALU.mult, ALU.add))
            c.link(dve.tensor_tensor(slf, base, pos, ALU.add))
            c.link(dve.tensor_tensor(slf, slf, kept, ALU.add))
            c.link(dve.tensor_copy(slotw, slf))
            c.link(dve.tensor_scalar(pos, pos, float(CAP), None, ALU.min))
            c.link(dve.tensor_scalar(base, ms, -float(2 * HALF), float(EXPERTS * 2 * HALF - 1), ALU.mult, ALU.add))
            c.link(dve.tensor_tensor(slf, base, pos, ALU.add))
            c.link(dve.tensor_copy(slotr, slf))
            dve.sem_inc(s["slots_ready"], 1)
            def add_bias(m, first):
                for r in range(2):
                    dve.wait_ge(w_ex[r], m * (5 * 16) + 5 * 16)
                    if r or not first:
                        dve.wait_ge(s["y_st"], m * 64 + r * 32)
                    for t in range(CT):
                        n = min(P, 2 * HALF - t * P)
                        bank = (psA, psT)[t % 2]
                        dve.wait_ge(s["y_mm"], m * (2 * CT) + (r * CT + t + 1 + 2 * CT))
                        dve.tensor_tensor(yb[0:n, t, :], bank[0:n, 0:D], b2b[0:n, r, :], ALU.add
                                          ).then_inc(s["y_ev"], 1)

            rounds(dve, EXPERTS // 2, add_bias)
            fc = Chain(dve, s["final"], 6)
            def combine(m, first):
                for r in range(EU):
                    fc.at(m * EU + r)
                    dve.wait_ge(yg_in[r], m * 16 + 16)
                    fc.link(dve.tensor_scalar(ty, yg[:, r, :], wgt[:, ds(m * EU + r, 1)], None, ALU.mult))
                    fc.inc(dve.tensor_scalar(fin, ty, 0.0, 0.0, ALU.mult, ALU.is_equal))
                    fc.inc(dve.tensor_scalar(cl, ty, HUGE, 10000.0, ALU.is_ge, ALU.mult))
                    fc.link(dve.tensor_scalar(nn, ty, -HUGE, -10000.0, ALU.is_le, ALU.mult))
                    fc.link(dve.tensor_tensor(cl, cl, nn, ALU.add))
                    held(dve)
                    fc.link(dve.copy_predicated(cl, fin.bitcast(I32), ty))
                    dve.wait_ge(x2_in[r], m * 16 + 16)
                    if not first:
                        dve.wait_ge(o_st[r], m * 16)
                    dve.tensor_tensor(fo[:, r, :], cl, x2b[:, r, :], ALU.add).then_inc(s["fo_done"], 1)
                    dve.wait_ge(s["fo_done"], m * EU + (r + 1 + EU))

            rounds(dve, SROUNDS, combine)

        block = ctx.enter_context(nc.Block())

        @block.sync
        def _(sp):
            sp.dma_start(lastI[0:KH, :], a["last"].to_broadcast([KH, SUPER - 1])).then_inc(s["last_in"], 16)
            sp.wait_ge(s["steps_ready"], 1)
            for g in range(2):
                for h in range(HEADS):
                    sp.dma_start(res_dram[g * KH * HEADS + h:(g + 1) * KH * HEADS:HEADS, :],
                                 res2[0:KH, g, :]).then_inc(s["setup_st"], 16)
                for i in range(3):
                    sp.dma_start(meta_dram[i:i + 1, g * KH:(g + 1) * KH].rearrange("a k -> k a"),
                                 small3[0:KH, g, i:i + 1], allow_slow_non_contiguous=True).then_inc(s["setup_st"], 16)
            sp.wait_ge(s["setup_st"], 2 * (HEADS + 3) * 16)
            for i in range(3):
                sp.dma_start(row[i][0:HEADS, :], meta_dram[i:i + 1, :].to_broadcast([HEADS, SLOTS])
                             ).then_inc(s["rows_in"], 16)
            sp.wait_ge(s["rows_ready"], 1)
            sp.dma_start(meta_dram[3:4, :], row[9][0:1, :]).then_inc(s["setup_st"], 16)
            sp.wait_ge(s["setup_st"], 2 * (HEADS + 3) * 16 + 16)
            for i in range(U):
                sp.dma_start(crossc[i * HEADS:(i + 1) * HEADS, :],
                             meta_dram[3:4, i:STEPS:U].to_broadcast([HEADS, NB]),
                             allow_slow_non_contiguous=True).then_inc(s["cross_in"], 16)

            def turn(phase):
                for c in range(2):
                    sp.dma_start(wcat[:, c, :], a["wcat"][ds(phase * D + c * P, P), :]).then_inc(s["w_in"], 16)
                sp.dma_start(bias_bc[:, :], a["bcat"][ds(phase, 1), :].to_broadcast([P, 4 * D])
                             ).then_inc(s["w_in"], 16)
                sp.dma_start(we_next[:, :], a["we"][ds(phase, 1), :].to_broadcast([P, D])).then_inc(s["w_in"], 16)
                for i in range(2):
                    sp.dma_start(wb_next[:, i, :], a["wbeta"][ds(phase * 3 + (i + 1), 1), :].to_broadcast([P, D])
                                 ).then_inc(s["w_in"], 16)

            def rows_of(phase, source, first):
                with sp.Fori(0, LOOPS) as m:
                    for r in range(EU):
                        sp.wait_ge(s["h_ready"], phase * PAIRS + m * EU + r + 1)
                        sp.dma_start(xr[:, r, :, first:], pair_rows(source, m * EU + r)).then_inc(xr_in[r], 16)

            def epilogue_weights(l):
                sp.dma_start(we_bc[:, :], a["we"][ds(l, 1), :].to_broadcast([P, D])).then_inc(s["e_in"], 16)
                for i in range(2):
                    sp.dma_start(wb_bc[:, i, :], a["wbeta"][ds(l * 3 + 2 * i, 1), :].to_broadcast([P, D])
                                 ).then_inc(s["e_in"], 16)

            def edges(l):
                for r in range(EU):
                    sp.wait_ge(pst[r], (l + 1) * STORED)
                held(sp)

                def body(step, batch):
                    an = batch(0)
                    if an is None:
                        return
                    steps = [step(i) for i in range(U)]
                    blocks = [sp.value_load(blkI[0:1, ds(x.k, 1)], min_val=0, max_val=NBLK - 1) for x in steps]
                    for x, b in zip(steps, blocks):
                        sp.wait_ge(s["q_ready"], (x.n + 1) * 2)
                        sp.dma_start(qring[:, x.i, :], qx_dram[ds(b * P, P), 0:QW]).then_inc(q_in[x.i], 16)
                    sp.wait_ge(s["scanned"], an.g + START)
                    sp.dma_start(res[:, :], res_dram[ds(steps[0].k * HEADS, PB), :]).then_inc(s["res_in"], 16)

                edge_loop(sp, l, body)
                sp.wait_ge(s["acc_done"], (l + 1) * STEPS + START)
                held(sp)

            sp.wait_ge(s["setup_done"], 1)
            turn(0)
            rows_of(0, a["x"], 1)
            with sp.Fori(0, LAYERS - 1) as l:
                edges(l)
                epilogue_weights(l)
                turn(l + 1)
                rows_of(l + 1, skip_rows, 0)
            edges(LAYERS - 1)
            epilogue_weights(LAYERS - 1)
            for c in range(2):
                sp.dma_start(gw[:, c, :], a["gate_w"][c * P:(c + 1) * P, :]).then_inc(s["gate_in"], 16)
            sp.dma_start(gb_bc, a["gate_b"].to_broadcast([P, EXPERTS])).then_inc(s["gate_in"], 16)
            with sp.Fori(0, LOOPS) as m:
                for r in range(EU):
                    sp.wait_ge(s["h_ready"], m * EU + (LAYERS * PAIRS + r + 1))
                    sp.dma_start(xr[:, r, :, :], pair_rows(skip_rows, m * EU + r)).then_inc(xr_in[r], 16)
                    sp.dma_start(lx[:, r, :, :], pair_rows(a["x"], m * EU + r)).then_inc(x_in[r], 16)
            moe_sync(sp)

        @block.gpsimd
        def _(pool):
            for name, n in (("q_ready", 2 * U), ("agg_done", RS), ("g_used", RS), ("v_used", RS), ("qk_done", 2), ("edge_term_done", 2),
                            ("w_dve", RS), ("w_act", RS), ("scaled", RS), ("tr_done", 2 * EU), ("hT_done", 2),
                            ("mm_done", 2), ("ev_done", 2), ("h_ready", EU), ("y_mm", 2 * CT),
                            ("y_ev", 2), ("fo_done", EU)):
                pool.sem_inc(s[name], n)
            for name in ("scanned", "pb_done", "alpha_ready", "acc_done", "oh_done", "chain_B", "act_B",
                         "h_cp"):
                pool.sem_inc(s[name], START)
            pool.iota(iota_i[:, :], [[1, SUPER]], base=0, channel_multiplier=0).then_inc(s["iotas"], 1)
            pool.iota(part_i[:, 0:1], [[1, 1]], base=0, channel_multiplier=1).then_inc(s["iotas"], 1)
            pool.iota(part_i[:, 1:3], [[KH, 2]], base=0, channel_multiplier=1).then_inc(s["iotas"], 1)
            pool.iota(sel_i[0:PB, 0:HEADS], [[-1, HEADS]], base=0, channel_multiplier=1).then_inc(s["iotas"], 1)
            pool.iota(sel_i[0:PB, HEADS:HEADS + U], [[-HEADS, U]], base=0, channel_multiplier=1
                      ).then_inc(s["iotas"], 1)
            pool.iota(sel_i[0:HEADS, HEADS + U:], [[0, U], [1, HEADS]], base=0, channel_multiplier=-1
                      ).then_inc(s["iotas"], 1)
            pool.memset(ones[:, :], 1.0).then_inc(s["iotas"], 1)
            pool.memset(Us[:, :], 0.0).then_inc(s["iotas"], 1)
            pool.memset(zeros, 0.0).then_inc(s["zeros"], 1)
            pool.wait_ge(s["zeros"], 1)
            flat_slots = slots_dram.rearrange("(p r) d -> p (r d)", p=P)
            for i in range(ZERO_DMAS):
                pool.dma_start(flat_slots[:, i * ZW:(i + 1) * ZW], zeros).then_inc(s["zero_st"], 16)
            pool.wait_ge(s["t_ready"], 1)
            for g in range(2):
                for name, dst in (("dst", rawI), ("src", srcR), ("ew", ewF)):
                    pool.indirect_dma_start(dst[0:KH, g, :], None, a[name],
                                            bass.IndirectOffsetOnAxis(ap=tI[0:KH, g:g + 1], axis=0)
                                            ).then_inc(s["steps_in"], 16)

            def turn(phase):
                with pool.Fori(0, LOOPS) as m:
                    for r in range(EU):
                        pool.wait_ge(s["pout"], phase * PAIRS + m * EU + r + 1)
                        pool.dma_start(pair_rows(kv_dram, m * EU + r), kvb[:, r, :, :]).then_inc(pst[r], 16)
                        pool.dma_start(pair_rows(qx_dram, m * EU + r), qx_rows[:, r, :, 0:QX]).then_inc(pst[r], 16)

            def edges(l):
                pool.memset(accT[:, :], 0.0).then_inc(s["acc_zero"], 1)
                for r in range(EU):
                    pool.wait_ge(pst[r], (l + 1) * STORED)
                held(pool)

                def body(step, batch):
                    an = batch(0)
                    if an is None:
                        return
                    for i in range(U):
                        x = step(i)
                        pool.wait_ge(s["v_used"], x.n + 1)
                        if i == 0:
                            held(pool)
                            pool.tensor_copy(idxb[:, an.r, :, :], srcI[:, ds(x.k, U), :]).then_inc(s["idx_done"], 1)
                            pool.wait_ge(s["idx_done"], an.g + 1)
                        held(pool)
                        for j in range(J):
                            pool.indirect_dma_start(
                                kv[:, an.r, i, j, :], None, kv_dram,
                                bass.IndirectOffsetOnAxis(ap=idxb[:, an.r, i, j:j + 1], axis=0)
                            ).then_inc(kv_in[an.r][i], 16)

                edge_loop(pool, l, body)

            pool.wait_ge(s["zero_st"], ZERO_DMAS * 16)
            pool.wait_ge(s["rows_used"], 1)
            turn(0)
            with pool.Fori(0, LAYERS - 1) as l:
                edges(l)
                turn(l + 1)
            edges(LAYERS - 1)
            moe_pool(pool)

        @block.scalar
        def _(act):
            def deviations(it):
                act.wait_ge(s["ln_var"], it + 1)
                act.activation(sd[:, :], ve[:, :], ACT.Sqrt).then_inc(s["ln_sd"], 1)

            def mixing(it):
                act.wait_ge(s["z_ready"], it + 1)
                act.activation(ez[:, :], zc[:, :], ACT.Exp, scale=-1.0).then_inc(s["z_exp"], 1)

            def turn(phase, of_source):
                with act.Fori(0, LOOPS) as m:
                    for r in range(EU):
                        of_source(m, r)
                        for n in range(2):
                            gi = (phase * PAIRS + m * EU + r) * 2 + n
                            act.wait_ge(s["tr_done"], gi + 1 + 2 * EU)
                            act.wait_ge(s["mm_done"], gi + 1)
                            act.activation(hT[:, n, :, :].rearrange("p c t -> p (c t)"), (psG, psT)[n][:, 0:D],
                                           ACT.Copy).then_inc(s["hT_done"], 1)

            def edges(l):
                def build_G(x):
                    act.wait_ge(s["g_used"], x.n + 1)
                    for j in range(J):
                        act.activation(G[:, x.r, x.i, j, :], iota_r[:, :], ACT.Abs,
                                       bias=ndl[:, ds(x.k, 1), j]).then_inc(s["g_abs"], 1)

                def finish_G(x):
                    act.wait_ge(s["g_abs"], (x.n + 1) * J)
                    flat = G[:, x.r, x.i, :, :].rearrange("p j n -> p (j n)")
                    act.activation(flat, flat, ACT.Relu, bias=1.0, scale=-1.0).then_inc(s["g_ready"], 1)

                def copy_OH(x):
                    act.wait_ge(s["gt_done"], x.n + 1)
                    act.wait_ge(s["q_ready"], x.n * 2 - 2 + 2 * U)
                    act.activation(OH[:, x.half, :, :].rearrange("p j e -> p (j e)"), psG[:, :], ACT.Copy
                                   ).then_inc(s["oh_done"], 1)

                def edge_term(x):
                    act.wait_ge(s["alpha_ready"], x.n + START)
                    for jj in range(2):
                        act.wait_ge(s["qk_done"], x.n * 2 + jj + 1 + 2)
                        for j in (2 * jj, 2 * jj + 1):
                            last = act.activation(prod[:, j, :, HD], psQ[:, j, D:QW], ACT.Copy,
                                                  scale=ewT[:, ds(x.k, 1), j])
                        last.then_inc(s["edge_term_done"], 1)

                def exponentials(bn):
                    act.wait_ge(s["chain_B"], bn.g * KB + 10 + START)
                    act.wait_ge(s["pb_done"], bn.g + START)
                    act.activation(pT[:, :], Dm[:, :], ACT.Exp, scale=SCALE).then_inc(s["act_B"], 1)
                    act.wait_ge(s["chain_B"], bn.g * KB + 11 + START)
                    act.activation(gx[:, :], gd[:, :], ACT.Exp, scale=SCALE).then_inc(s["act_B"], 1)

                def copy_weights(bn):
                    act.wait_ge(s["pb_done"], bn.g + 1 + START)
                    for name in ("w_dve", "w_act", "scaled"):
                        act.wait_ge(s[name], bn.g * U - U + RS)
                    act.activation(pB[:, bn.r, :, :, :].rearrange("p j s h -> p (j s h)"),
                                   psB[:, 128:128 + J * PB], ACT.Copy).then_inc(s["act_B"], 1)
                    act.activation(fB[:, bn.r, :, :].rearrange("p s h -> p (s h)"), psB[:, 64:64 + PB], ACT.Copy,
                                   bias=1.0).then_inc(s["act_B"], 1)

                def weight_column(x):
                    act.wait_ge(s["act_B"], x.batch.g * KACT + 3 + START)
                    act.wait_ge(s["g_used"], x.n - 1 + RS)
                    act.activation(W[:, x.half, :, :, HD], pB[:, x.r, :, x.i, :], ACT.Copy).then_inc(s["w_act"], 1)

                def keep_sums(x, b):
                    here = accF[:, ds(b, 1), :].rearrange("p b w -> p (b w)")
                    act.wait_ge(s["agg_done"], x.n + 1 + RS)
                    held(act)
                    act.activation(here, psA[:, 0:HEADS * AW], ACT.Copy).then_inc(s["acc_done"], 1)

                def body(step, batch):
                    for i in range(U):
                        b = block_of(act, step(i - LAG - 1))
                        if step(i + 1):
                            copy_OH(step(i + 1))
                        if i == 1 and batch(-1):
                            exponentials(batch(-1))
                        if step(i):
                            edge_term(step(i))
                        if step(i - LAG):
                            weight_column(step(i - LAG))
                        if step(i + 2):
                            build_G(step(i + 2))
                        if step(i - LAG - 1):
                            keep_sums(step(i - LAG - 1), b)
                        if step(i + 2):
                            finish_G(step(i + 2))
                        if i == 1 and batch(-1):
                            copy_weights(batch(-1))

                edge_loop(act, l, body)

            act.wait_ge(s["setup_done"], 1)
            turn(0, lambda m, r: deviations(m * EU + r))
            with act.Fori(0, LAYERS - 1) as l:
                edges(l)
                turn(l + 1, lambda m, r: mixing(l * PAIRS + m * EU + r))
            edges(LAYERS - 1)

            def last_rows(m, r):
                mixing(m * EU + ((LAYERS - 1) * PAIRS + r))
                deviations(m * EU + (PAIRS + r))

            turn(LAYERS, last_rows)
            moe_act(act)

        @block.tensor
        def _(pe):
            pe.wait_ge(s["steps_ready"], 1)
            for g in range(2):
                for i, arr in enumerate((srcF, dloc, ewF)):
                    bank = (psQ[:, 0, :], psQ[:, 1, :], psQ[:, 2, :], psQ[:, 3, :], psG[:, :], psA[:, :])[3 * g + i]
                    for j in range(J):
                        last = pe.transpose(bank[:, j * P:j * P + KH], arr[0:KH, g, j:SE:J], ident[0:KH, 0:KH])
                    last.then_inc(s["setup_t"], 1)
            pe.wait_ge(s["setup_done"], 1)
            def turn(phase, rows, products):
                with pe.Fori(0, LOOPS) as m:
                    for r in range(EU):
                        it = phase * PAIRS + m * EU + r
                        pe.wait_ge(s["h_ready"], it + 1 + EU)
                        for n in range(2):
                            pe.wait_ge(s["hT_done"], it * 2 + n + 1)
                            for c in range(2):
                                last = pe.transpose((psG, psT)[n][:, c * P:(c + 1) * P],
                                                    rows[:, r, n, c * P:(c + 1) * P], ident[:, :])
                            last.then_inc(s["tr_done"], 1)
                        for n in range(2):
                            pe.wait_ge(s["hT_done"], it * 2 + n + 1 + 2)
                            pe.wait_ge(s["ev_done"], it * 2 + n + 1)
                            for sums, weights in products(n):
                                for c in range(2):
                                    last = pe.matmul(sums, hT[:, n, c, :], weights(c), start=(c == 0), stop=(c == 1))
                            last.then_inc(s["mm_done"], 1)

            def edges(l):
                def turn_G(x):
                    pe.wait_ge(s["g_ready"], x.n + 1)
                    pe.wait_ge(s["oh_done"], x.n + START)
                    for j in range(J):
                        last = pe.transpose(psG[:, j * P:(j + 1) * P], G[:, x.r, x.i, j, :], ident[:, :])
                    last.then_inc(s["gt_done"], 1)

                def expand_q(x):
                    pe.wait_ge(s["oh_done"], x.n + 1 + START)
                    pe.wait_ge(q_in[x.i], (x.batch.g + 1) * 16)
                    for jj in range(2):
                        pe.wait_ge(s["edge_term_done"], x.n * 2 + jj + 1)
                        for j in (2 * jj, 2 * jj + 1):
                            last = pe.matmul(psQ[:, j, 0:QW], OH[:, x.half, j, :], qring[:, x.i, :],
                                             start=True, stop=True)
                        last.then_inc(s["q_ready"], 1)

                def turn_scores(bn):
                    pe.wait_ge(s["alpha_ready"], (bn.g + 1) * U + START)
                    pe.wait_ge(s["chain_B"], bn.g * KB + START)
                    held(pe)
                    for j in range(J):
                        last = pe.transpose(psT[0:PB, j:SE:J], alpha[:, bn.r, j, :, :].rearrange(
                            "p s h -> p (s h)"), ident[:, :])
                    last.then_inc(s["at_done"], 1)

                def maxima_up(bn):
                    pe.wait_ge(s["act_B"], bn.g * KACT + START)
                    pe.wait_ge(s["chain_B"], bn.g * KB + 2 + START)
                    held(pe)
                    pe.matmul(psB[0:HEADS, 0:U], selA[:, :], LB[:, :], start=True, stop=True
                              ).then_inc(s["max_up"], 1)

                def maxima_down(bn):
                    pe.wait_ge(s["chain_B"], bn.g * KB + 5 + START)
                    held(pe)
                    pe.matmul(psB[0:PB, 32:33], lhs2[:, :, :].rearrange("a s h -> a (s h)"), ones[0:HEADS, 0:1],
                              start=True, stop=True).then_inc(s["max_down"], 1)

                def turn_weights(bn):
                    pe.wait_ge(s["chain_B"], bn.g * KB + KB + START)
                    held(pe)
                    pe.matmul(psB[:, 64:64 + PB], crossOH[:, :], gm[:, :], start=True, stop=True)
                    pe.wait_ge(s["act_B"], bn.g * KACT + 1 + START)
                    held(pe)
                    for j in range(J):
                        last = pe.transpose(psB[:, 128 + j * PB:128 + (j + 1) * PB], pT[:, j:SE:J],
                                            ident[0:PB, 0:PB])
                    last.then_inc(s["pb_done"], 1)

                def add_up(x):
                    pe.wait_ge(s["w_dve"], x.n + 1 + RS)
                    pe.wait_ge(s["w_act"], x.n + 1 + RS)
                    pe.wait_ge(s["acc_done"], x.n + START)
                    for j in range(J):
                        last = pe.matmul(psA[:, 0:HEADS * AW], G[:, x.r, x.i, j, :],
                                         W[:, x.half, j, :, :].rearrange("p h w -> p (h w)"),
                                         start=(j == 0), stop=False)
                    last.then_inc(s["g_used"], 1)

                def add_before(x, b):
                    here = accF[:, ds(b, 1), :].rearrange("p b w -> p (b w)")
                    pe.wait_ge(s["scaled"], x.n + 1 + RS)
                    held(pe)
                    pe.matmul(psA[:, 0:HEADS * AW], ident[:, :], here, start=False, stop=True
                              ).then_inc(s["agg_done"], 1)

                def body(step, batch):
                    for i in range(U):
                        b = block_of(pe, step(i - LAG - 1))
                        if step(i + 1):
                            turn_G(step(i + 1))
                        if step(i - LAG - 1):
                            add_up(step(i - LAG - 1))
                            add_before(step(i - LAG - 1), b)
                        if i == 0 and batch(-1):
                            maxima_up(batch(-1))
                        if step(i + 1):
                            expand_q(step(i + 1))
                        if i == 0 and batch(-1):
                            maxima_down(batch(-1))
                        if i == 1 and batch(-1):
                            turn_weights(batch(-1))
                        if i == U - 1 and batch(0):
                            turn_scores(batch(0))

                edge_loop(pe, l, body)

            def project(phase):
                pe.wait_ge(s["w_in"], (phase + 1) * (6 * 16))
                pe.wait_ge(s["wx_chain"], (phase + 1) * 5)
                held(pe)
                turn(phase, hin, lambda n: [(psQ[:, 2 * n, :], lambda c: wcat[:, c, 0:2 * D]),
                                            (psQ[:, 2 * n + 1, :], lambda c: wcat[:, c, 2 * D:4 * D]),
                                            ((psA, psB)[n][:, 0:HEADS + 1], lambda c: wx[:, c, :])])

            project(0)
            with pe.Fori(0, LAYERS - 1) as l:
                edges(l)
                project(l + 1)
            edges(LAYERS - 1)
            pe.wait_ge(s["gate_in"], 3 * 16)
            held(pe)
            turn(LAYERS, ly, lambda n: [(psQ[:, 2 * n, 0:EXPERTS], lambda c: gw[:, c, :])])
            moe_pe(pe)

        @block.vector
        def _(dve):
            setup = Chain(dve, s["setup_chain"])
            dve.wait_ge(s["iotas"], 8)
            dve.tensor_copy(iota_r[:, :], iota_i[:, 0:P])
            dve.tensor_copy(iota_c[:, :], part_i[:, 0:1])
            dve.tensor_copy(kcol[:, :], part_i[:, 1:3])
            nsA, nsB = sel_i[0:PB, 0:HEADS], sel_i[0:PB, HEADS:HEADS + U]
            dve.tensor_scalar(nsA, nsA, 7, None, ALU.bitwise_and)
            setup.link(dve.tensor_scalar(nsB, nsB, 3, None, ALU.arith_shift_right))
            dve.tensor_scalar(selA[:, :], nsA, 0.0, None, ALU.is_equal)
            dve.tensor_scalar(selB[:, :], nsB, 0.0, None, ALU.is_equal)
            dve.tensor_scalar(selD[:, :, :].rearrange("a s h -> a (s h)"), sel_i[0:HEADS, HEADS + U:], 0.0, None,
                              ALU.is_equal)
            dve.tensor_scalar(ident[:, :], iota_r[:, :], iota_c[:, 0:1], None, ALU.is_equal)
            dve.tensor_scalar(tri[:, :], iota_r[:, :], iota_c[:, 0:1], None, ALU.is_ge)
            dve.tensor_scalar(e8[:, :], iota_r[:, 0:EXPERTS], -1.0, float(EXPERTS), ALU.mult, ALU.add)
            dve.wait_ge(s["last_in"], 16)
            setup.link(dve.tensor_scalar(lastI[0:KH, :], lastI[0:KH, :], 7, None, ALU.logical_shift_right))
            setup.link(dve.tensor_copy(posA[0:KH, :], lastI[0:KH, :]))
            setup.link(dve.tensor_copy(cmpT[0:KH, :], iota_i[0:KH, 0:SUPER - 1]))
            setup.link(dve.tensor_tensor(posA[0:KH, :], posA[0:KH, :], cmpT[0:KH, :], ALU.add))
            for g in range(2):
                setup.link(dve.tensor_scalar(cmpT[0:KH, :], posA[0:KH, :], kcol[0:KH, g:g + 1], None, ALU.is_lt))
                setup.link(dve.tensor_reduce(tcol[0:KH, g:g + 1], cmpT[0:KH, :], AX, ALU.add))
            setup.link(dve.tensor_copy(tI[0:KH, :], tcol[0:KH, :]))
            dve.sem_inc(s["t_ready"], 1)
            setup.link(dve.tensor_tensor(nbc[0:KH, :], kcol[0:KH, :], tcol[0:KH, :], ALU.subtract))
            setup.link(dve.tensor_scalar(small3[0:KH, :, 2], nbc[0:KH, :], float(NBLK - 1), None, ALU.min))
            setup.link(dve.tensor_scalar(nbc[0:KH, :], small3[0:KH, :, 2], -float(P), None, ALU.mult))
            dve.wait_ge(s["steps_in"], 6 * 16)
            dve.tensor_copy(dstF[0:KH, :, :], rawI[0:KH, :, :])
            setup.link(dve.tensor_copy(srcF[0:KH, :, :], srcR[0:KH, :, :]))
            for g in range(2):
                dve.tensor_copy(small3[0:KH, g, 0:1], dstF[0:KH, g, 0:1])
                dve.tensor_copy(small3[0:KH, g, 1:2], dstF[0:KH, g, SE - 1:SE])
                setup.link(dve.tensor_scalar(dloc[0:KH, g, :], dstF[0:KH, g, :], nbc[0:KH, g:g + 1], -1.0,
                                             ALU.add, ALU.max))
                setup.link(dve.tensor_scalar(dloc[0:KH, g, :], dloc[0:KH, g, :], float(P), None, ALU.min))
                dve.memset(res2[0:KH, g, 0:1], 0.0)
                dve.memset(res2[0:KH, g, SE:SE + 1], 0.0)
                setup.link(dve.tensor_tensor(res2[0:KH, g, 1:SE], dloc[0:KH, g, 1:SE], dloc[0:KH, g, 0:SE - 1],
                                             ALU.not_equal))
                setup.link(dve.tensor_scalar(res2[0:KH, g, 1:SE], res2[0:KH, g, 1:SE], -BIG, None, ALU.mult))
            dve.sem_inc(s["steps_ready"], 1)
            for g in range(2):
                for i, dst in enumerate((srcI, ndl, ewT)):
                    bank = (psQ[:, 0, :], psQ[:, 1, :], psQ[:, 2, :], psQ[:, 3, :], psG[:, :], psA[:, :])[3 * g + i]
                    dve.wait_ge(s["setup_t"], 3 * g + i + 1)
                    turned = dst[:, g * KH:(g + 1) * KH, :].rearrange("p k j -> p j k")
                    sums = bank.rearrange("p (j k) -> p j k", j=J)[:, :, 0:KH]
                    if i == 1:
                        dve.tensor_scalar(turned, sums, -1.0, None, ALU.mult)
                    else:
                        dve.tensor_copy(turned, sums)
            r_first, r_last, r_blk, cont, whole, t0, t1, t2, t3, crs = [x[0:HEADS, :] for x in row]
            dve.wait_ge(s["rows_in"], 3 * 16)
            dve.tensor_copy(blkI[:, :], r_blk[0:1, :])
            dve.memset(cont[:, 0:1], 0.0)
            setup.link(dve.tensor_tensor(cont[:, 1:], r_blk[:, 1:], r_blk[:, :SLOTS - 1], ALU.is_equal))
            setup.link(dve.tensor_tensor(t0[:, 1:], r_first[:, 1:], r_last[:, :SLOTS - 1], ALU.is_equal))
            setup.link(dve.tensor_tensor(cont[:, 1:], cont[:, 1:], t0[:, 1:], ALU.mult))
            setup.link(dve.tensor_tensor(whole, r_first, r_last, ALU.is_equal))
            setup.link(dve.tensor_tensor(whole, whole, cont, ALU.mult))
            dve.tensor_scalar(dn8[:, :], cont, 1.0, BIG, ALU.subtract, ALU.mult)
            dve.tensor_scalar(dd8[:, :], whole, 1.0, BIG, ALU.subtract, ALU.mult)
            setup.link(dve.tensor_scalar(t1, r_blk, -float(P), 1.0, ALU.mult, ALU.add))
            setup.link(dve.tensor_tensor(t1, t1, r_first, ALU.add))
            setup.link(dve.tensor_tensor(t1, t1, cont, ALU.mult))
            setup.link(dve.tensor_scalar(crs, t1, 1.0, None, ALU.subtract))
            dve.sem_inc(s["rows_ready"], 1)
            dve.wait_ge(s["setup_st"], 2 * (HEADS + 3) * 16 + 16)
            dve.sem_inc(s["rows_used"], 1)
            dve.sem_inc(s["setup_done"], 1)

            ln = Chain(dve, s["ln_chain"], 3)

            def layer_norm(x, y, it, free):
                ln.at(it)
                for n in range(2):
                    last = dve.bn_stats(stats[:, n, :], x[:, n, :])
                ln.link(last)
                held(dve)
                for n in range(2):
                    last = dve.bn_aggr(mv[:, n, :], stats[:, n, :])
                ln.link(last)
                dve.tensor_scalar(ve[:, :], mv[:, :, 1], 1e-5, None, ALU.add).then_inc(s["ln_var"], 1)
                dve.wait_ge(s["ln_sd"], it + 1)
                ln.link(dve.reciprocal(rstd[:, :], sd[:, :]))
                free()
                for n in range(2):
                    last = dve.tensor_scalar(y[:, n, :], x[:, n, :], mv[:, n, 0:1], rstd[:, n:n + 1],
                                             ALU.subtract, ALU.mult)
                last.then_inc(s["h_ready"], 1)

            ep = Chain(dve, s["ep_chain"], 11)

            def epilogue(l, m, r, free):
                it = l * PAIRS + m * EU + r
                ep.at(it)
                two = acc[:, ds((m * EU + r) * 2, 2), :, :]
                bc = lambda x: x.unsqueeze(3).to_broadcast([P, 2, HEADS, HD])
                over = lambda w: w[:, :].unsqueeze(1).to_broadcast([P, 2, D])
                ep.link(dve.tensor_scalar(den[:, :, :], two[:, :, :, HD], 1e-16, None, ALU.add))
                ep.link(dve.reciprocal(rden[:, :, :], den[:, :, :]))
                ep.inc(dve.tensor_tensor(tew[:, :, :], two[:, :, :, HD + 1], rden[:, :, :], ALU.mult))
                ep.link(dve.tensor_tensor(split(ov), two[:, :, :, 0:HD], bc(rden[:, :, :]), ALU.mult))
                ep.link(dve.tensor_tensor(split(tw), split(over(we_bc)), bc(tew[:, :, :]), ALU.mult))
                ep.link(dve.tensor_tensor(ov, ov, tw, ALU.add))
                dve.wait_ge(xr_in[r], ((l + 1) * LOOPS + m + 1) * 16)
                ep.link(dve.tensor_tensor(q1, ov, over(wA), ALU.mult))
                ep.link(dve.tensor_reduce(zr[:, :], q1, AX, ALU.add))
                dve.tensor_tensor(zc[:, :], zr[:, :], xr[:, r, :, 0], ALU.add).then_inc(s["z_ready"], 1)
                ep.inc(dve.tensor_tensor(tw, xr[:, r, :, 1:], ov, ALU.subtract))
                dve.wait_ge(s["z_exp"], it + 1)
                ep.link(dve.tensor_scalar(zc[:, :], ez[:, :], 1.0, None, ALU.add))
                ep.link(dve.reciprocal(beta[:, :], zc[:, :]))
                free()
                for n in range(2):
                    last = dve.scalar_tensor_tensor(hin[:, r, n, :], tw[:, n, :], beta[:, n:n + 1],
                                                    ov[:, n, :], ALU.mult, ALU.add)
                return last

            wc = Chain(dve, s["wx_chain"], 5)

            def turn(phase, source):
                def make_weights():
                    dve.wait_ge(s["w_in"], (phase + 1) * (6 * 16))
                    wc.at(phase)
                    over = lambda w: w.unsqueeze(1).to_broadcast([P, 3, D])
                    wc.link(dve.tensor_tensor(wB[:, :], wb_next[:, 0, :], wb_next[:, 1, :], ALU.subtract))
                    wc.link(dve.tensor_tensor(tmp, w_and_bias[:, :, 2 * D:3 * D], over(we_next), ALU.mult))
                    wc.link(dve.tensor_reduce(wx[:, :, 0:HEADS], split(tmp), AX, ALU.add))
                    wc.link(dve.tensor_tensor(tmp, w_and_bias[:, :, 3 * D:4 * D], over(wB[:, :]), ALU.mult))
                    wc.link(dve.tensor_reduce(wx[:, :, HEADS], tmp, AX, ALU.add))

                def take(m, r, first):
                    it = phase * PAIRS + m * EU + r
                    if not first:
                        dve.wait_ge(pst[r], phase * STORED + m * 32)
                    for n in range(2):
                        dve.wait_ge(s["mm_done"], it * 2 + n + 1 + 2)
                        dve.tensor_tensor(kvb[:, r, n, :], psQ[:, 2 * n, :], bias_bc[:, 0:2 * D], ALU.add)
                        dve.tensor_tensor(qxb[:, r, n, :, 0:D], psQ[:, 2 * n + 1, :].rearrange("p (t w) -> p t w", t=2),
                                          bias_bc[:, 2 * D:].rearrange("p (t w) -> p t w", t=2), ALU.add)
                        last = dve.tensor_tensor(qxb[:, r, n, 0, D:], (psA, psB)[n][:, 0:HEADS + 1], wx[:, 2, :],
                                                 ALU.add)
                        last.then_inc(s["ev_done"], 1)
                    dve.wait_ge(s["ev_done"], it * 2 + 2 + 2)
                    dve.sem_inc(s["pout"], 1)

                def round_(m, first):
                    for r in range(EU):
                        source(m, r)
                        if r == 0 and first:
                            make_weights()
                        if r > 0:
                            take(m, r - 1, first)
                        elif not first:
                            take(m - 1, EU - 1, isinstance(m, int) and m == 1)

                round_(0, True)
                round_(1, False)
                with dve.Fori(2, LOOPS) as m:
                    round_(m, False)
                take(LOOPS - 1, EU - 1, False)
                dve.wait_ge(s["pout"], (phase + 1) * PAIRS)
                held(dve)

            def input_rows(m, r):
                dve.wait_ge(xr_in[r], (m + 1) * 16)
                layer_norm(xr[:, r, :, 1:], hin[:, r, :, :], m * EU + r,
                           lambda: dve.wait_ge(s["tr_done"], (m * EU + r) * 2 + 2))

            def edges(l):
                dve.wait_ge(s["acc_zero"], l + 1)
                dve.wait_ge(s["cross_in"], U * 16)

                def scores(x):
                    dve.wait_ge(s["alpha_ready"], x.n + START)
                    for jj in range(2):
                        dve.wait_ge(s["q_ready"], x.n * 2 + jj + 1 + 2 * U)
                        if jj == 0:
                            dve.wait_ge(kv_in[x.r][x.i], (x.use + 1) * (16 * J))
                        jr = slice(2 * jj, 2 * jj + 2)
                        dve.tensor_tensor(prod[:, jr, :, 0:HD], split(psQ[:, jr, 0:D]),
                                          split(kv[:, x.r, x.i, jr, 0:D]), ALU.mult).then_inc(s["qk_done"], 1)

                def reduce_scores(x):
                    dve.wait_ge(s["qk_done"], (x.n + 1) * 2 + 2)
                    dve.wait_ge(s["edge_term_done"], (x.n + 1) * 2 + 2)
                    dve.tensor_reduce(alpha[:, x.r, :, x.i, :], prod[:, :, :, :], AX, ALU.add
                                      ).then_inc(s["alpha_ready"], 1)

                cb = Chain(dve, s["chain_B"], KB, START)

                def maxima_1(bn):
                    cb.at(bn.g)
                    dve.wait_ge(s["res_in"], (bn.g + 1) * 16)
                    dve.wait_ge(s["at_done"], bn.g + 1)
                    cb.link(dve.tensor_tensor_scan(F1[:, :], res[:, 0:SE], psT[0:PB, :], -BIG, ALU.add, ALU.max))
                    cb.inc(dve.tensor_scalar(LB[:, :], selB[:, :], F1[:, SE - 1:SE], None, ALU.mult))

                def maxima_2(bn):
                    cb.at(bn.g, 2)
                    dve.wait_ge(s["max_up"], bn.g + 1)
                    cb.link(dve.tensor_tensor_scan(Us[:, 1:], dd8[:, ds(bn.B * U, U)], psB[0:HEADS, 0:U], Us[:, 0:1],
                                                   ALU.add, ALU.max))
                    cb.link(dve.tensor_tensor(cc[:, :], Us[:, 0:U], dn8[:, ds(bn.B * U, U)], ALU.add))
                    cb.inc(dve.tensor_tensor(lhs2[:, :, :], selD[:, :, :],
                                             cc[:, :].unsqueeze(2).to_broadcast([HEADS, U, HEADS]), ALU.mult))
                    cb.inc(dve.tensor_copy(Us[:, 0:1], Us[:, U:U + 1]))

                def maxima_3(bn):
                    cb.at(bn.g, 6)
                    dve.wait_ge(s["max_down"], bn.g + 1)
                    cb.link(dve.tensor_copy(ccol[:, :], psB[0:PB, 32:33]))
                    cb.link(dve.tensor_tensor_scan(F2[:, :], res[:, 0:SE], psT[0:PB, :], ccol[:, 0:1],
                                                   ALU.add, ALU.max))
                    cb.inc(dve.tensor_tensor_scan(M[:, ::-1], res[:, SE:0:-1], F2[:, ::-1], -BIG,
                                                  ALU.add, ALU.max))
                    cb.wait()
                    dve.sem_inc(s["scanned"], 1)
                    cb.inc(dve.tensor_tensor(Dm[:, :], psT[0:PB, :], M[:, :], ALU.subtract))
                    cb.inc(dve.tensor_tensor(gd[:, :], ccol[:, :], M[:, 0:1], ALU.subtract))

                def maxima_4(bn):
                    cb.at(bn.g, 11)
                    cb.inc(dve.tensor_scalar(crossOH[:, :], iota_r[0:PB, :], crossc[:, ds(bn.B, 1)], None,
                                             ALU.is_equal))
                    dve.wait_ge(s["act_B"], bn.g * KACT + 2 + START)
                    cb.inc(dve.scalar_tensor_tensor(gm[:, :], ident[0:PB, 0:PB], gx[:, 0:1], ident[0:PB, 0:PB],
                                                    ALU.mult, ALU.subtract))

                def weigh(x):
                    dve.wait_ge(s["act_B"], x.batch.g * KACT + 3 + START)
                    dve.wait_ge(s["g_used"], x.n - 1 + RS)
                    dve.tensor_tensor(W[:, x.half, :, :, 0:HD], split(kv[:, x.r, x.i, :, D:2 * D]),
                                      pB[:, x.r, :, x.i, :].unsqueeze(3).to_broadcast([P, J, HEADS, HD]), ALU.mult
                                      ).then_inc(s["v_used"], 1)
                    dve.tensor_tensor(W[:, x.half, :, :, HD + 1], pB[:, x.r, :, x.i, :],
                                      ewT[:, ds(x.k, 1), :].rearrange("p k j -> p (k j)").unsqueeze(2)
                                      .to_broadcast([P, J, HEADS]), ALU.mult).then_inc(s["w_dve"], 1)

                def rescale(x, b):
                    here = acc[:, ds(b, 1), :, :].rearrange("p b h w -> p (b h) w")
                    dve.wait_ge(s["act_B"], x.batch.g * KACT + 4 + START)
                    dve.wait_ge(s["acc_done"], x.n + START)
                    dve.tensor_tensor(here, here, fB[:, x.r, x.i, :].unsqueeze(2).to_broadcast([P, HEADS, AW]),
                                      ALU.mult).then_inc(s["scaled"], 1)

                def body(step, batch):
                    for i in range(U):
                        if step(i):
                            scores(step(i))
                        if i == 0 and batch(-1):
                            maxima_1(batch(-1))
                        if step(i - LAG):
                            weigh(step(i - LAG))
                        b = block_of(dve, step(i - LAG))
                        if i == 0 and batch(-1):
                            maxima_2(batch(-1))
                        if i == 1 and batch(-1):
                            maxima_4(batch(-1))
                        if step(i):
                            reduce_scores(step(i))
                        if step(i - LAG):
                            rescale(step(i - LAG), b)
                        if i == 0 and batch(-1):
                            maxima_3(batch(-1))

                edge_loop(dve, l, body)

                dve.wait_ge(s["acc_done"], (l + 1) * STEPS + START)
                dve.wait_ge(s["e_in"], (l + 1) * (3 * 16))
                dve.tensor_tensor(wA[:, :], wb_bc[:, 0, :], wb_bc[:, 1, :], ALU.add
                                  ).then_inc(s["mix_ready"], 1)
                dve.wait_ge(s["mix_ready"], l + 1)
                held(dve)

            turn(0, input_rows)
            with dve.Fori(0, LAYERS - 1) as l:
                edges(l)

                def result_rows(m, r):
                    last = epilogue(l, m, r, lambda: dve.wait_ge(
                        s["tr_done"], ((l + 1) * PAIRS + m * EU + r) * 2 + 2))
                    last.then_inc(s["h_ready"], 1)

                turn(l + 1, result_rows)
            edges(LAYERS - 1)
            add = Chain(dve, s["add_input"], 2)

            def gate_logits(m, r):
                it = m * EU + (LAYERS * PAIRS + r)
                for n in range(2):
                    dve.wait_ge(s["mm_done"], it * 2 + n + 1 + 2)
                    dve.tensor_tensor(lg[:, ds((m * EU + r) * 2 + n, 1), :].rearrange("p b e -> p (b e)"),
                                      psQ[:, 2 * n, 0:EXPERTS], gb_bc, ALU.add).then_inc(s["ev_done"], 1)

            def last_rows(m, first):
                for r in range(EU):
                    add.at(m * EU + r)
                    add.link(epilogue(LAYERS - 1, m, r, lambda: None))
                    dve.wait_ge(x_in[r], (m + 1) * 16)
                    if not first:
                        dve.wait_ge(h_st[r], m * 32)
                    add.link(dve.tensor_tensor(lh[:, r, :, :], hin[:, r, :, :], lx[:, r, :, :], ALU.add))
                    layer_norm(lh[:, r, :, :], ly[:, r, :, :], m * EU + (PAIRS + r),
                               lambda: dve.wait_ge(s["tr_done"], (m * EU + r) * 2 + (2 * LAYERS * PAIRS + 2)))
                    if r > 0:
                        gate_logits(m, r - 1)
                    elif not first:
                        gate_logits(m - 1, EU - 1)

            dve.wait_ge(s["gate_in"], 3 * 16)
            rounds(dve, LOOPS, last_rows)
            gate_logits(LOOPS - 1, EU - 1)
            moe_dve(dve)


def kernel(**inputs):
    import concourse.bacc as bacc
    from concourse.bass_utils import run_bass_kernel_spmd

    g = {k: np.asarray(v) for k, v in inputs.items()}
    gnn = lambda name, layer: g[f"L0_gnn_{name}{min(layer, 1) + 1}"]
    pad = SUPER * SE - EDGES
    dst = np.concatenate([g["dst"], np.full(pad, FAR, np.int32)]).reshape(SUPER, SE)
    arrays = {
        "x": np.concatenate([g["x"], np.zeros((NPAD - NODES, D), np.float32)]),
        "dst": dst,
        "last": np.ascontiguousarray(dst[:SUPER - 1, SE - 1]).reshape(1, -1),
        "src": np.concatenate([g["src"], np.zeros(pad, np.int32)]).reshape(SUPER, SE),
        "ew": np.concatenate([g["edge_weight"], np.zeros(pad, np.float32)]).reshape(SUPER, SE),
        "wcat": np.concatenate([np.concatenate([gnn(n, l) for n in ("Wk", "Wv", "Wq", "Wskip")], axis=1)
                                for l in range(LAYERS)]),
        "bcat": np.stack([np.concatenate([gnn(n, l) for n in ("bk", "bv", "bq", "bskip")])
                          for l in range(LAYERS)]),
        "we": np.concatenate([gnn("We", l) for l in range(LAYERS)]),
        "wbeta": np.concatenate([gnn("Wbeta", l).reshape(3, D) for l in range(LAYERS)]),
        "gate_w": g["L0_ffn_gate_w"],
        "gate_b": g["L0_ffn_gate_b"].reshape(1, EXPERTS),
        "w1": g["L0_ffn_w1"].reshape(EXPERTS * D, FF),
        "b1": np.ascontiguousarray(g["L0_ffn_b1"].reshape(EXPERTS, FF // P, P).transpose(0, 2, 1)
                                   ).reshape(EXPERTS * P, FF // P),
        "w2": g["L0_ffn_w2"].reshape(EXPERTS * FF, D),
        "b2": g["L0_ffn_b2"],
    }
    arrays = {f"in_{k}": np.ascontiguousarray(v) for k, v in arrays.items()}
    nc = bacc.Bacc("TRN2", target_bir_lowering=False, num_devices=1)
    a = {k[3:]: nc.dram_tensor(k, v.shape, mybir.dt.from_np(v.dtype), kind="ExternalInput").ap()
         for k, v in arrays.items()}
    out = nc.dram_tensor("out", (NPAD, D), F32, kind="ExternalOutput").ap()
    build(nc, a, out)
    r = run_bass_kernel_spmd(nc, [arrays], core_ids=[0])
    return r.results[0]["out"][:NODES]
```
